# Optimizing a Trainium2 kernel written in Bass

```python
import numpy as np
import jax
import jax.numpy as jnp

def _softmax(x, axis=-1):
    return jax.nn.softmax(x, axis=axis)

def _gelu(x):
    return jax.nn.gelu(x, approximate=True)

def _silu(x):
    return jax.nn.silu(x)

def _sigmoid(x):
    return jax.nn.sigmoid(x)

def _layernorm(x, axis=-1, eps=1e-05):
    m = jnp.mean(x, axis=axis, keepdims=True)
    v = jnp.var(x, axis=axis, keepdims=True)
    return (x - m) / jnp.sqrt(v + eps)

def _scatter_add(tgt, idx, src, axis=0):
    return tgt.at[idx].add(src)

def _segment_sum(src, seg, n):
    return jax.ops.segment_sum(src, seg, n)
kernel_name = 'mk_seq_preln_d1_jaxref_r8_29154b'

def setup_inputs(seed: int=0):
    np.random.seed(seed)
    _w = jnp.asarray

    def _L0_attn_setup():
        import jax, jax.numpy as jnp
        import numpy as np
        H_HEADS = 16
        STATE_N = 64

        def _mamba2_forward(inp, W_logA, b_logA, W_XBC, b_XBC, W_gate, b_gate, W_out, b_out):
            B, T, D = inp.shape
            H, N = (H_HEADS, STATE_N)
            ch = D // H
            x = inp.reshape(B, T, H, ch)
            logA = jnp.einsum('hoc,bthc->btho', W_logA, x)[..., 0] + b_logA[:, 0]
            XBC = jax.nn.silu(jnp.einsum('hoc,bthc->btho', W_XBC, x) + b_XBC)
            X = XBC[..., :ch]
            Bm = XBC[..., ch:ch + N]
            Cm = XBC[..., ch + N:]
            cum = jnp.cumsum(jnp.swapaxes(logA, 1, 2), axis=-1)
            diff = cum[..., :, None] - cum[..., None, :]
            causal = jnp.tril(jnp.ones((T, T), dtype=bool))
            A_ss = jnp.where(causal, jnp.exp(jnp.where(causal, diff, 0.0)), 0.0)
            G = jnp.einsum('bihn,bjhn->bhij', Cm, Bm)
            Y = jnp.einsum('bhij,bjhc->bihc', A_ss * G, X)
            gate = jnp.einsum('hoc,bthc->btho', W_gate, x) + b_gate
            Yg = (gate * Y).reshape(B, T, D)
            return Yg @ W_out.T + b_out
        key = jax.random.key(seed)
        ks = jax.random.split(key, 9)
        B, T, D = (2, 128, 128)
        H, ch, N = (H_HEADS, D // H_HEADS, STATE_N)
        inp = jax.random.normal(ks[0], (B, T, D), dtype=jnp.float32)
        W_logA = jax.random.normal(ks[1], (H, 1, ch), dtype=jnp.float32) * 0.01
        b_logA = jnp.full((H, 1), -0.05, dtype=jnp.float32)
        W_XBC = jax.random.normal(ks[3], (H, ch + 2 * N, ch), dtype=jnp.float32) * (1.0 / np.sqrt(ch))
        b_XBC = jax.random.normal(ks[4], (H, ch + 2 * N), dtype=jnp.float32) * 0.02
        W_gate = jax.random.normal(ks[5], (H, ch, ch), dtype=jnp.float32) * (1.0 / np.sqrt(ch))
        b_gate = jax.random.normal(ks[6], (H, ch), dtype=jnp.float32) * 0.02
        W_out = jax.random.normal(ks[7], (D, D), dtype=jnp.float32) * (1.0 / np.sqrt(D))
        b_out = jax.random.normal(ks[8], (D,), dtype=jnp.float32) * 0.02
        return {'inp': inp, 'W_logA': W_logA, 'b_logA': b_logA, 'W_XBC': W_XBC, 'b_XBC': b_XBC, 'W_gate': W_gate, 'b_gate': b_gate, 'W_out': W_out, 'b_out': b_out}
    _L0_attn_in = _L0_attn_setup()

    def _L0_ffn_setup():
        import jax, jax.numpy as jnp
        import numpy as np
        DIM = 128
        DEPTH = 2
        HEADS = 8
        DIM_HEAD = 64
        WINDOW = 64
        INNER = HEADS * DIM_HEAD
        HID = int(DIM * 4 * 2 / 3)
        B, N = (2, 1024)
        QK_SCALE = 8.0

        def shift_token(t):
            t1, t2 = jnp.split(t, 2, axis=-1)
            t2 = jnp.pad(t2, ((0, 0), (1, 0), (0, 0)))[:, :-1]
            return jnp.concatenate([t1, t2], axis=-1)

        def l2norm(t):
            return t / jnp.clip(jnp.linalg.norm(t, axis=-1, keepdims=True), 1e-12)

        def rotate_half(x):
            x1, x2 = jnp.split(x, 2, axis=-1)
            return jnp.concatenate([-x2, x1], axis=-1)

        def rotary_xpos(q, k):
            n = q.shape[-2]
            half_idx = jnp.arange(0, DIM_HEAD, 2, dtype=jnp.float32)
            inv_freq = 1.0 / 10000.0 ** (half_idx / DIM_HEAD)
            t = jnp.arange(n, dtype=jnp.float32)
            freqs = t[:, None] * inv_freq[None, :]
            freqs = jnp.concatenate([freqs, freqs], axis=-1)
            base = (half_idx + 0.4 * DIM_HEAD) / (1.4 * DIM_HEAD)
            power = (t - n // 2) / float(WINDOW // 2)
            scale = base[None, :] ** power[:, None]
            scale = jnp.concatenate([scale, scale], axis=-1)
            cos, sin = (jnp.cos(freqs), jnp.sin(freqs))
            q = q * cos * scale + rotate_half(q) * sin * scale
            k = k * cos / scale + rotate_half(k) * sin / scale
            return (q, k)

        def local_attention(q, k, v):
            b, h, n, d = q.shape
            w = n // WINDOW
            bq = q.reshape(b, h, w, WINDOW, d) * QK_SCALE
            bk = k.reshape(b, h, w, WINDOW, d)
            bv = v.reshape(b, h, w, WINDOW, d)

            def look_around(t):
                p = jnp.pad(t, ((0, 0), (0, 0), (1, 0), (0, 0), (0, 0)))
                return jnp.concatenate([p[:, :, :w], p[:, :, 1:]], axis=3)
            bk, bv = (look_around(bk), look_around(bv))
            bt = jnp.arange(n).reshape(w, WINDOW)
            btp = jnp.pad(bt, ((1, 0), (0, 0)), constant_values=-1)
            btk = jnp.concatenate([btp[:w], btp[1:]], axis=1)
            sim = jnp.einsum('bhwid,bhwjd->bhwij', bq, bk)
            i = bt[:, :, None]
            j = btk[:, None, :]
            mask = (i < j) | (i > j + WINDOW) | (j == -1)
            sim = jnp.where(mask, -jnp.finfo(sim.dtype).max, sim)
            attn = jax.nn.softmax(sim, axis=-1)
            out = jnp.einsum('bhwij,bhwjd->bhwid', attn, bv)
            return out.reshape(b, h, n, d)

        def _layer(x, wqkv, qs, ksc, wo, lg, lb, w1, b1, w2, b2):
            b, n, _ = x.shape
            h = shift_token(x)
            qkv = h @ wqkv
            q, k, v = jnp.split(qkv, 3, axis=-1)
            to_heads = lambda t: t.reshape(b, n, HEADS, DIM_HEAD).transpose(0, 2, 1, 3)
            q, k, v = (to_heads(q), to_heads(k), to_heads(v))
            q = l2norm(q) * qs
            k = l2norm(k) * ksc
            q, k = rotary_xpos(q, k)
            o = local_attention(q, k, v)
            o = o.transpose(0, 2, 1, 3).reshape(b, n, INNER)
            x = x + o @ wo
            h = shift_token(x)
            mu = h.mean(-1, keepdims=True)
            var = h.var(-1, keepdims=True)
            h = (h - mu) / jnp.sqrt(var + 1e-05) * lg + lb
            h = h @ w1 + b1
            a, g = jnp.split(h, 2, axis=-1)
            h = a * jax.nn.gelu(g, approximate=False)
            x = x + h @ w2 + b2
            return x
        key = jax.random.key(seed)
        ks = jax.random.split(key, 6)
        return {'x': jax.random.normal(ks[0], (B, N, DIM), jnp.float32), 'wqkv': jax.random.normal(ks[1], (DEPTH, DIM, 3 * INNER), jnp.float32) * 0.02, 'q_scale': jnp.ones((DEPTH, DIM_HEAD), jnp.float32), 'k_scale': jnp.ones((DEPTH, DIM_HEAD), jnp.float32), 'wo': jax.random.normal(ks[2], (DEPTH, INNER, DIM), jnp.float32) * 0.02, 'ln_g': jnp.ones((DEPTH, DIM), jnp.float32), 'ln_b': jnp.zeros((DEPTH, DIM), jnp.float32), 'w1': jax.random.normal(ks[3], (DEPTH, DIM, 2 * HID), jnp.float32) * 0.02, 'b1': jnp.zeros((DEPTH, 2 * HID), jnp.float32), 'w2': jax.random.normal(ks[4], (DEPTH, HID, DIM), jnp.float32) * 0.02, 'b2': jnp.zeros((DEPTH, DIM), jnp.float32)}
    _L0_ffn_in = _L0_ffn_setup()
    _d = {'L0_attn_inp': _L0_attn_in['inp'], 'L0_attn_W_logA': _L0_attn_in['W_logA'], 'L0_attn_b_logA': _L0_attn_in['b_logA'], 'L0_attn_W_XBC': _L0_attn_in['W_XBC'], 'L0_attn_b_XBC': _L0_attn_in['b_XBC'], 'L0_attn_W_gate': _L0_attn_in['W_gate'], 'L0_attn_b_gate': _L0_attn_in['b_gate'], 'L0_attn_W_out': _L0_attn_in['W_out'], 'L0_attn_b_out': _L0_attn_in['b_out'], 'L0_ffn_wqkv': _L0_ffn_in['wqkv'], 'L0_ffn_q_scale': _L0_ffn_in['q_scale'], 'L0_ffn_k_scale': _L0_ffn_in['k_scale'], 'L0_ffn_wo': _L0_ffn_in['wo'], 'L0_ffn_ln_g': _L0_ffn_in['ln_g'], 'L0_ffn_ln_b': _L0_ffn_in['ln_b'], 'L0_ffn_w1': _L0_ffn_in['w1'], 'L0_ffn_b1': _L0_ffn_in['b1'], 'L0_ffn_w2': _L0_ffn_in['w2'], 'L0_ffn_b2': _L0_ffn_in['b2']}
    _x0 = _d['L0_attn_inp']
    _d['L0_attn_inp'] = jax.random.normal(jax.random.fold_in(jax.random.key(seed), 1), (8, 512, 128), dtype=_x0.dtype)
    del _x0
    return _d

def reference(L0_attn_inp, L0_attn_W_logA, L0_attn_b_logA, L0_attn_W_XBC, L0_attn_b_XBC, L0_attn_W_gate, L0_attn_b_gate, L0_attn_W_out, L0_attn_b_out, L0_ffn_wqkv, L0_ffn_q_scale, L0_ffn_k_scale, L0_ffn_wo, L0_ffn_ln_g, L0_ffn_ln_b, L0_ffn_w1, L0_ffn_b1, L0_ffn_w2, L0_ffn_b2):

    def _L0_attn_ref(inp, W_logA, b_logA, W_XBC, b_XBC, W_gate, b_gate, W_out, b_out):
        import jax, jax.numpy as jnp
        import numpy as np
        H_HEADS = 16
        STATE_N = 64

        def _mamba2_forward(inp, W_logA, b_logA, W_XBC, b_XBC, W_gate, b_gate, W_out, b_out):
            B, T, D = inp.shape
            H, N = (H_HEADS, STATE_N)
            ch = D // H
            x = inp.reshape(B, T, H, ch)
            logA = jnp.einsum('hoc,bthc->btho', W_logA, x)[..., 0] + b_logA[:, 0]
            XBC = jax.nn.silu(jnp.einsum('hoc,bthc->btho', W_XBC, x) + b_XBC)
            X = XBC[..., :ch]
            Bm = XBC[..., ch:ch + N]
            Cm = XBC[..., ch + N:]
            cum = jnp.cumsum(jnp.swapaxes(logA, 1, 2), axis=-1)
            diff = cum[..., :, None] - cum[..., None, :]
            causal = jnp.tril(jnp.ones((T, T), dtype=bool))
            A_ss = jnp.where(causal, jnp.exp(jnp.where(causal, diff, 0.0)), 0.0)
            G = jnp.einsum('bihn,bjhn->bhij', Cm, Bm)
            Y = jnp.einsum('bhij,bjhc->bihc', A_ss * G, X)
            gate = jnp.einsum('hoc,bthc->btho', W_gate, x) + b_gate
            Yg = (gate * Y).reshape(B, T, D)
            return Yg @ W_out.T + b_out
        return _mamba2_forward(inp, W_logA, b_logA, W_XBC, b_XBC, W_gate, b_gate, W_out, b_out)

    def _L0_ffn_ref(x, wqkv, q_scale, k_scale, wo, ln_g, ln_b, w1, b1, w2, b2):
        import jax, jax.numpy as jnp
        import numpy as np
        DIM = 128
        DEPTH = 2
        HEADS = 8
        DIM_HEAD = 64
        WINDOW = 64
        INNER = HEADS * DIM_HEAD
        HID = int(DIM * 4 * 2 / 3)
        B, N = (2, 1024)
        QK_SCALE = 8.0

        def shift_token(t):
            t1, t2 = jnp.split(t, 2, axis=-1)
            t2 = jnp.pad(t2, ((0, 0), (1, 0), (0, 0)))[:, :-1]
            return jnp.concatenate([t1, t2], axis=-1)

        def l2norm(t):
            return t / jnp.clip(jnp.linalg.norm(t, axis=-1, keepdims=True), 1e-12)

        def rotate_half(x):
            x1, x2 = jnp.split(x, 2, axis=-1)
            return jnp.concatenate([-x2, x1], axis=-1)

        def rotary_xpos(q, k):
            n = q.shape[-2]
            half_idx = jnp.arange(0, DIM_HEAD, 2, dtype=jnp.float32)
            inv_freq = 1.0 / 10000.0 ** (half_idx / DIM_HEAD)
            t = jnp.arange(n, dtype=jnp.float32)
            freqs = t[:, None] * inv_freq[None, :]
            freqs = jnp.concatenate([freqs, freqs], axis=-1)
            base = (half_idx + 0.4 * DIM_HEAD) / (1.4 * DIM_HEAD)
            power = (t - n // 2) / float(WINDOW // 2)
            scale = base[None, :] ** power[:, None]
            scale = jnp.concatenate([scale, scale], axis=-1)
            cos, sin = (jnp.cos(freqs), jnp.sin(freqs))
            q = q * cos * scale + rotate_half(q) * sin * scale
            k = k * cos / scale + rotate_half(k) * sin / scale
            return (q, k)

        def local_attention(q, k, v):
            b, h, n, d = q.shape
            w = n // WINDOW
            bq = q.reshape(b, h, w, WINDOW, d) * QK_SCALE
            bk = k.reshape(b, h, w, WINDOW, d)
            bv = v.reshape(b, h, w, WINDOW, d)

            def look_around(t):
                p = jnp.pad(t, ((0, 0), (0, 0), (1, 0), (0, 0), (0, 0)))
                return jnp.concatenate([p[:, :, :w], p[:, :, 1:]], axis=3)
            bk, bv = (look_around(bk), look_around(bv))
            bt = jnp.arange(n).reshape(w, WINDOW)
            btp = jnp.pad(bt, ((1, 0), (0, 0)), constant_values=-1)
            btk = jnp.concatenate([btp[:w], btp[1:]], axis=1)
            sim = jnp.einsum('bhwid,bhwjd->bhwij', bq, bk)
            i = bt[:, :, None]
            j = btk[:, None, :]
            mask = (i < j) | (i > j + WINDOW) | (j == -1)
            sim = jnp.where(mask, -jnp.finfo(sim.dtype).max, sim)
            attn = jax.nn.softmax(sim, axis=-1)
            out = jnp.einsum('bhwij,bhwjd->bhwid', attn, bv)
            return out.reshape(b, h, n, d)

        def _layer(x, wqkv, qs, ksc, wo, lg, lb, w1, b1, w2, b2):
            b, n, _ = x.shape
            h = shift_token(x)
            qkv = h @ wqkv
            q, k, v = jnp.split(qkv, 3, axis=-1)
            to_heads = lambda t: t.reshape(b, n, HEADS, DIM_HEAD).transpose(0, 2, 1, 3)
            q, k, v = (to_heads(q), to_heads(k), to_heads(v))
            q = l2norm(q) * qs
            k = l2norm(k) * ksc
            q, k = rotary_xpos(q, k)
            o = local_attention(q, k, v)
            o = o.transpose(0, 2, 1, 3).reshape(b, n, INNER)
            x = x + o @ wo
            h = shift_token(x)
            mu = h.mean(-1, keepdims=True)
            var = h.var(-1, keepdims=True)
            h = (h - mu) / jnp.sqrt(var + 1e-05) * lg + lb
            h = h @ w1 + b1
            a, g = jnp.split(h, 2, axis=-1)
            h = a * jax.nn.gelu(g, approximate=False)
            x = x + h @ w2 + b2
            return x
        for l in range(DEPTH):
            x = _layer(x, wqkv[l], q_scale[l], k_scale[l], wo[l], ln_g[l], ln_b[l], w1[l], b1[l], w2[l], b2[l])
        return x
    x = L0_attn_inp
    x = x + _L0_attn_ref(_layernorm(x, axis=-1), L0_attn_W_logA, L0_attn_b_logA, L0_attn_W_XBC, L0_attn_b_XBC, L0_attn_W_gate, L0_attn_b_gate, L0_attn_W_out, L0_attn_b_out)
    x = x + _L0_ffn_ref(_layernorm(x, axis=-1), L0_ffn_wqkv, L0_ffn_q_scale, L0_ffn_k_scale, L0_ffn_wo, L0_ffn_ln_g, L0_ffn_ln_b, L0_ffn_w1, L0_ffn_b1, L0_ffn_w2, L0_ffn_b2)
    return x

_drawn_inputs = setup_inputs


def setup_inputs(seed=0):
    import zlib

    import numpy as np

    out = dict(_drawn_inputs(seed))
    spreads = {'L0_attn_b_logA': (-0.05000000074505806, 0.2),
     'L0_ffn_q_scale': (1.0, 0.6),
     'L0_ffn_k_scale': (1.0, 0.6),
     'L0_ffn_ln_g': (1.0, 0.6),
     'L0_ffn_ln_b': (0.0, 0.8),
     'L0_ffn_b1': (0.0, 0.8),
     'L0_ffn_b2': (0.0, 0.8)}
    factors = {'L0_attn_b_gate': 3.21,
     'L0_attn_b_out': 8.0,
     'L0_ffn_wqkv': 8.0,
     'L0_ffn_wo': 8.0,
     'L0_ffn_w1': 8.0,
     'L0_ffn_w2': 8.0}
    for name, (base, spread) in spreads.items():
        noise = np.random.default_rng([zlib.crc32(name.encode()), seed]).standard_normal(out[name].shape)
        drawn = base * np.exp(spread * noise) if base else spread * noise
        out[name] = jnp.asarray(drawn.astype(out[name].dtype))
    for name, factor in factors.items():
        out[name] = (out[name] * factor).astype(out[name].dtype)
    return out
```

```python
from contextlib import ExitStack

import concourse.bass as bass
from concourse import mybir

F32 = mybir.dt.float32
BF16 = mybir.dt.bfloat16
ALU = mybir.AluOpType
ACT = mybir.ActivationFunctionType
AX = mybir.AxisListType

NB, T, D = 8, 512, 128
P = 128
NT = T // P
MH, CH, NS = 16, D // 16, 64
PAIRS = MH // 2
HQ = 4
XW = 160
PARTS = 80
EPS = 1e-5
HEADS, DH, WIN, DEPTH = 8, 64, 64, 2
HID = D * 4 * 2 // 3
F_QKV, F_O, F_1 = 0, 1536, 2048
F_2 = F_1 + 2 * HID
F_N = F_2 + 3 * P

C_ID, C_CAUSAL, C_MASK, C_MASK0, C_CENTRE, C_NAT, C_OWN, C_SCAN, C_TAB = 0, 128, 256, 384, 512, 640, 768, 1024, 1536
C_SEL = C_TAB + 4 * NT * 64
C_NSEL = C_SEL + MH * P
C_N = C_NSEL + MH * P
W_B, W_C, W_X, W_G, W_O, W_LA, W_BB, W_BC, W_BG, W_BLA = 0, 1024, 2048, 2176, 2304, 2432, 2448, 2456, 2464, 2465
W_N = 2466


def mixer_phase(nc, x, wm, rows, consts, X1, XT):
    with ExitStack() as ctx:
        def sb(name, shape, dt=F32):
            return ctx.enter_context(nc.sbuf_tensor(name, shape, dt))

        def sem(name):
            return ctx.enter_context(nc.semaphore(name))

        cst = sb("m_const", [P, C_TAB])
        w = sb("m_w", [P, W_N])
        bias_x = sb("m_bias_x", [P, D])
        bias_o = sb("m_bias_o", [P, D])
        ident_b = sb("m_ident_b", [P, P], BF16)
        causal_b = sb("m_causal_b", [P, NT, P], BF16)
        nat_b = sb("m_nat_b", [P, P], BF16)
        sel_b = sb("m_sel_b", [P, MH, P], BF16)
        nsel_b = sb("m_nsel_b", [P, MH, P], BF16)
        half_neg = sb("m_half_neg", [P, NT])

        sums = sb("m_sums", [P, NT])
        mean = sb("m_mean", [P, NT])
        centred = sb("m_centred", [P, NT, D])
        csq = sb("m_csq", [P, NT, D])
        square_sums = sb("m_square_sums", [P, NT])
        var_eps = sb("m_var_eps", [P, NT])
        rstd = sb("m_rstd", [P, NT])
        xn = sb("m_xn", [P, NT, D])
        xnT = sb("m_xnT", [P, T])
        log_a = sb("m_log_a", [MH, T])
        cum = sb("m_cum", [MH, T])
        rest1 = sb("m_rest1", [MH, T])
        rest2 = sb("m_rest2", [MH, T])
        part2 = sb("m_part2", [MH, T], BF16)
        cum_parts = sb("m_cum_parts", [P, T], BF16)
        x_biased = sb("m_x_biased", [P, T])
        x_spread = sb("m_x_spread", [P, NT * HQ, XW])
        x_fade = sb("m_x_fade", [P, NT - 1, D])
        BT = sb("m_BT", [P, PAIRS, T])
        CT = sb("m_CT", [P, PAIRS, T])
        decay = sb("m_decay", [P, MH, T])
        sel_f = decay[:, 0:8, :].rearrange("p h t -> p (h t)")
        AG = sb("m_AG", [P, 4, T])
        B_tok = sb("m_B_tok", [P, NT - 1, PAIRS * P])
        from_start = sb("m_from_start", [P, T])
        chunk_decay = sb("m_chunk_decay", [P, NT - 2, D])
        delta = sb("m_delta", [P, NT - 1, PAIRS, 32])
        state = sb("m_state", [P, NT - 1, PAIRS, 32])
        gate = sb("m_gate", [P, T])
        y_gated = sb("m_y_gated", [P, T])
        y_inter = sb("m_y_inter", [P, T - P])
        x_plus = sb("m_x_plus", [P, T])
        xn2 = sb("m_xn2", [P, NT, D])

        psP = [ctx.enter_context(nc.psum_tensor(f"m_ring{i}", [P, 512], F32)) for i in range(2)]
        psD = [ctx.enter_context(nc.psum_tensor(f"m_diff{i}", [P, 512], F32)) for i in range(2)]
        psG = [ctx.enter_context(nc.psum_tensor(f"m_G{i}", [P, 512], F32)) for i in range(2)]
        psY = ctx.enter_context(nc.psum_tensor("m_Y", [P, 512], F32))
        psI = ctx.enter_context(nc.psum_tensor("m_I", [P, 512], F32))

        ident = cst[:, C_ID:C_ID + P]
        own = cst[:, C_OWN:C_OWN + 256].rearrange("p (a b) -> p a b", b=32)

        ring = (["xT", "la", "X"] + [k + str(p) for p in range(PAIRS) for k in "BC"] + ["gate", "start", "fade"]
                + [f"Bt{i}" for i in range(6)] + ["dS0", "dS1", "dS2", "o", "x1T"])
        uses = [len(ring[b::2]) for b in range(2)]
        ring_full = [sem(f"m_ring_full{b}") for b in range(2)]

        per = {}

        def counted(name, n):
            per[name] = n
            return name, sem(name), n

        s_const = sem("m_s_const")
        s_setup = sem("m_s_setup")
        s_x = sem("m_s_x")
        mean_done = counted("m_mean_done", 4)
        centred_done = counted("m_centred_done", 2)
        csq_done = counted("m_csq_done", 2)
        ve_done = counted("m_ve_done", 4)
        rstd_done = counted("m_rstd_done", 2)
        xn_done = counted("m_xn_done", 1)
        xnT_done = counted("m_xnT_done", 1)
        la_done = counted("m_la_done", 1)
        cum_done = counted("m_cum_done", 1)
        part_done = counted("m_part_done", 4)
        rest_done = counted("m_rest_done", 2)
        xb_done = counted("m_xb_done", 1)
        xs_done = counted("m_xs_done", 1)
        bc_done = counted("m_bc_done", 2 * PAIRS)
        gate_done = counted("m_gate_done", 1)
        start_done = counted("m_start_done", 1)
        fade_done = counted("m_fade_done", 1)
        diff_full = counted("m_diff_full", MH)
        decay_done = counted("m_decay_done", MH)
        g_full = counted("m_g_full", MH)
        ag_done = counted("m_ag_done", MH)
        y_full = counted("m_y_full", MH)
        bt_done = counted("m_bt_done", 6)
        xf_done = counted("m_xf_done", NT - 1)
        delta_done = counted("m_delta_done", 3)
        state_done = counted("m_state_done", 4)
        i_full = counted("m_i_full", 1)
        mix_done = counted("m_mix_done", 4)
        plus_done = counted("m_plus_done", 1)
        x1_done = counted("m_x1_done", 1)
        xn2_done = counted("m_xn2_done", 1)
        xT2_done = counted("m_xT2_done", 1)

        def has(eng, c, s, k=None):
            _, semaphore, n = c
            assert k is None or k > -n
            eng.wait_ge(semaphore, (s + 1) * n + (n if k is None else k))

        read_by = {"xT": (xnT_done, 1), "la": (la_done, 1), "X": (xb_done, 1), "gate": (gate_done, 1),
                   "start": (start_done, 1), "fade": (fade_done, 1), "o": (x1_done, 1), "x1T": (xT2_done, 1)}
        read_by |= {k + str(p): (bc_done, 2 * p + i + 1) for p in range(PAIRS) for i, k in enumerate("BC")}
        read_by |= {f"Bt{i}": (bt_done, i + 1) for i in range(6)}
        read_by |= {f"dS{c}": (delta_done, c + 1) for c in range(NT - 1)}

        def ring_use(name):
            i = ring.index(name)
            return i % 2, i // 2

        def ring_wait_free(eng, name, s):
            b, u = ring_use(name)
            before, k = read_by[ring[b::2][u - 1]]
            has(eng, before, s, k if u else k - before[2])
            return psP[b]

        def ring_wait_full(eng, name, s):
            b, u = ring_use(name)
            eng.wait_ge(ring_full[b], (s + 1) * uses[b] + u + 1)
            return psP[b]

        def filled(mm, name):
            mm.then_inc(ring_full[ring_use(name)[0]], 1)

        producers = {
            "pe": [diff_full, g_full, y_full, i_full],
            "act": [csq_done, xnT_done, la_done, part_done, xs_done, bc_done, gate_done, start_done, fade_done, decay_done,
                    bt_done, xT2_done],
            "dve": [mean_done, centred_done, ve_done, xn_done, cum_done, rest_done, xb_done, ag_done, xf_done, delta_done, state_done,
                    mix_done, x1_done, xn2_done],
            "pool": [rstd_done, plus_done],
        }

        def credit(eng, who):
            for _, semaphore, n in producers[who]:
                eng.sem_inc(semaphore, n)

        block = ctx.enter_context(nc.Block())

        @block.sync
        def _(sp):
            sp.dma_start(cst[:, :], consts[:, 0:C_TAB]).then_inc(s_const, 16)
            sp.dma_start(w[:, :], wm).then_inc(s_const, 16)
            sp.dma_start(sel_f, consts[:, C_SEL:C_N]).then_inc(s_const, 16)
            sp.dma_start(bias_x[:, :], rows[0:1, :].broadcast_to([P, D])).then_inc(s_const, 16)
            sp.dma_start(bias_o[:, :], rows[1:2, :].broadcast_to([P, D])).then_inc(s_const, 16)
            for s in range(NB):
                if s:
                    sp.wait_ge(s_x, 16 * s)
                sp.dma_start(X1[:, s * NT:(s + 1) * NT, :],
                             x[s].rearrange("(t p) d -> p t d", p=P)).then_inc(s_x, 16)

        @block.tensor
        def _(pe):
            credit(pe, "pe")
            for b in range(2):
                pe.sem_inc(ring_full[b], uses[b])
            pe.wait_ge(s_setup, 8)

            with pe.Fori(0, NB) as s:
                bank = ring_wait_free(pe, "xT", s)
                has(pe, xn_done, s)
                for t in range(NT):
                    mm = pe.transpose(bank[:, t * P:(t + 1) * P], xn[:, t, :], ident)
                filled(mm, "xT")

                has(pe, xnT_done, s)
                bank = ring_wait_free(pe, "la", s)
                filled(pe.matmul(bank[0:MH, :], w[:, W_LA:W_LA + MH], xnT[:, :], start=True, stop=True), "la")
                bank = ring_wait_free(pe, "X", s)
                for t in range(NT):
                    mm = pe.matmul(bank[:, t * P:(t + 1) * P], xnT[:, t * P:(t + 1) * P], w[:, W_X:W_X + D],
                                   start=True, stop=True)
                filled(mm, "X")
                for p in range(PAIRS):
                    for k, off in (("B", W_B), ("C", W_C)):
                        bank = ring_wait_free(pe, f"{k}{p}", s)
                        filled(pe.matmul(bank[:, :], w[:, off + p * P:off + (p + 1) * P], xnT[:, :], start=True,
                                         stop=True), f"{k}{p}")
                bank = ring_wait_free(pe, "gate", s)
                filled(pe.matmul(bank[:, :], w[:, W_G:W_G + D], xnT[:, :], start=True, stop=True), "gate")

                has(pe, part_done, s)
                bank = ring_wait_free(pe, "start", s)
                filled(pe.matmul(bank[:, :], nat_b[0:PARTS, :], cum_parts[0:PARTS, :], start=True, stop=True), "start")
                bank = ring_wait_free(pe, "fade", s)
                for c in range(1, NT - 1):
                    last = c * P + P - 1
                    mm = pe.matmul(bank[:, (c - 1) * D:c * D], cum_parts[0:PARTS, last:last + 1].broadcast_to([PARTS, P]),
                                   nat_b[0:PARTS, :], start=True, stop=True)
                filled(mm, "fade")

                def intra(h):
                    g, j = h // HQ, h % HQ
                    has(pe, ag_done, s, h + 1)
                    if h == 0:
                        has(pe, xs_done, s)
                        has(pe, mix_done, s, 0)
                    for c in range(NT):
                        mm = pe.matmul(psY[32 * g:32 * g + 32, c * P:(c + 1) * P],
                                       x_spread[:, c * HQ + g, 32 * j:32 * j + 32], AG[:, h % 4, c * P:(c + 1) * P],
                                       start=(j == 0 and c == 0), stop=(j == HQ - 1), skip_group_check=True)
                    mm.then_inc(y_full[1], 1)

                for h in range(MH):
                    p, r = h // 2, 64 * (h % 2)
                    has(pe, bc_done, s, 2 * p + 2)
                    has(pe, ag_done, s, h - 1)
                    for c in range(NT):
                        cols = slice(c * P, (c + 1) * P)
                        mm = pe.matmul(psG[h % 2][:, cols], BT[r:r + NS, p, cols], CT[r:r + NS, p, cols],
                                       start=True, stop=True)
                    mm.then_inc(g_full[1], 1)
                    has(pe, decay_done, s, h - 1)
                    pe.matmul(psD[h % 2][:, :], sel_b[0:PARTS, h, :], cum_parts[0:PARTS, :], start=True, stop=False,
                              skip_group_check=True)
                    pe.matmul(psD[h % 2][:, :], ident_b[:, :], causal_b[:, :, :].rearrange("p c i -> p (c i)"),
                              start=False, stop=False, skip_group_check=True)
                    for c in range(NT):
                        cols = slice(c * P, (c + 1) * P)
                        mm = pe.matmul(psD[h % 2][:, cols], cum_parts[0:PARTS, cols], nsel_b[0:PARTS, h, :],
                                       start=False, stop=(c == NT - 1), skip_group_check=True)
                    mm.then_inc(diff_full[1], 1)
                    if h:
                        intra(h - 1)
                intra(MH - 1)

                for i in range(6):
                    bank = ring_wait_free(pe, f"Bt{i}", s)
                    for q in range(4):
                        p = (i % 2) * 4 + q
                        mm = pe.transpose(bank[:, q * P:(q + 1) * P], BT[:, p, (i // 2) * P:(i // 2 + 1) * P], ident)
                    filled(mm, f"Bt{i}")
                has(pe, xf_done, s)
                for c in range(NT - 1):
                    has(pe, bt_done, s, 2 * c + 2)
                    bank = ring_wait_free(pe, f"dS{c}", s)
                    for p in range(PAIRS):
                        g = p // 2
                        mm = pe.matmul(bank[:, 32 * p:32 * p + 32], B_tok[:, c, p * P:(p + 1) * P],
                                       x_fade[:, c, 32 * g:32 * g + 32], start=True, stop=True)
                    filled(mm, f"dS{c}")
                has(pe, mix_done, s, 0)
                has(pe, delta_done, s)
                for c in range(NT - 1):
                    if c:
                        has(pe, state_done, s, 2 * c)
                    for p in range(PAIRS):
                        g = p // 2
                        mm = pe.matmul(psI[32 * g:32 * g + 32, c * P:(c + 1) * P], state[:, c, p, :],
                                       CT[:, p, (c + 1) * P:(c + 2) * P], start=(c == 0 and p % 2 == 0),
                                       stop=(p % 2 == 1), skip_group_check=True)
                mm.then_inc(i_full[1], 1)

                has(pe, mix_done, s)
                bank = ring_wait_free(pe, "o", s)
                for t in range(NT):
                    mm = pe.matmul(bank[:, t * P:(t + 1) * P], y_gated[:, t * P:(t + 1) * P], w[:, W_O:W_O + D],
                                   start=True, stop=True)
                filled(mm, "o")
                bank = ring_wait_free(pe, "x1T", s)
                has(pe, xn2_done, s)
                for t in range(NT):
                    mm = pe.transpose(bank[:, t * P:(t + 1) * P], xn2[:, t, :], ident)
                filled(mm, "x1T")

        @block.scalar
        def _(act):
            credit(act, "act")
            act.wait_ge(s_const, 80)
            act.activation(ident_b[:, :], cst[:, C_ID:C_ID + P], ACT.Copy).then_inc(s_setup, 1)
            act.activation(nat_b[:, :], cst[:, C_NAT:C_NAT + P], ACT.Copy).then_inc(s_setup, 1)
            act.activation(causal_b[:, :, :], cst[:, C_CAUSAL:C_CAUSAL + P].unsqueeze(1).broadcast_to([P, NT, P]),
                           ACT.Copy).then_inc(s_setup, 1)
            act.activation(sel_b[:, :, :].rearrange("p h i -> p (h i)"), sel_f[:, 0:MH * P], ACT.Copy).then_inc(s_setup, 1)
            act.activation(nsel_b[:, :, :].rearrange("p h i -> p (h i)"), sel_f[:, MH * P:], ACT.Copy).then_inc(s_setup, 1)
            act.wait_ge(s_setup, 8)

            with act.Fori(0, NB) as s:
                def squares(which):
                    has(act, centred_done, s, which)
                    has(act, ve_done, s, 2 * which - 3)
                    act.activation(csq[:, :, :], centred[:, :, :], ACT.Square).then_inc(csq_done[1], 1)

                squares(1)
                bank = ring_wait_full(act, "xT", s)
                act.activation(xnT[:, :], bank[:, :], ACT.Copy).then_inc(xnT_done[1], 1)
                bank = ring_wait_full(act, "la", s)
                has(act, cum_done, s, 0)
                act.activation(log_a[:, :], bank[0:MH, :], ACT.Identity,
                               bias=w[0:MH, W_BLA:W_BLA + 1]).then_inc(la_done[1], 1)

                has(act, cum_done, s)
                has(act, diff_full, s, 0)
                act.activation(cum_parts[0:MH, :], cum[:, :], ACT.Copy).then_inc(part_done[1], 1)
                has(act, xb_done, s)
                has(act, y_full, s, 0)
                has(act, xf_done, s, 0)
                act.activation(x_spread[:, :, :].rearrange("p a (h x) -> p a h x", x=40)[:, :, :, 0:CH],
                               x_biased[:, :].rearrange("p (a h x) -> p a h x", h=HQ, x=CH),
                               ACT.Silu).then_inc(xs_done[1], 1)
                has(act, rest_done, s, 1)
                act.activation(part2[:, :], rest1[:, :], ACT.Copy).then_inc(part_done[1], 1)
                act.activation(cum_parts[32:32 + MH, :], rest1[:, :], ACT.Copy).then_inc(part_done[1], 1)
                for p in range(PAIRS):
                    for k, off, to in (("B", W_BB, BT), ("C", W_BC, CT)):
                        bank = ring_wait_full(act, f"{k}{p}", s)
                        act.activation(to[:, p, :], bank[:, :], ACT.Silu,
                                       bias=w[:, off + p:off + p + 1]).then_inc(bc_done[1], 1)
                    if p == 0:
                        has(act, rest_done, s, 2)
                        act.activation(cum_parts[64:64 + MH, :], rest2[:, :], ACT.Copy).then_inc(part_done[1], 1)
                bank = ring_wait_full(act, "gate", s)
                act.activation(gate[:, :], bank[:, :], ACT.Identity, bias=w[:, W_BG:W_BG + 1]).then_inc(gate_done[1], 1)
                bank = ring_wait_full(act, "start", s)
                act.activation(from_start[:, :], bank[:, :], ACT.Exp).then_inc(start_done[1], 1)
                bank = ring_wait_full(act, "fade", s)
                act.activation(chunk_decay[:, :, :].rearrange("p c d -> p (c d)"), bank[:, 0:(NT - 2) * D],
                               ACT.Exp).then_inc(fade_done[1], 1)
                for h in range(MH):
                    has(act, diff_full, s, h + 1)
                    act.activation(decay[:, h, :], psD[h % 2][:, :], ACT.Exp).then_inc(decay_done[1], 1)
                for i in range(6):
                    bank = ring_wait_full(act, f"Bt{i}", s)
                    act.activation(B_tok[:, i // 2, (i % 2) * 512:(i % 2) * 512 + 512], bank[:, :],
                                   ACT.Copy).then_inc(bt_done[1], 1)
                squares(2)
                bank = ring_wait_full(act, "x1T", s)
                act.activation(XT[:, bass.ds(s * T, T)], bank[:, :], ACT.Copy).then_inc(xT2_done[1], 1)

        @block.gpsimd
        def _(pool):
            credit(pool, "pool")
            pool.memset(half_neg[:, :], -0.5).then_inc(s_setup, 1)
            pool.memset(cum_parts[:, :], 0.0).then_inc(s_setup, 1)
            pool.memset(x_spread[:, :, :], 0.0).then_inc(s_setup, 1)
            pool.wait_ge(s_setup, 8)

            with pool.Fori(0, NB) as s:
                has(pool, ve_done, s, 2)
                pool.tensor_tensor(rstd[:, :], var_eps[:, :], half_neg[:, :], ALU.pow).then_inc(rstd_done[1], 1)
                pool.wait_ge(s_x, (s + 1) * 16)
                has(pool, x1_done, s, 0)
                pool.tensor_tensor(x_plus[:, :].rearrange("p (t d) -> p t d", d=D), X1[:, bass.ds(s * NT, NT), :],
                                   bias_o[:, :].unsqueeze(1).broadcast_to([P, NT, D]), ALU.add).then_inc(plus_done[1], 1)
                has(pool, ve_done, s, 4)
                pool.tensor_tensor(rstd[:, :], var_eps[:, :], half_neg[:, :], ALU.pow).then_inc(rstd_done[1], 1)

        @block.vector
        def _(dve):
            credit(dve, "dve")
            dve.wait_ge(s_const, 80)
            dve.wait_ge(s_setup, 8)

            with dve.Fori(0, NB) as s:
                tiles = X1[:, bass.ds(s * NT, NT), :]

                def normalise(which, out, out_done):
                    def spread(v):
                        return v.unsqueeze(2).broadcast_to([P, NT, D])
                    dve.nop(nofuse=True)
                    dve.tensor_reduce(sums[:, :], tiles, AX.X, ALU.add).then_inc(mean_done[1], 1)
                    has(dve, mean_done, s, 2 * which - 1)
                    dve.tensor_scalar(mean[:, :], sums[:, :], 1 / D, None, ALU.mult).then_inc(mean_done[1], 1)
                    has(dve, mean_done, s, 2 * which)
                    dve.tensor_tensor(centred[:, :, :], tiles, spread(mean[:, :]), ALU.subtract).then_inc(centred_done[1], 1)
                    has(dve, csq_done, s, which)
                    dve.tensor_reduce(square_sums[:, :], csq[:, :, :], AX.X, ALU.add).then_inc(ve_done[1], 1)
                    has(dve, ve_done, s, 2 * which - 1)
                    dve.tensor_scalar(var_eps[:, :], square_sums[:, :], 1 / D, EPS, ALU.mult, ALU.add).then_inc(ve_done[1], 1)
                    has(dve, rstd_done, s, which)
                    dve.tensor_tensor(out[:, :, :], centred[:, :, :], spread(rstd[:, :]), ALU.mult).then_inc(out_done[1], 1)

                dve.wait_ge(s_x, (s + 1) * 16)
                has(dve, xn2_done, s, 0)
                has(dve, xnT_done, s, 0)
                normalise(1, xn, xn_done)

                has(dve, la_done, s)
                dve.tensor_tensor_scan(cum[:, :], cst[0:MH, C_SCAN:C_SCAN + T], log_a[:, :], 0.0, ALU.mult,
                                       ALU.add).then_inc(cum_done[1], 1)
                has(dve, part_done, s, 1)
                dve.tensor_tensor(rest1[:, :], cum[:, :], cum_parts[0:MH, :], ALU.subtract).then_inc(rest_done[1], 1)
                bank = ring_wait_full(dve, "X", s)
                has(dve, xs_done, s, 0)
                dve.tensor_tensor(x_biased[:, :].rearrange("p (t d) -> p t d", d=D), bank[:, :].rearrange("p (t d) -> p t d", d=D),
                                  bias_x[:, :].unsqueeze(1).broadcast_to([P, NT, D]), ALU.add).then_inc(xb_done[1], 1)
                has(dve, part_done, s, 2)
                has(dve, rest_done, s, 1)
                dve.tensor_tensor(rest2[:, :], rest1[:, :], part2[:, :], ALU.subtract).then_inc(rest_done[1], 1)

                for h in range(MH):
                    has(dve, g_full, s, h + 1)
                    has(dve, decay_done, s, h + 1)
                    has(dve, y_full, s, h - 3)
                    dve.tensor_tensor(AG[:, h % 4, :], psG[h % 2][:, :], decay[:, h, :], ALU.mult).then_inc(ag_done[1], 1)

                spread = x_spread[:, :, :].rearrange("p a (h x) -> p (a h) x", x=40)
                for c in range(NT - 1):
                    end = c * P + P - 1
                    has(dve, decay_done, s)
                    dve.tensor_tensor(x_fade[:, c, :].rearrange("p (h x) -> p h x", x=CH),
                                      spread[:, c * MH:(c + 1) * MH, 0:CH],
                                      decay[:, :, end:end + 1].broadcast_to([P, MH, CH]), ALU.mult).then_inc(xf_done[1], 1)

                for c in range(NT - 1):
                    bank = ring_wait_full(dve, f"dS{c}", s)
                    to = state[:, 0, :, :] if c == 0 else delta[:, c, :, :]
                    dve.tensor_tensor(to, bank[:, 0:PAIRS * 32].rearrange("p (a b) -> p a b", b=32), own,
                                      ALU.mult).then_inc(delta_done[1], 1)
                has(dve, fade_done, s)
                for c in range(1, NT - 1):
                    if c == 1:
                        has(dve, delta_done, s)
                    else:
                        has(dve, state_done, s, 2 * c - 2)
                    halves = lambda ap: ap.rearrange("p (g r) x -> p g r x", r=2)
                    dve.tensor_tensor(halves(state[:, c, :, :]), halves(state[:, c - 1, :, :]),
                                      chunk_decay[:, c - 1, :].rearrange("p (g x) -> p g x", x=32).unsqueeze(2)
                                      .broadcast_to([P, HQ, 2, 32]), ALU.mult).then_inc(state_done[1], 1)
                    has(dve, state_done, s, 2 * c - 1)
                    dve.tensor_tensor(state[:, c, :, :], state[:, c, :, :], delta[:, c, :, :],
                                      ALU.add).then_inc(state_done[1], 1)

                has(dve, i_full, s)
                has(dve, start_done, s)
                dve.tensor_tensor(y_inter[:, :], psI[:, 0:T - P], from_start[:, P:], ALU.mult).then_inc(mix_done[1], 1)
                has(dve, y_full, s)
                has(dve, gate_done, s)
                dve.tensor_tensor(y_gated[:, :], psY[:, :], gate[:, :], ALU.mult).then_inc(mix_done[1], 1)
                has(dve, mix_done, s, 1)
                dve.tensor_tensor(y_inter[:, :], y_inter[:, :], gate[:, P:], ALU.mult).then_inc(mix_done[1], 1)
                has(dve, mix_done, s, 3)
                dve.tensor_tensor(y_gated[:, P:], y_gated[:, P:], y_inter[:, :], ALU.add).then_inc(mix_done[1], 1)

                bank = ring_wait_full(dve, "o", s)
                has(dve, plus_done, s)
                dve.tensor_tensor(X1[:, bass.ds(s * NT, NT), :], bank[:, :].rearrange("p (t d) -> p t d", d=D),
                                  x_plus[:, :].rearrange("p (t d) -> p t d", d=D), ALU.add).then_inc(x1_done[1], 1)
                has(dve, x1_done, s)
                normalise(2, xn2, xn2_done)


def layers_phase(nc, wf, vecs, qk_scales, consts, XT):
    with ExitStack() as ctx:
        def sb(name, shape, dt=F32):
            return ctx.enter_context(nc.sbuf_tensor(name, shape, dt))

        def ps(name):
            return ctx.enter_context(nc.psum_tensor(name, [P, 512], F32))

        def sem(name):
            return ctx.enter_context(nc.semaphore(name))

        cst = sb("f_const", [P, C_OWN])
        tab = sb("f_tab", [P, 4, NT, DH])
        w = sb("f_w", [P, F_N])
        vec = sb("f_vec", [P, 9])
        scales = sb("f_scales", [P, 2, DH])
        cos_t = sb("f_cos_t", [P, NT, 2, DH])
        sin_t = sb("f_sin_t", [P, NT, 2, DH])
        w1s = sb("f_w1s", [P, 2 * HID])
        b1s = sb("f_b1s", [P, 6])
        half_neg = sb("f_half_neg", [P, 2 * HEADS])

        hT = sb("f_hT", [P, T])
        sq = sb("f_sq", [P, 2, 512])
        qk = sb("f_qk", [P, 2, 512])
        ssq = sb("f_ssq", [P, 2 * HEADS])
        ssq_c = sb("f_ssq_c", [P, 2 * HEADS])
        rnorm = sb("f_rnorm", [P, 2 * HEADS])
        by_cos = sb("f_by_cos", [P, 2 * 512])
        by_sin = sb("f_by_sin", [P, 2 * 512])
        qk_n = sb("f_qk_n", [P, 2 * 512])
        qT = sb("f_qT", [P, 4, P])
        kT = sb("f_kT", [P, 4, WIN + T])
        V_here = sb("f_V_here", [P, NT, HEADS, DH + 1])
        V_prev = sb("f_V_prev", [P, NT, HEADS, DH + 1])
        masked = sb("f_masked", [P, 8, P])
        top = sb("f_top", [P, 8])
        probs = sb("f_probs", [P, 8, P])
        PT = sb("f_PT", [P, 8, P])
        rden = sb("f_rden", [P, 8])
        o_tok = sb("f_o_tok", [P, 512])
        oT = sb("f_oT", [P, 4, T])
        h2T = sb("f_h2T", [P, T])
        h2c = sb("f_h2c", [P, T])
        h2sq = sb("f_h2sq", [P, T])
        var_eps = sb("f_var_eps", [P, NT])
        rstd = sb("f_rstd", [P, NT])
        one_dth = sb("f_one_dth", [P, 1])
        h2n = sb("f_h2n", [P, T])
        gelu = sb("f_gelu", [P, 3, T])
        hid = sb("f_hid", [P, 3, T])

        ps0, ps1, ps2, psF, psE, psO, psU, psW = (ps(f"f_bank{i}") for i in range(8))
        psS, psV = (psE, psO), (psU, psW)

        ident, centring = cst[:, C_ID:C_ID + P], cst[:, C_CENTRE:C_CENTRE + P]
        masks = [cst[:, m:m + P] for m in (C_MASK0, C_MASK)]

        def counted(name, n):
            return sem("f_" + name), n

        s_const, s_setup, s_w = sem("f_s_const"), sem("f_s_setup"), sem("f_s_w")
        w1s_done, b1_full, tab_done = counted("w1s_done", 1), counted("b1_full", 1), counted("tab_done", 8)
        hT_done = counted("hT_done", 1)
        q_full, k_full, v_full = counted("q_full", 4), counted("k_full", 4), counted("v_full", 4)
        shift_done = [counted(f"shift_done{u}", 32 if u < NT - 1 else 16) for u in range(NT)]
        sq_done, qk_done, v_done = counted("sq_done", 8), counted("qk_done", 8), counted("v_done", 4)
        ssq_done, cos_done, sin_done = counted("ssq_done", 12), counted("cos_done", 8), counted("sin_done", 8)
        rnorm_done, rot_done, unit_done = counted("rnorm_done", 4), counted("rot_done", 8), counted("unit_done", 4)
        tq_full, tk_full = counted("tq_full", 4), counted("tk_full", 4)
        tq_done, tk_done = counted("tq_done", 4), counted("tk_done", 4)
        sim_full = counted("sim_full", 8)
        masked_done, top_done, less_done = counted("masked_done", 8), counted("top_done", 8), counted("less_done", 8)
        probs_done = counted("probs_done", 8)
        pt_full, pt_done = counted("pt_full", 8), counted("pt_done", 8)
        pv_full, rden_done, o_done = counted("pv_full", 8), counted("rden_done", 8), counted("o_done", 8)
        ot_full, ot_done = counted("ot_full", 4), counted("ot_done", 4)
        f_full = counted("f_full", 11)
        x2_done, h2_done, h2c_done, h2sq_done = (counted(n, 1) for n in ("x2_done", "h2_done", "h2c_done", "h2sq_done"))
        ve_done, rstd_done, h2n_done = (counted(n, 1) for n in ("ve_done", "rstd_done", "h2n_done"))
        gelu_done, hid_done, y_done = counted("gelu_done", 3), counted("hid_done", 3), counted("y_done", 1)
        f_order = {"wo": (x2_done, 1), "centre": (h2sq_done, 1), "var": (ve_done, 1), "rstd": (h2n_done, 1),
                   "g0": (gelu_done, 1), "g1": (gelu_done, 2), "g2": (gelu_done, 3),
                   "a0": (hid_done, 1), "a1": (hid_done, 2), "a2": (hid_done, 3), "y": (y_done, 1)}
        names = list(f_order)

        producers = {
            "pe": [q_full, k_full, v_full, tq_full, tk_full, sim_full, pt_full, pv_full, ot_full, f_full],
            "act": [hT_done, sq_done, qk_done, v_done, tq_done, tk_done, probs_done, pt_done, ot_done, h2_done,
                    h2c_done, h2sq_done, gelu_done],
            "dve": [ssq_done, cos_done, sin_done, masked_done, top_done, less_done, rden_done, o_done, x2_done,
                    ve_done, h2n_done, hid_done, y_done],
            "pool": [rnorm_done, rot_done, unit_done, rstd_done],
            "sp": shift_done,
        }

        def credit(eng, who):
            for semaphore, n in producers[who]:
                eng.sem_inc(semaphore, n)

        def has(eng, c, G, k=None):
            l, s = G
            assert k is None or k > -c[1]
            eng.wait_ge(c[0], (l * NB + s + 1) * c[1] + (c[1] if k is None else k))

        def f_bank(eng, name, G):
            i = names.index(name)
            before, k = f_order[names[i - 1]]
            has(eng, before, G, k if i else k - before[1])
            return psF

        def f_wait(eng, name, G):
            has(eng, f_full, G, names.index(name) + 1)
            return psF

        def tile_back(l, s, t, back):
            ds, at = divmod(t - back, NT)
            if isinstance(s, int) and not 0 <= s + ds < NB:
                return None
            return (l, s + ds), at

        def seq_back(l, s, back):
            if isinstance(s, int) and not 0 <= s - back < NB:
                return None
            return l, s - back

        slots = {(2, 4): ("wo", 1), (3, 1): ("centre", 1), (3, 2): ("var", 1), (3, 3): ("rstd", 1),
                 (0, 2): ("g0", 2), (0, 3): ("g1", 2), (0, 4): ("g2", 2),
                 (1, 1): ("a0", 2), (1, 2): ("a1", 2), (1, 3): ("a2", 2), (2, 1): ("y", 2)}

        def f_slot(l, s, t, n, do):
            if (t, n) in slots:
                name, back = slots[t, n]
                G = seq_back(l, s, back)
                if G is not None:
                    do(name, G)

        def over_layers(eng, body, start=lambda l: None):
            with eng.Fori(0, DEPTH) as l:
                start(l)
                for s in (0, 1):
                    body(l, s)
                with eng.Fori(2, NB - 1) as s:
                    body(l, s)
                for s in (NB - 1, NB, NB + 1):
                    body(l, s)

        def rows_of(c):
            return min(P, HID - c * P)

        block = ctx.enter_context(nc.Block())

        @block.sync
        def _(sp):
            sp.dma_start(cst[:, :], consts[:, 0:C_OWN]).then_inc(s_const, 16)
            sp.dma_start(tab[:, :, :, :].rearrange("p a t d -> p (a t d)"), consts[:, C_TAB:C_SEL]).then_inc(s_const, 16)
            credit(sp, "sp")

            def start(l):
                sp.wait_ge(y_done[0], l * NB + 1)
                sp.dma_start(w[:, :], wf[bass.ds(l, 1), :, :].rearrange("a p n -> (a p) n")).then_inc(s_w, 16)
                sp.dma_start(vec[:, :], vecs[bass.ds(l, 1), :, :].rearrange("a p n -> (a p) n")).then_inc(s_w, 16)
                sp.dma_start(scales[:, :, :].rearrange("p a d -> p (a d)"),
                             qk_scales[bass.ds(l, 1), :].broadcast_to([P, 2 * DH])).then_inc(s_w, 16)

            def body(l, s):
                for t in range(NT):
                    now = tile_back(l, s, t, 0)
                    if now:
                        G, u = now
                        has(sp, v_done, G, u + 1)
                        has(sp, pv_full, G, 2 * u - 6)
                        sp.dma_start(V_prev[WIN:P, u, :, :], V_here[0:WIN, u, :, :]).then_inc(shift_done[u][0], 16)
                        if u < NT - 1:
                            has(sp, pv_full, G, 2 * u - 4)
                            sp.dma_start(V_prev[0:WIN, u + 1, :, :], V_here[WIN:P, u, :, :]).then_inc(shift_done[u][0], 16)

            over_layers(sp, body, start)

        @block.tensor
        def _(pe):
            credit(pe, "pe")
            pe.wait_ge(s_const, 32)
            pe.wait_ge(s_setup, 8)

            def start(l):
                pe.wait_ge(s_w, (l + 1) * 48)
                for c in range(6):
                    r, at = rows_of(c % 3), (c // 3) * HID + (c % 3) * P
                    mm = pe.matmul(psF[0:r, c:c + 1], w[:, F_1 + at:F_1 + at + r], vec[:, 7:8], start=True, stop=True)
                mm.then_inc(b1_full[0], 1)
                pe.wait_ge(w1s_done[0], l + 1)
                pe.wait_ge(tab_done[0], (l + 1) * 8)

            def half(name, G):
                bank = f_bank(pe, name, G)
                if name == "wo":
                    has(pe, ot_done, G)
                    for p in range(4):
                        mm = pe.matmul(bank[:, :], w[:, F_O + p * P:F_O + (p + 1) * P], oT[:, p, :], start=(p == 0),
                                       stop=(p == 3))
                elif name == "centre":
                    has(pe, h2_done, G)
                    mm = pe.matmul(bank[:, :], centring, h2T[:, :], start=True, stop=True)
                elif name == "var":
                    has(pe, h2sq_done, G)
                    for t in range(NT):
                        mm = pe.matmul(bank[:, t:t + 1], h2sq[:, t * P:(t + 1) * P], one_dth[:, :], start=True, stop=True)
                elif name == "rstd":
                    has(pe, rstd_done, G)
                    for t in range(NT):
                        mm = pe.matmul(bank[:, t * P:(t + 1) * P], rstd[:, t:t + 1].broadcast_to([P, P]), ident,
                                       start=True, stop=True)
                elif name == "y":
                    has(pe, hid_done, G)
                    for c in range(3):
                        r = rows_of(c)
                        mm = pe.matmul(bank[:, :], w[0:r, F_2 + c * P:F_2 + (c + 1) * P], hid[0:r, c, :],
                                       start=(c == 0), stop=(c == 2))
                else:
                    has(pe, h2n_done, G)
                    c = int(name[1])
                    r, at = rows_of(c), (HID if name[0] == "g" else 0) + c * P
                    mm = pe.matmul(bank[0:r, :], w1s[:, at:at + r], h2n[:, :], start=True, stop=True)
                mm.then_inc(f_full[0], 1)

            def body(l, s):
                for t in range(NT):
                    now, b1, b2, b3 = (tile_back(l, s, t, k) for k in range(4))
                    if now:
                        G, u = now
                        has(pe, hT_done, G)
                        x = hT[:, u * P:(u + 1) * P]
                        if not b2:
                            has(pe, qk_done, G, 2 * u - 1)
                            has(pe, v_done, G, u)
                        has(pe, tq_done, G, u - 1)
                        pe.matmul(ps0[:, :], x, w[:, F_QKV + 512:F_QKV + 1024], start=True,
                                  stop=True).then_inc(k_full[0], 1)
                        has(pe, tk_done, G, u - 1)
                        pe.matmul(ps1[:, :], x, w[:, F_QKV + 1024:F_QKV + 1536], start=True,
                                  stop=True).then_inc(v_full[0], 1)
                        has(pe, ot_done, G, u - 3)
                        has(pe, qk_done, G, 2 * u)
                        pe.matmul(ps2[:, :], x, w[:, F_QKV:F_QKV + 512], start=True, stop=True).then_inc(q_full[0], 1)
                    f_slot(l, s, t, 1, half)
                    if b1:
                        G, u = b1
                        has(pe, unit_done, G, u + 1)
                        if now:
                            has(pe, qk_done, G, 2 * (u + 1) + 1)
                        else:
                            has(pe, tk_done, G, u)
                        for p in range(4):
                            mm = pe.transpose(ps0[:, p * P:(p + 1) * P], qk_n[:, p * P:(p + 1) * P], ident)
                        mm.then_inc(tq_full[0], 1)
                        if now:
                            has(pe, v_done, G, u + 2)
                        for p in range(4):
                            mm = pe.transpose(ps1[:, p * P:(p + 1) * P], qk_n[:, 512 + p * P:512 + (p + 1) * P], ident)
                        mm.then_inc(tk_full[0], 1)
                    if b2:
                        G, u = b2
                        for e in range(2):
                            has(pe, probs_done, G, 2 * u + e + 1)
                            for p in range(4):
                                mm = pe.transpose(psS[e][:, p * P:(p + 1) * P], probs[:, e * 4 + p, :], ident)
                            mm.then_inc(pt_full[0], 1)
                    f_slot(l, s, t, 2, half)
                    if b3:
                        G, u = b3
                        has(pe, o_done, G, 2 * u + 2)
                        if now:
                            has(pe, qk_done, G, 2 * (u + 3) + 2)
                        else:
                            has(pe, ot_done, G, u)
                        for p in range(4):
                            mm = pe.transpose(ps2[:, p * P:(p + 1) * P], o_tok[:, p * P:(p + 1) * P], ident)
                        mm.then_inc(ot_full[0], 1)
                    if b2:
                        G, u = b2
                        has(pe, shift_done[u], G)
                        for e in range(2):
                            has(pe, pt_done, G, 2 * u + e + 1)
                            has(pe, o_done, G, 2 * u + e - 1)
                            for p in range(4):
                                for win, V in enumerate((V_prev, V_here)):
                                    r = slice(win * WIN, (win + 1) * WIN)
                                    mm = pe.matmul(psV[e][r, p * (DH + 1):(p + 1) * (DH + 1)], PT[:, e * 4 + p, r],
                                                   V[:, u, 2 * p + e, :], start=True, stop=True)
                            mm.then_inc(pv_full[0], 1)
                    f_slot(l, s, t, 3, half)
                    if b1:
                        G, u = b1
                        has(pe, tq_done, G, u + 1)
                        has(pe, tk_done, G, u + 1)
                        for e in range(2):
                            r = slice(e * DH, (e + 1) * DH)
                            has(pe, pt_done, G, 2 * u + e - 1)
                            pe.nop(nofuse=True)
                            for p in range(4):
                                for win in range(2):
                                    at = u * P + win * WIN
                                    mm = pe.matmul(psS[e][win * WIN:(win + 1) * WIN, p * P:(p + 1) * P],
                                                   qT[r, p, win * WIN:(win + 1) * WIN], kT[r, p, at:at + P],
                                                   start=True, stop=True)
                            mm.then_inc(sim_full[0], 1)
                    f_slot(l, s, t, 4, half)

            over_layers(pe, body, start)

        @block.scalar
        def _(act):
            credit(act, "act")
            act.wait_ge(s_setup, 8)

            def start(l):
                act.wait_ge(y_done[0], l * NB + 1)
                act.wait_ge(s_w, (l + 1) * 48)
                act.activation(w1s[:, :], w[:, F_1:F_1 + 2 * HID], ACT.Copy, scale=vec[:, 6:7]).then_inc(w1s_done[0], 1)
                shifted(hT, (l, 0), hT_done)

            def shifted(dst, G, done):
                act.activation(dst[0:64, :], XT[0:64, bass.ds(G[1] * T, T)], ACT.Copy)
                act.activation(dst[64:P, 1:T], XT[64:P, bass.ds(G[1] * T, T - 1)],
                               ACT.Copy).then_inc(done[0], 1)

            def half(name, G):
                if name == "wo":
                    has(act, x2_done, G)
                    shifted(h2T, G, h2_done)
                elif name == "centre":
                    bank = f_wait(act, name, G)
                    has(act, h2n_done, G, 0)
                    act.activation(h2c[:, :], bank[:, :], ACT.Copy).then_inc(h2c_done[0], 1)
                    act.activation(h2sq[:, :], bank[:, :], ACT.Square).then_inc(h2sq_done[0], 1)
                elif name[0] == "g":
                    bank, c = f_wait(act, name, G), int(name[1])
                    r = rows_of(c)
                    has(act, hid_done, G, 0)
                    act.activation(gelu[0:r, c, :], bank[0:r, :], ACT.Gelu, bias=b1s[0:r, 3 + c:4 + c]).then_inc(gelu_done[0], 1)

            def body(l, s):
                for t in range(NT):
                    now, b1, b2, b3 = (tile_back(l, s, t, k) for k in range(4))
                    if now:
                        G, u = now

                        def take(half_of, bank, full):
                            has(act, full, G, u + 1)
                            has(act, ssq_done, G, 3 * u - 1 - half_of)
                            act.activation(sq[:, half_of, :], bank[:, :], ACT.Square).then_inc(sq_done[0], 1)
                            has(act, sin_done, G, 2 * u - half_of)
                            act.activation(qk[:, half_of, :], bank[:, :], ACT.Copy).then_inc(qk_done[0], 1)

                        take(1, ps0, k_full)
                        has(act, v_full, G, u + 1)
                        heads = ps1[:, :].rearrange("p (h d) -> p h d", d=DH)
                        has(act, shift_done[u], G, 0)
                        act.activation(V_here[:, u, :, 0:DH], heads, ACT.Copy).then_inc(v_done[0], 1)
                    if b2:
                        for e in range(2):
                            h = slice(e * 4, e * 4 + 4)
                            has(act, less_done, b2[0], 2 * b2[1] + e + 1)
                            has(act, pt_full, b2[0], 2 * b2[1] + e - 1)
                            act.activation(probs[:, h, :], masked[:, h, :], ACT.Exp).then_inc(probs_done[0], 1)
                    f_slot(l, s, t, 1, half)
                    if now:
                        take(0, ps2, q_full)
                    if b2:
                        G, u = b2
                        has(act, pv_full, G, 2 * u)
                        for e in range(2):
                            has(act, pt_full, G, 2 * u + e + 1)
                            act.activation(PT[:, e * 4:e * 4 + 4, :], psS[e][:, :].rearrange("p (a b) -> p a b", a=4),
                                           ACT.Copy).then_inc(pt_done[0], 1)
                    f_slot(l, s, t, 2, half)
                    if b1:
                        G, u = b1
                        has(act, sim_full, G, 2 * u)
                        has(act, tq_full, G, u + 1)
                        act.activation(qT[:, :, :], ps0[:, :].rearrange("p (a b) -> p a b", a=4),
                                       ACT.Copy).then_inc(tq_done[0], 1)
                        has(act, tk_full, G, u + 1)
                        act.activation(kT[:, :, WIN + u * P:WIN + (u + 1) * P], ps1[:, :].rearrange("p (a b) -> p a b", a=4),
                                       ACT.Copy).then_inc(tk_done[0], 1)
                    if b3:
                        G, u = b3
                        has(act, ot_full, G, u + 1)
                        act.activation(oT[:, :, u * P:(u + 1) * P], ps2[:, :].rearrange("p (a b) -> p a b", a=4),
                                       ACT.Copy).then_inc(ot_done[0], 1)
                    if now and t == NT - 1 and not (isinstance(s, int) and s == NB - 1):
                        shifted(hT, (l, s + 1), hT_done)
                    f_slot(l, s, t, 3, half)
                    f_slot(l, s, t, 4, half)

            over_layers(act, body, start)

        @block.gpsimd
        def _(pool):
            credit(pool, "pool")
            for n, (part, value) in enumerate((
                    (half_neg[:, :], -0.5), (one_dth[:, :], 1 / D), (hT[64:P, 0:1], 0.0), (h2T[64:P, 0:1], 0.0), (kT[:, :, 0:WIN], 0.0),
                    (V_prev[0:WIN, 0, :, 0:DH], 0.0), (V_prev[0:WIN, 0, :, DH:DH + 1], 1.0),
                    (V_here[:, :, :, DH:DH + 1], 1.0))):
                pool.memset(part, value).then_inc(s_setup, 1)
                pool.wait_ge(s_setup, n + 1)

            def half(name, G):
                if name == "var":
                    has(pool, ve_done, G)
                    has(pool, h2n_done, G, 0)
                    pool.tensor_tensor(rstd[:, :], var_eps[:, :], half_neg[:, 0:NT], ALU.pow).then_inc(rstd_done[0], 1)

            def body(l, s):
                for t in range(NT):
                    now = tile_back(l, s, t, 0)
                    if not now:
                        f_slot(l, s, t, 2, half)
                    else:
                        G, u = now
                        for n, i in ((1, 1), (2, 0)):
                            if n == 2:
                                f_slot(l, s, t, 2, half)
                            part = slice(i * 512, (i + 1) * 512)
                            has(pool, sin_done, G, 2 * u + n)
                            has(pool, tk_full, G, u)
                            pool.tensor_tensor(qk_n[:, part], by_cos[:, part], by_sin[:, part],
                                               ALU.add).then_inc(rot_done[0], 1)
                        has(pool, ssq_done, G, 3 * u + 3)
                        has(pool, unit_done, G, u)
                        pool.tensor_tensor(rnorm[:, :], ssq_c[:, :], half_neg[:, :], ALU.pow).then_inc(rnorm_done[0], 1)
                        has(pool, rot_done, G, 2 * u + 2)
                        has(pool, rnorm_done, G, u + 1)
                        heads = qk_n[:, :].rearrange("p (h d) -> p h d", d=DH)
                        pool.tensor_tensor(heads, heads, rnorm[:, :].unsqueeze(2).broadcast_to([P, 2 * HEADS, DH]),
                                           ALU.mult).then_inc(unit_done[0], 1)

            over_layers(pool, body)

        @block.vector
        def _(dve):
            credit(dve, "dve")
            dve.wait_ge(s_const, 32)
            dve.wait_ge(s_setup, 8)

            def start(l):
                dve.wait_ge(s_w, (l + 1) * 48)
                for i in range(2):
                    scale = scales[:, i:i + 1, :].broadcast_to([P, NT, DH])
                    dve.tensor_tensor(cos_t[:, :, i, :], tab[:, 2 * i, :, :], scale, ALU.mult).then_inc(tab_done[0], 1)
                    for a, b in ((0, 32), (32, 0)):
                        dve.tensor_tensor(sin_t[:, :, i, a:a + 32], tab[:, 2 * i + 1, :, a:a + 32],
                                          scale[:, :, b:b + 32], ALU.mult).then_inc(tab_done[0], 1)
                dve.wait_ge(b1_full[0], l + 1)
                r = rows_of(2)
                b1 = vec[:, 0:6].rearrange("p (a c) -> p a c", c=3)
                b1_to = b1s[:, :].rearrange("p (a c) -> p a c", c=3)
                b1_ps = psF[:, 0:6].rearrange("p (a c) -> p a c", c=3)
                dve.tensor_tensor(b1_to[:, :, 0:2], b1_ps[:, :, 0:2], b1[:, :, 0:2], ALU.add).then_inc(tab_done[0], 1)
                dve.tensor_tensor(b1_to[0:r, :, 2:3], b1_ps[0:r, :, 2:3], b1[0:r, :, 2:3], ALU.add).then_inc(tab_done[0], 1)
                dve.wait_ge(tab_done[0], (l + 1) * 8)

            def cols(G):
                return bass.ds(G[1] * T, T)

            def half(name, G):
                if name == "wo":
                    bank = f_wait(dve, name, G)
                    x = XT[:, cols(G)]
                    dve.tensor_tensor(x, bank[:, :], x, ALU.add).then_inc(x2_done[0], 1)
                elif name == "var":
                    bank = f_wait(dve, name, G)
                    dve.tensor_scalar(var_eps[:, :], bank[:, 0:NT], EPS, None, ALU.add).then_inc(ve_done[0], 1)
                elif name == "rstd":
                    bank = f_wait(dve, name, G)
                    has(dve, h2c_done, G)
                    dve.tensor_tensor(h2n[:, :], bank[:, :], h2c[:, :], ALU.mult).then_inc(h2n_done[0], 1)
                elif name[0] == "a":
                    bank, c = f_wait(dve, name, G), int(name[1])
                    r = rows_of(c)
                    dve.scalar_tensor_tensor(out=hid[0:r, c, :], in0=bank[0:r, :], scalar=b1s[0:r, c:c + 1],
                                             in1=gelu[0:r, c, :], op0=ALU.add, op1=ALU.mult).then_inc(hid_done[0], 1)
                elif name == "y":
                    bank = f_wait(dve, name, G)
                    x = XT[:, cols(G)]
                    has(dve, x2_done, G)
                    dve.scalar_tensor_tensor(out=x, in0=bank[:, :], scalar=vec[:, 8:9], in1=x, op0=ALU.add,
                                             op1=ALU.add).then_inc(y_done[0], 1)

            def body(l, s):
                for t in range(NT):
                    now, b1, b2, _ = (tile_back(l, s, t, k) for k in range(4))

                    def by_tables(i, n):
                        G, u = now
                        x = qk[:, i, :].rearrange("p (h d) -> p h d", d=DH)
                        c = by_cos[:, i * 512:(i + 1) * 512].rearrange("p (h d) -> p h d", d=DH)
                        sn = by_sin[:, i * 512:(i + 1) * 512].rearrange("p (h d) -> p h d", d=DH)
                        tabs = sin_t[:, u, i, :].unsqueeze(1).broadcast_to([P, HEADS, DH])
                        has(dve, qk_done, G, 2 * u + n)
                        has(dve, rot_done, G, 2 * u + n - 2)
                        dve.tensor_tensor(c, x, cos_t[:, u, i, :].unsqueeze(1).broadcast_to([P, HEADS, DH]),
                                          ALU.mult).then_inc(cos_done[0], 1)
                        if n == 2:
                            f_slot(l, s, t, 2, half)
                        dve.tensor_tensor(sn[:, :, 0:32], x[:, :, 32:64], tabs[:, :, 0:32], ALU.mult)
                        dve.tensor_tensor(sn[:, :, 32:64], x[:, :, 0:32], tabs[:, :, 32:64],
                                          ALU.mult).then_inc(sin_done[0], 1)
                        has(dve, sq_done, G, 2 * u + n)
                        has(dve, ssq_done, G, 3 * u)
                        dve.tensor_reduce(ssq[:, i * HEADS:(i + 1) * HEADS], sq[:, i, :].rearrange("p (h d) -> p h d", d=DH),
                                          AX.X, ALU.add).then_inc(ssq_done[0], 1)

                    if now:
                        by_tables(1, 1)
                    f_slot(l, s, t, 1, half)
                    if now:
                        by_tables(0, 2)
                        G, u = now
                        has(dve, ssq_done, G, 3 * u + 2)
                        has(dve, rnorm_done, G, u)
                        dve.tensor_scalar(ssq_c[:, :], ssq[:, :], 1e-24, None, ALU.max).then_inc(ssq_done[0], 1)
                    else:
                        f_slot(l, s, t, 2, half)
                    if b2:
                        G, u = b2
                        has(dve, ot_full, G, u)
                        for e in range(2):
                            has(dve, pv_full, G, 2 * u + e + 1)
                            pv = psV[e][:, 0:4 * (DH + 1)].rearrange("p (a d) -> p a d", d=DH + 1)
                            dve.reciprocal(rden[:, e * 4:e * 4 + 4], pv[:, :, DH]).then_inc(rden_done[0], 1)
                        for e in range(2):
                            has(dve, rden_done, G, 2 * u + e + 1)
                            pv = psV[e][:, 0:4 * (DH + 1)].rearrange("p (a d) -> p a d", d=DH + 1)
                            dve.tensor_tensor(o_tok[:, :].rearrange("p (a e d) -> p a e d", e=2, d=DH)[:, :, e, :],
                                              pv[:, :, 0:DH], rden[:, e * 4:e * 4 + 4].unsqueeze(2).broadcast_to([P, 4, DH]),
                                              ALU.mult).then_inc(o_done[0], 1)
                    f_slot(l, s, t, 3, half)
                    if b1:
                        G, u = b1
                        for e in range(2):
                            h = slice(e * 4, e * 4 + 4)
                            has(dve, probs_done, G, 2 * u + e - 1)
                            has(dve, sim_full, G, 2 * u + e + 1)
                            dve.tensor_tensor(masked[:, h, :], psS[e][:, :].rearrange("p (a b) -> p a b", a=4),
                                              masks[min(u, 1)].unsqueeze(1).broadcast_to([P, 4, P]),
                                              ALU.add).then_inc(masked_done[0], 1)
                            has(dve, masked_done, G, 2 * u + e + 1)
                            dve.tensor_reduce(top[:, h], masked[:, h, :], AX.X, ALU.max).then_inc(top_done[0], 1)
                            has(dve, top_done, G, 2 * u + e + 1)
                            dve.tensor_tensor(masked[:, h, :], masked[:, h, :], top[:, h].unsqueeze(2).broadcast_to([P, 4, P]),
                                              ALU.subtract).then_inc(less_done[0], 1)
                    f_slot(l, s, t, 4, half)

            over_layers(dve, body, start)


def output_phase(nc, consts, X1, XT, out):
    with ExitStack() as ctx:
        ident = ctx.enter_context(nc.sbuf_tensor("o_ident", [P, P], F32))
        back = ctx.enter_context(nc.sbuf_tensor("o_back", [P, 2, T], F32))
        banks = [ctx.enter_context(nc.psum_tensor(f"o_bank{i}", [P, 512], F32)) for i in range(2)]
        s_id, s_copied, s_turned, s_added, s_out = (ctx.enter_context(nc.semaphore("o_" + n)) for n in
                                                    ("s_id", "s_copied", "s_turned", "s_added", "s_out"))
        block = ctx.enter_context(nc.Block())

        @block.sync
        def _(sp):
            sp.dma_start(ident[:, :], consts[:, C_ID:C_ID + P]).then_inc(s_id, 16)
            with sp.Fori(0, NB) as s:
                sp.wait_ge(s_added, s + 3)
                sp.dma_start(out[bass.ds(s, 1)].rearrange("a (t p) d -> p (a t) d", p=P),
                             X1[:, bass.ds(s * NT, NT), :]).then_inc(s_out, 16)
            sp.wait_ge(s_out, 16 * NB)

        @block.scalar
        def _(act):
            act.sem_inc(s_copied, 2)
            with act.Fori(0, NB // 2) as pair:
                for b in range(2):
                    s = pair * 2
                    act.wait_ge(s_turned, s + b + 1)
                    act.activation(back[:, b, :], XT[:, bass.ds((s + b) * T, T)], ACT.Copy).then_inc(s_copied, 1)

        @block.tensor
        def _(pe):
            pe.sem_inc(s_turned, 2)
            pe.wait_ge(s_id, 16)
            with pe.Fori(0, NB // 2) as pair:
                for b in range(2):
                    s = pair * 2
                    pe.wait_ge(s_copied, s + b + 3)
                    pe.wait_ge(s_added, s + b + 1)
                    for t in range(NT):
                        mm = pe.transpose(banks[b][:, t * P:(t + 1) * P], back[:, b, t * P:(t + 1) * P], ident[:, :])
                    mm.then_inc(s_turned, 1)

        @block.vector
        def _(dve):
            dve.sem_inc(s_added, 2)
            with dve.Fori(0, NB // 2) as pair:
                for b in range(2):
                    s = pair * 2
                    dve.wait_ge(s_turned, s + b + 3)
                    x = X1[:, bass.ds((s + b) * NT, NT), :]
                    dve.tensor_tensor(x, banks[b][:, :].rearrange("p (t d) -> p t d", d=D), x, ALU.add).then_inc(s_added, 1)


def program(nc, x, wm, rows, wf, vecs, qk_scales, consts, out):
    with ExitStack() as top:
        X1 = top.enter_context(nc.sbuf_tensor("X1", [P, NB * NT, D], F32))
        XT = top.enter_context(nc.sbuf_tensor("XT", [P, NB * T], F32))
        mixer_phase(nc, x, wm, rows, consts, X1, XT)
        layers_phase(nc, wf, vecs, qk_scales, consts, XT)
        output_phase(nc, consts, X1, XT, out)


def constants():
    import numpy as np
    f = np.float32
    c = np.zeros((P, C_N), f)
    j, i = np.arange(P)[:, None], np.arange(P)[None, :]
    c[:, C_ID:C_ID + P] = j == i
    c[:, C_CAUSAL:C_CAUSAL + P] = np.where(j > i, f(-1e30), f(0))
    q, k = j % 64, i
    ok = np.where(k < 64, q <= k, k - 64 <= q)
    c[:, C_MASK:C_MASK + P] = np.where(ok, f(0), f(-1e30))
    c[:, C_MASK0:C_MASK0 + P] = np.where(ok & ((j >= 64) | (k >= 64)), f(0), f(-1e30))
    c[:, C_CENTRE:C_CENTRE + P] = (j == i) - f(1 / D)
    head = np.arange(D) // CH
    for part in range(3):
        for h in range(MH):
            r = 32 * part + h
            c[r, C_NAT:C_NAT + D] = head == h
            c[r, C_SEL + h * P:C_SEL + (h + 1) * P] = 1
            c[r, C_NSEL + h * P:C_NSEL + (h + 1) * P] = -1
    for r in range(P):
        for p in range(PAIRS):
            own_head = 2 * p + r // 64
            at = C_OWN + 32 * p + (own_head % HQ) * CH
            c[r, at:at + CH] = 1
    c[:, C_SCAN:C_SCAN + T] = (np.arange(T) % P != 0)
    half = np.arange(0, DH, 2, dtype=f)
    inv_freq = f(1) / f(10000) ** (half / f(DH))
    pos = np.arange(T, dtype=f)
    angle = pos[:, None] * inv_freq[None, :]
    base = (half + f(0.4 * DH)) / f(1.4 * DH)
    scale = base[None, :] ** ((pos - T // 2) / f(WIN // 2))[:, None]
    sign = np.concatenate([-np.ones(32, f), np.ones(32, f)])
    twice = lambda m: np.concatenate([m, m], 1)
    tabs = [twice(np.cos(angle) * scale) * f(8), twice(np.sin(angle) * scale) * sign * f(8),
            twice(np.cos(angle) / scale), twice(np.sin(angle) / scale) * sign]
    tabs = np.stack(tabs).reshape(4, NT, P, DH).transpose(2, 0, 1, 3)
    c[:, C_TAB:C_SEL] = tabs.reshape(P, -1)
    return c


def kernel(**inputs):
    import numpy as np
    import concourse.bacc as bacc
    from concourse.bass_utils import run_bass_kernel_spmd

    a = {k: np.asarray(v) for k, v in inputs.items()}
    n = "L0_attn_"
    xbc, bxbc = a[n + "W_XBC"], a[n + "b_XBC"]
    wm = np.zeros((P, W_N), np.float32)
    for h in range(MH):
        r, pc = slice(h * CH, (h + 1) * CH), (h // 2) * P + (h % 2) * NS
        wm[r, W_X + h * CH:W_X + (h + 1) * CH] = xbc[h, 0:CH].T
        wm[r, W_B + pc:W_B + pc + NS] = xbc[h, CH:CH + NS].T
        wm[r, W_C + pc:W_C + pc + NS] = xbc[h, CH + NS:].T
        wm[r, W_G + h * CH:W_G + (h + 1) * CH] = a[n + "W_gate"][h].T
        wm[r, W_LA + h] = a[n + "W_logA"][h, 0]
        half = slice((h % 2) * NS, (h % 2) * NS + NS)
        wm[half, W_BB + h // 2] = bxbc[h, CH:CH + NS]
        wm[half, W_BC + h // 2] = bxbc[h, CH + NS:]
    wm[:, W_O:W_O + D] = a[n + "W_out"].T
    wm[:, W_BG] = a[n + "b_gate"].reshape(D)
    wm[0:MH, W_BLA] = a[n + "b_logA"][:, 0]
    rows = np.stack([bxbc[:, 0:CH].reshape(D), a[n + "b_out"]])

    n = "L0_ffn_"
    by_rows = lambda m: m.reshape(-1, P, m.shape[-1]).transpose(1, 0, 2).reshape(P, -1)
    wf = np.zeros((DEPTH, P, F_N), np.float32)
    vecs = np.zeros((DEPTH, P, 9), np.float32)
    for l in range(DEPTH):
        wf[l, :, F_QKV:F_O] = a[n + "wqkv"][l]
        wf[l, :, F_O:F_1] = by_rows(a[n + "wo"][l])
        wf[l, :, F_1:F_2] = a[n + "w1"][l]
        for c in range(3):
            r = min(P, HID - c * P)
            wf[l, 0:r, F_2 + c * P:F_2 + (c + 1) * P] = a[n + "w2"][l, c * P:c * P + r]
            vecs[l, 0:r, c] = a[n + "b1"][l, c * P:c * P + r]
            vecs[l, 0:r, 3 + c] = a[n + "b1"][l, HID + c * P:HID + c * P + r]
        vecs[l, :, 6], vecs[l, :, 7], vecs[l, :, 8] = a[n + "ln_g"][l], a[n + "ln_b"][l], a[n + "b2"][l]
    qk_scales = np.concatenate([a[n + "q_scale"], a[n + "k_scale"]], 1)

    arrays = {"x": a["L0_attn_inp"], "wm": wm, "rows": rows, "wf": wf, "vecs": vecs, "qk_scales": qk_scales,
              "consts": constants()}
    nc = bacc.Bacc("TRN2", target_bir_lowering=False, num_devices=1)
    args = [nc.dram_tensor(k, v.shape, mybir.dt.from_np(v.dtype), kind="ExternalInput").ap() for k, v in arrays.items()]
    out = nc.dram_tensor("out", (NB, T, D), F32, kind="ExternalOutput").ap()
    program(nc, *args, out)
    r = run_bass_kernel_spmd(nc, [arrays], core_ids=[0])
    return r.results[0]["out"]
```

```python
from contextlib import ExitStack

import concourse.bass as bass
from concourse import mybir

F32 = mybir.dt.float32
BF16 = mybir.dt.bfloat16
ALU = mybir.AluOpType
ACT = mybir.ActivationFunctionType
AX = mybir.AxisListType

NB, T, D = 8, 512, 128
P = 128
NT = T // P
MH, CH, NS = 16, D // 16, 64
PAIRS = MH // 2
HQ = 4
XW = 160
PARTS = 80
EPS = 1e-5
HEADS, DH, WIN, DEPTH = 8, 64, 64, 2
HID = D * 4 * 2 // 3
F_QKV, F_O, F_1 = 0, 1536, 2048
F_2 = F_1 + 2 * HID
F_N = F_2 + 3 * P

FADE_N = (NT - 2) * D
OUT_AT, TURN_AT, TURN1_AT, LOG_A_AT = 1, 5, 8, 10

C_ID, C_CAUSAL, C_MASK, C_MASK0, C_CENTRE, C_NAT, C_OWN, C_HEADS = 0, 128, 256, 384, 512, 640, 768, 1024
C_SCAN = C_HEADS + 2 * MH
C_TAB = C_SCAN + T
C_SEL = C_TAB + 4 * NT * 64
C_NSEL = C_SEL + MH * P
C_N = C_NSEL + MH * P
W_B, W_C, W_X, W_G, W_O, W_LA, W_BB, W_BC, W_BG, W_BLA = 0, 1024, 2048, 2176, 2304, 2432, 2448, 2456, 2464, 2465
W_N = 2466


def mixer_phase(nc, x, wm, rows, consts, X1, XT):
    with ExitStack() as ctx:
        def sb(name, shape, dt=F32):
            return ctx.enter_context(nc.sbuf_tensor(name, shape, dt))

        def sem(name):
            return ctx.enter_context(nc.semaphore(name))

        cst = sb("m_const", [P, C_TAB])
        w = sb("m_w", [P, W_N])
        bias_x = sb("m_bias_x", [P, D])
        bias_o = sb("m_bias_o", [P, D])
        ident_b = sb("m_ident_b", [P, P], BF16)
        causal_b = sb("m_causal_b", [P, NT, P], BF16)
        nat_b = sb("m_nat_b", [P, P], BF16)
        sel_b = sb("m_sel_b", [P, MH, P], BF16)
        nsel_b = sb("m_nsel_b", [P, MH, P], BF16)
        heads_b = sb("m_heads_b", [P, 2 * MH], BF16)
        half_neg = sb("m_half_neg", [P, NT])

        sums = [sb(f"m_sums{n}", [P, NT]) for n in range(2)]
        mean = [sb(f"m_mean{n}", [P, NT]) for n in range(2)]
        centred = [sb(f"m_centred{n}", [P, NT, D]) for n in range(2)]
        csq = [sb(f"m_csq{n}", [P, NT, D]) for n in range(2)]
        square_sums = [sb(f"m_square_sums{n}", [P, NT]) for n in range(2)]
        var_eps = [sb(f"m_var_eps{n}", [P, NT]) for n in range(2)]
        rstd = [sb(f"m_rstd{n}", [P, NT]) for n in range(2)]
        xn = [sb(f"m_xn{n}", [P, NT, D]) for n in range(2)]

        xnT = sb("m_xnT", [P, T])
        log_a = sb("m_log_a", [MH, T])
        cum = sb("m_cum", [MH, T])
        rest1 = sb("m_rest1", [MH, T])
        rest2 = sb("m_rest2", [MH, T])
        part2 = sb("m_part2", [MH, T], BF16)
        cum_parts = sb("m_cum_parts", [P, T], BF16)
        x_biased = sb("m_x_biased", [P, T])
        x_spread = sb("m_x_spread", [P, NT * HQ, XW])
        x_fade = sb("m_x_fade", [P, NT - 1, D])
        BT = sb("m_BT", [P, PAIRS, T])
        sel_f = BT[:, :, :].rearrange("p a t -> p (a t)")
        CT = sb("m_CT", [P, PAIRS, T])
        decay = sb("m_decay", [P, 4, T])
        AG = sb("m_AG", [P, 4, T])
        B_tok = sb("m_B_tok", [P, NT - 1, PAIRS * P])
        from_start = sb("m_from_start", [P, T])
        fades = sb("m_fades", [P, FADE_N + (NT - 1) * MH])
        delta = sb("m_delta", [P, NT - 1, PAIRS, 32])
        state = sb("m_state", [P, NT - 1, PAIRS, 32])
        gate = sb("m_gate", [P, T])
        y_gated = sb("m_y_gated", [P, T])
        y_inter = sb("m_y_inter", [P, T - P])
        x_plus = sb("m_x_plus", [P, T])

        psP = [ctx.enter_context(nc.psum_tensor(f"m_ring{i}", [P, 512], F32)) for i in range(2)]
        psD = [ctx.enter_context(nc.psum_tensor(f"m_diff{i}", [P, 512], F32)) for i in range(2)]
        psG = [ctx.enter_context(nc.psum_tensor(f"m_G{i}", [P, 512], F32)) for i in range(2)]
        psY = ctx.enter_context(nc.psum_tensor("m_Y", [P, 512], F32))
        psI = ctx.enter_context(nc.psum_tensor("m_I", [P, 512], F32))

        ident = cst[:, C_ID:C_ID + P]
        own = cst[:, C_OWN:C_OWN + 256].rearrange("p (a b) -> p a b", b=32)

        ring = (["X"] + [k + str(p) for p in range(PAIRS) for k in "BC"] + ["gate", "start", "fade"]
                + [f"Bt{i}" for i in range(6)] + ["dS0", "dS1", "dS2"])
        uses = [len(ring[b::2]) for b in range(2)]
        ring_full = [sem(f"m_ring_full{b}") for b in range(2)]

        def counted(name, n):
            return name, sem("m_" + name), n

        s_const, s_setup, s_x = sem("m_s_const"), sem("m_s_setup"), sem("m_s_x")
        norm_names = ("mean", "centred", "csq", "ve", "rstd", "xn")
        norm_done = [{k: counted(f"{k}{n}_done", 2 if k in ("mean", "ve") else 1) for k in norm_names} for n in range(2)]
        xT_full, xnT_done = counted("xT_full", 1), counted("xnT_done", 1)
        la_full, la_done, cum_done = counted("la_full", 1), counted("la_done", 1), counted("cum_done", 1)
        part_done = counted("part_done", 4)
        rest_done = counted("rest_done", 2)
        xb_done, xs_done = counted("xb_done", 1), counted("xs_done", 1)
        bc_done, gate_done = counted("bc_done", 2 * PAIRS), counted("gate_done", 1)
        start_done, fade_done = counted("start_done", 1), counted("fade_done", 1)
        diff_full, decay_done = counted("diff_full", MH), counted("decay_done", MH)
        g_full, ag_done, y_full = counted("g_full", MH), counted("ag_done", MH), counted("y_full", MH)
        bt_done, xf_done, delta_done = counted("bt_done", 6), counted("xf_done", 1), counted("delta_done", 3)
        state_done, i_full, mix_done = counted("state_done", 4), counted("i_full", 1), counted("mix_done", 4)
        plus_done, o_full, x1_done = counted("plus_done", 1), counted("o_full", 1), counted("x1_done", 1)
        x1T_full, xT2_done = counted("x1T_full", 1), counted("xT2_done", 1)

        def has(eng, c, s, k=None):
            _, semaphore, n = c
            assert k is None or k > -n
            eng.wait_ge(semaphore, (s + 1) * n + (n if k is None else k))

        read_by = {"X": (xb_done, 1), "gate": (gate_done, 1), "start": (start_done, 1), "fade": (fade_done, 1)}
        read_by |= {k + str(p): (bc_done, 2 * p + i + 1) for p in range(PAIRS) for i, k in enumerate("BC")}
        read_by |= {f"Bt{i}": (bt_done, i + 1) for i in range(6)}
        read_by |= {f"dS{c}": (delta_done, c + 1) for c in range(NT - 1)}

        def ring_use(name):
            i = ring.index(name)
            return i % 2, i // 2

        def ring_wait_free(eng, name, s):
            b, u = ring_use(name)
            before, k = read_by[ring[b::2][u - 1]]
            has(eng, before, s, k if u else k - before[2])
            return psP[b]

        def ring_wait_full(eng, name, s):
            b, u = ring_use(name)
            eng.wait_ge(ring_full[b], (s + 1) * uses[b] + u + 1)
            return psP[b]

        def filled(mm, name):
            mm.then_inc(ring_full[ring_use(name)[0]], 1)

        producers = {
            "pe": [xT_full, la_full, diff_full, g_full, y_full, i_full, o_full, x1T_full],
            "act": [norm_done[0]["csq"], norm_done[1]["csq"], xnT_done, la_done, part_done, xs_done, bc_done, gate_done,
                    start_done, fade_done, decay_done, bt_done, xT2_done],
            "dve": [norm_done[n][k] for n in range(2) for k in ("mean", "centred", "ve", "xn")]
                   + [cum_done, rest_done, xb_done, ag_done, xf_done, delta_done, state_done, mix_done, x1_done],
            "pool": [norm_done[0]["rstd"], norm_done[1]["rstd"], plus_done],
        }

        def credit(eng, who):
            for _, semaphore, n in producers[who]:
                eng.sem_inc(semaphore, n)

        def over_sequences(eng, first, body, last):
            first()
            body(0, False, True)
            with eng.Fori(1, NB - 1) as s:
                body(s, True, True)
            body(NB - 1, True, False)
            last()

        block = ctx.enter_context(nc.Block())

        @block.sync
        def _(sp):
            sp.dma_start(cst[:, :], consts[:, 0:C_TAB]).then_inc(s_const, 16)
            sp.dma_start(w[:, :], wm).then_inc(s_const, 16)
            sp.dma_start(sel_f, consts[:, C_SEL:C_N]).then_inc(s_const, 16)
            sp.dma_start(bias_x[:, :], rows[0:1, :].broadcast_to([P, D])).then_inc(s_const, 16)
            sp.dma_start(bias_o[:, :], rows[1:2, :].broadcast_to([P, D])).then_inc(s_const, 16)
            for s in range(NB):
                if s:
                    sp.wait_ge(s_x, 16 * s)
                sp.dma_start(X1[:, s * NT:(s + 1) * NT, :],
                             x[s].rearrange("(t p) d -> p t d", p=P)).then_inc(s_x, 16)

        @block.tensor
        def _(pe):
            credit(pe, "pe")
            for b in range(2):
                pe.sem_inc(ring_full[b], uses[b])
            pe.wait_ge(s_setup, 9)

            def turn_norm(n, s):
                has(pe, norm_done[n]["xn"], s)
                for t in range(NT):
                    mm = pe.transpose(psI[:, t * P:(t + 1) * P], xn[n][:, t, :], ident)
                mm.then_inc((xT_full, x1T_full)[n][1], 1)

            def turn_first(s):
                has(pe, xT2_done, s - 1, 0)
                has(pe, la_done, s - 1)
                turn_norm(0, s)

            def log_a_of(s):
                has(pe, xnT_done, s)
                pe.matmul(psI[0:MH, :], w[:, W_LA:W_LA + MH], xnT[:, :], start=True, stop=True).then_inc(la_full[1], 1)

            def project_out(s):
                has(pe, mix_done, s)
                for t in range(NT):
                    mm = pe.matmul(psI[:, t * P:(t + 1) * P], y_gated[:, t * P:(t + 1) * P], w[:, W_O:W_O + D],
                                   start=True, stop=True)
                mm.then_inc(o_full[1], 1)

            def turn_second(s):
                has(pe, x1_done, s)
                turn_norm(1, s)

            def intra(h, s):
                g, j = h // HQ, h % HQ
                has(pe, ag_done, s, h + 1)
                if h == 0:
                    has(pe, xs_done, s)
                    has(pe, mix_done, s, 0)
                for c in range(NT):
                    mm = pe.matmul(psY[32 * g:32 * g + 32, c * P:(c + 1) * P],
                                   x_spread[:, c * HQ + g, 32 * j:32 * j + 32], AG[:, h % 4, c * P:(c + 1) * P],
                                   start=(j == 0 and c == 0), stop=(j == HQ - 1), skip_group_check=True)
                mm.then_inc(y_full[1], 1)

            def states(i, s, after):
                if i < 6:
                    bank = ring_wait_free(pe, f"Bt{i}", s)
                    for q in range(4):
                        p = (i % 2) * 4 + q
                        mm = pe.transpose(bank[:, q * P:(q + 1) * P], BT[:, p, (i // 2) * P:(i // 2 + 1) * P], ident)
                    filled(mm, f"Bt{i}")
                elif i < 9:
                    c = i - 6
                    has(pe, xf_done, s)
                    has(pe, bt_done, s, 2 * c + 2)
                    bank = ring_wait_free(pe, f"dS{c}", s)
                    for p in range(PAIRS):
                        g = p // 2
                        mm = pe.matmul(bank[:, 32 * p:32 * p + 32], B_tok[:, c, p * P:(p + 1) * P],
                                       x_fade[:, c, 32 * g:32 * g + 32], start=True, stop=True)
                    filled(mm, f"dS{c}")
                elif i >= 12 and i < 15:
                    c = i - 12
                    if c == 0:
                        has(pe, delta_done, s)
                        if after:
                            has(pe, la_done, s + 1)
                        else:
                            has(pe, xT2_done, s, 0)
                    else:
                        has(pe, state_done, s, 2 * c)
                    for p in range(PAIRS):
                        g = p // 2
                        mm = pe.matmul(psI[32 * g:32 * g + 32, c * P:(c + 1) * P], state[:, c, p, :],
                                       CT[:, p, (c + 1) * P:(c + 2) * P], start=(c == 0 and p % 2 == 0),
                                       stop=(p % 2 == 1), skip_group_check=True)
                    if c == NT - 2:
                        mm.then_inc(i_full[1], 1)

            def first():
                turn_first(0)
                log_a_of(0)

            def body(s, before, after):
                has(pe, xnT_done, s)
                bank = ring_wait_free(pe, "X", s)
                for t in range(NT):
                    mm = pe.matmul(bank[:, t * P:(t + 1) * P], xnT[:, t * P:(t + 1) * P], w[:, W_X:W_X + D],
                                   start=True, stop=True)
                filled(mm, "X")
                for p in range(PAIRS):
                    for k, off in (("B", W_B), ("C", W_C)):
                        bank = ring_wait_free(pe, f"{k}{p}", s)
                        filled(pe.matmul(bank[:, :], w[:, off + p * P:off + (p + 1) * P], xnT[:, :], start=True,
                                         stop=True), f"{k}{p}")
                    if before and p == OUT_AT:
                        project_out(s - 1)
                    if before and p == TURN_AT:
                        turn_second(s - 1)
                bank = ring_wait_free(pe, "gate", s)
                filled(pe.matmul(bank[:, :], w[:, W_G:W_G + D], xnT[:, :], start=True, stop=True), "gate")

                has(pe, part_done, s)
                bank = ring_wait_free(pe, "start", s)
                filled(pe.matmul(bank[:, :], nat_b[0:PARTS, :], cum_parts[0:PARTS, :], start=True, stop=True), "start")
                bank = ring_wait_free(pe, "fade", s)
                for c in range(NT - 1):
                    end = cum_parts[0:PARTS, c * P + P - 1:c * P + P].broadcast_to([PARTS, P])
                    if c:
                        pe.matmul(bank[:, (c - 1) * D:c * D], end, nat_b[0:PARTS, :], start=True, stop=True)
                    to = bank[:, FADE_N + c * MH:FADE_N + (c + 1) * MH]
                    pe.matmul(to, end, heads_b[0:PARTS, 0:MH], start=True, stop=False)
                    mm = pe.matmul(to, cum_parts[0:PARTS, c * P:(c + 1) * P], heads_b[0:PARTS, MH:2 * MH], start=False,
                                   stop=True)
                filled(mm, "fade")

                for h in range(MH):
                    p, r = h // 2, 64 * (h % 2)
                    has(pe, bc_done, s, 2 * p + 2)
                    has(pe, ag_done, s, h - 1)
                    for c in range(NT):
                        cols = slice(c * P, (c + 1) * P)
                        mm = pe.matmul(psG[h % 2][:, cols], BT[r:r + NS, p, cols], CT[r:r + NS, p, cols],
                                       start=True, stop=True)
                    mm.then_inc(g_full[1], 1)
                    has(pe, decay_done, s, h - 1)
                    pe.matmul(psD[h % 2][:, :], sel_b[0:PARTS, h, :], cum_parts[0:PARTS, :], start=True, stop=False,
                              skip_group_check=True)
                    pe.matmul(psD[h % 2][:, :], ident_b[:, :], causal_b[:, :, :].rearrange("p c i -> p (c i)"),
                              start=False, stop=False, skip_group_check=True)
                    for c in range(NT):
                        cols = slice(c * P, (c + 1) * P)
                        mm = pe.matmul(psD[h % 2][:, cols], cum_parts[0:PARTS, cols], nsel_b[0:PARTS, h, :],
                                       start=False, stop=(c == NT - 1), skip_group_check=True)
                    mm.then_inc(diff_full[1], 1)
                    if after and h == TURN1_AT:
                        turn_first(s + 1)
                    if after and h == LOG_A_AT:
                        log_a_of(s + 1)
                    states(h, s, after)
                    if h:
                        intra(h - 1, s)
                intra(MH - 1, s)

            def last():
                project_out(NB - 1)
                turn_second(NB - 1)

            over_sequences(pe, first, body, last)

        @block.scalar
        def _(act):
            credit(act, "act")
            act.wait_ge(s_const, 80)
            act.activation(ident_b[:, :], cst[:, C_ID:C_ID + P], ACT.Copy).then_inc(s_setup, 1)
            act.activation(nat_b[:, :], cst[:, C_NAT:C_NAT + P], ACT.Copy).then_inc(s_setup, 1)
            act.activation(causal_b[:, :, :], cst[:, C_CAUSAL:C_CAUSAL + P].unsqueeze(1).broadcast_to([P, NT, P]),
                           ACT.Copy).then_inc(s_setup, 1)
            act.activation(heads_b[:, :], cst[:, C_HEADS:C_HEADS + 2 * MH], ACT.Copy).then_inc(s_setup, 1)
            act.activation(sel_b[:, :, :].rearrange("p h i -> p (h i)"), sel_f[:, 0:MH * P], ACT.Copy).then_inc(s_setup, 1)
            act.activation(nsel_b[:, :, :].rearrange("p h i -> p (h i)"), sel_f[:, MH * P:], ACT.Copy).then_inc(s_setup, 1)
            act.wait_ge(s_setup, 9)

            def squares(n, s):
                done = norm_done[n]
                has(act, done["centred"], s)
                has(act, done["ve"], s, -1)
                act.activation(csq[n][:, :, :], centred[n][:, :, :], ACT.Square).then_inc(done["csq"][1], 1)

            def xnT_of(s):
                has(act, xT_full, s)
                act.activation(xnT[:, :], psI[:, :], ACT.Copy).then_inc(xnT_done[1], 1)

            def log_a_of(s):
                has(act, la_full, s)
                has(act, cum_done, s, 0)
                act.activation(log_a[:, :], psI[0:MH, :], ACT.Identity,
                               bias=w[0:MH, W_BLA:W_BLA + 1]).then_inc(la_done[1], 1)

            def second_norm(s):
                has(act, x1T_full, s)
                act.activation(XT[:, bass.ds(s * T, T)], psI[:, :], ACT.Copy).then_inc(xT2_done[1], 1)

            def first():
                squares(0, 0)
                xnT_of(0)
                log_a_of(0)

            def body(s, before, after):
                has(act, cum_done, s)
                has(act, diff_full, s, 0)
                act.activation(cum_parts[0:MH, :], cum[:, :], ACT.Copy).then_inc(part_done[1], 1)
                has(act, xb_done, s)
                has(act, y_full, s, 0)
                has(act, xf_done, s, 0)
                act.activation(x_spread[:, :, :].rearrange("p a (h x) -> p a h x", x=40)[:, :, :, 0:CH],
                               x_biased[:, :].rearrange("p (a h x) -> p a h x", h=HQ, x=CH),
                               ACT.Silu).then_inc(xs_done[1], 1)
                has(act, g_full, s, 0)
                has(act, i_full, s, 0)
                for p in range(PAIRS):
                    for k, off, to in (("B", W_BB, BT), ("C", W_BC, CT)):
                        bank = ring_wait_full(act, f"{k}{p}", s)
                        act.activation(to[:, p, :], bank[:, :], ACT.Silu,
                                       bias=w[:, off + p:off + p + 1]).then_inc(bc_done[1], 1)
                    if p == 1:
                        has(act, rest_done, s, 1)
                        act.activation(part2[:, :], rest1[:, :], ACT.Copy).then_inc(part_done[1], 1)
                        act.activation(cum_parts[32:32 + MH, :], rest1[:, :], ACT.Copy).then_inc(part_done[1], 1)
                    if p == 2 and before:
                        squares(1, s - 1)
                    if p == 4:
                        has(act, rest_done, s, 2)
                        act.activation(cum_parts[64:64 + MH, :], rest2[:, :], ACT.Copy).then_inc(part_done[1], 1)
                    if p == TURN_AT and before:
                        second_norm(s - 1)
                bank = ring_wait_full(act, "gate", s)
                has(act, mix_done, s, 0)
                act.activation(gate[:, :], bank[:, :], ACT.Identity, bias=w[:, W_BG:W_BG + 1]).then_inc(gate_done[1], 1)
                bank = ring_wait_full(act, "start", s)
                act.activation(from_start[:, :], bank[:, :], ACT.Exp).then_inc(start_done[1], 1)
                bank = ring_wait_full(act, "fade", s)
                has(act, state_done, s, 0)
                act.activation(fades[:, :], bank[:, 0:FADE_N + (NT - 1) * MH], ACT.Exp).then_inc(fade_done[1], 1)
                for h in range(MH):
                    has(act, diff_full, s, h + 1)
                    has(act, ag_done, s, h - 3)
                    act.activation(decay[:, h % 4, :], psD[h % 2][:, :], ACT.Exp).then_inc(decay_done[1], 1)
                    if h < 6:
                        bank = ring_wait_full(act, f"Bt{h}", s)
                        has(act, delta_done, s, 0)
                        act.activation(B_tok[:, h // 2, (h % 2) * 512:(h % 2) * 512 + 512], bank[:, :],
                                       ACT.Copy).then_inc(bt_done[1], 1)
                    if after and h == 4:
                        squares(0, s + 1)
                    if after and h == TURN1_AT:
                        xnT_of(s + 1)
                    if after and h == LOG_A_AT:
                        log_a_of(s + 1)

            def last():
                squares(1, NB - 1)
                second_norm(NB - 1)

            over_sequences(act, first, body, last)

        @block.gpsimd
        def _(pool):
            credit(pool, "pool")
            pool.memset(half_neg[:, :], -0.5).then_inc(s_setup, 1)
            pool.memset(cum_parts[:, :], 0.0).then_inc(s_setup, 1)
            pool.memset(x_spread[:, :, :], 0.0).then_inc(s_setup, 1)
            pool.wait_ge(s_setup, 9)

            def inverse_root(n, s):
                has(pool, norm_done[n]["ve"], s)
                pool.tensor_tensor(rstd[n][:, :], var_eps[n][:, :], half_neg[:, :],
                                   ALU.pow).then_inc(norm_done[n]["rstd"][1], 1)

            def body(s, before, after):
                if before:
                    inverse_root(1, s - 1)
                pool.wait_ge(s_x, (s + 1) * 16)
                has(pool, x1_done, s, 0)
                pool.tensor_tensor(x_plus[:, :].rearrange("p (t d) -> p t d", d=D), X1[:, bass.ds(s * NT, NT), :],
                                   bias_o[:, :].unsqueeze(1).broadcast_to([P, NT, D]), ALU.add).then_inc(plus_done[1], 1)
                if after:
                    inverse_root(0, s + 1)

            over_sequences(pool, lambda: inverse_root(0, 0), body, lambda: inverse_root(1, NB - 1))

        @block.vector
        def _(dve):
            credit(dve, "dve")
            dve.wait_ge(s_const, 80)
            dve.wait_ge(s_setup, 9)

            def norm(n, s, step):
                done = norm_done[n]
                tiles = X1[:, bass.ds(s * NT, NT), :]

                def spread(v):
                    return v.unsqueeze(2).broadcast_to([P, NT, D])
                if step == 0:
                    dve.nop(nofuse=True)
                    dve.tensor_reduce(sums[n][:, :], tiles, AX.X, ALU.add).then_inc(done["mean"][1], 1)
                    has(dve, done["mean"], s, 1)
                    dve.tensor_scalar(mean[n][:, :], sums[n][:, :], 1 / D, None, ALU.mult).then_inc(done["mean"][1], 1)
                elif step == 1:
                    has(dve, done["mean"], s)
                    has(dve, done["csq"], s, 0)
                    has(dve, done["xn"], s, 0)
                    dve.tensor_tensor(centred[n][:, :, :], tiles, spread(mean[n][:, :]),
                                      ALU.subtract).then_inc(done["centred"][1], 1)
                elif step == 2:
                    has(dve, done["csq"], s)
                    dve.tensor_reduce(square_sums[n][:, :], csq[n][:, :, :], AX.X, ALU.add).then_inc(done["ve"][1], 1)
                    has(dve, done["ve"], s, 1)
                    dve.tensor_scalar(var_eps[n][:, :], square_sums[n][:, :], 1 / D, EPS, ALU.mult,
                                      ALU.add).then_inc(done["ve"][1], 1)
                else:
                    has(dve, (xnT_done, xT2_done)[n], s, 0)
                    has(dve, done["rstd"], s)
                    dve.tensor_tensor(xn[n][:, :, :], centred[n][:, :, :], spread(rstd[n][:, :]),
                                      ALU.mult).then_inc(done["xn"][1], 1)

            def cumulate(s):
                has(dve, part_done, s, 0)
                has(dve, rest_done, s, 0)
                has(dve, la_done, s)
                dve.tensor_tensor_scan(cum[:, :], cst[0:MH, C_SCAN:C_SCAN + T], log_a[:, :], 0.0, ALU.mult,
                                       ALU.add).then_inc(cum_done[1], 1)

            def combine(s):
                has(dve, i_full, s)
                has(dve, start_done, s)
                dve.tensor_tensor(y_inter[:, :], psI[:, 0:T - P], from_start[:, P:], ALU.mult).then_inc(mix_done[1], 1)
                has(dve, gate_done, s)
                has(dve, mix_done, s, 1)
                dve.tensor_tensor(y_inter[:, :], y_inter[:, :], gate[:, P:], ALU.mult).then_inc(mix_done[1], 1)
                has(dve, y_full, s)
                dve.tensor_tensor(y_gated[:, :], psY[:, :], gate[:, :], ALU.mult).then_inc(mix_done[1], 1)
                has(dve, mix_done, s, 3)
                dve.tensor_tensor(y_gated[:, P:], y_gated[:, P:], y_inter[:, :], ALU.add).then_inc(mix_done[1], 1)

            def add_output(s):
                has(dve, plus_done, s)
                has(dve, o_full, s)
                dve.tensor_tensor(X1[:, bass.ds(s * NT, NT), :], psI[:, :].rearrange("p (t d) -> p t d", d=D),
                                  x_plus[:, :].rearrange("p (t d) -> p t d", d=D), ALU.add).then_inc(x1_done[1], 1)
                has(dve, x1_done, s)
                for step in range(4):
                    norm(1, s, step)

            def states(i, s):
                if i == 0:
                    has(dve, fade_done, s)
                    has(dve, xs_done, s)
                    spread = x_spread[:, 0:(NT - 1) * HQ, :].rearrange("p a (h x) -> p (a h) x", x=40)
                    dve.tensor_tensor(x_fade[:, :, :].rearrange("p c (h x) -> p (c h) x", x=CH), spread[:, :, 0:CH],
                                      fades[:, FADE_N:].unsqueeze(2).broadcast_to([P, (NT - 1) * MH, CH]),
                                      ALU.mult).then_inc(xf_done[1], 1)
                elif 7 <= i < 10:
                    c = i - 7
                    bank = ring_wait_full(dve, f"dS{c}", s)
                    to = state[:, 0, :, :] if c == 0 else delta[:, c, :, :]
                    dve.tensor_tensor(to, bank[:, 0:PAIRS * 32].rearrange("p (a b) -> p a b", b=32), own,
                                      ALU.mult).then_inc(delta_done[1], 1)
                elif i in (10, 11):
                    c = i - 9
                    if c == 1:
                        has(dve, delta_done, s)
                    else:
                        has(dve, state_done, s, 2)
                    halves = lambda ap: ap.rearrange("p (g r) x -> p g r x", r=2)
                    dve.tensor_tensor(halves(state[:, c, :, :]), halves(state[:, c - 1, :, :]),
                                      fades[:, (c - 1) * D:c * D].rearrange("p (g x) -> p g x", x=32).unsqueeze(2)
                                      .broadcast_to([P, HQ, 2, 32]), ALU.mult).then_inc(state_done[1], 1)
                    has(dve, state_done, s, 2 * c - 1)
                    dve.tensor_tensor(state[:, c, :, :], state[:, c, :, :], delta[:, c, :, :],
                                      ALU.add).then_inc(state_done[1], 1)

            def first():
                dve.wait_ge(s_x, 16)
                for step in range(4):
                    norm(0, 0, step)
                cumulate(0)

            def body(s, before, after):
                if before:
                    combine(s - 1)
                bank = ring_wait_full(dve, "X", s)
                has(dve, xs_done, s, 0)
                dve.tensor_tensor(x_biased[:, :].rearrange("p (t d) -> p t d", d=D), bank[:, :].rearrange("p (t d) -> p t d", d=D),
                                  bias_x[:, :].unsqueeze(1).broadcast_to([P, NT, D]), ALU.add).then_inc(xb_done[1], 1)
                has(dve, part_done, s, 1)
                has(dve, rest_done, s, 0)
                dve.tensor_tensor(rest1[:, :], cum[:, :], cum_parts[0:MH, :], ALU.subtract).then_inc(rest_done[1], 1)
                if before:
                    add_output(s - 1)
                has(dve, part_done, s, 3)
                has(dve, rest_done, s, 1)
                dve.tensor_tensor(rest2[:, :], rest1[:, :], part2[:, :], ALU.subtract).then_inc(rest_done[1], 1)
                for h in range(MH):
                    has(dve, g_full, s, h + 1)
                    has(dve, decay_done, s, h + 1)
                    has(dve, y_full, s, h - 3)
                    dve.tensor_tensor(AG[:, h % 4, :], psG[h % 2][:, :], decay[:, h % 4, :], ALU.mult).then_inc(ag_done[1], 1)
                    states(h, s)
                    if after:
                        if h == 1:
                            dve.wait_ge(s_x, (s + 2) * 16)
                        if h in (1, 2, 4, 6):
                            norm(0, s + 1, (1, 2, 4, 6).index(h))
                        if h == LOG_A_AT + 1:
                            cumulate(s + 1)

            def last():
                combine(NB - 1)
                add_output(NB - 1)

            over_sequences(dve, first, body, last)


def layers_phase(nc, wf, vecs, qk_scales, consts, XT):
    with ExitStack() as ctx:
        def sb(name, shape, dt=F32):
            return ctx.enter_context(nc.sbuf_tensor(name, shape, dt))

        def ps(name):
            return ctx.enter_context(nc.psum_tensor(name, [P, 512], F32))

        def sem(name):
            return ctx.enter_context(nc.semaphore(name))

        cst = sb("f_const", [P, C_OWN])
        tab = sb("f_tab", [P, 4, NT, DH])
        w = sb("f_w", [P, F_N])
        vec = sb("f_vec", [P, 9])
        scales = sb("f_scales", [P, 2, DH])
        cos_t = sb("f_cos_t", [P, NT, 2, DH])
        sin_t = sb("f_sin_t", [P, NT, 2, DH])
        w1s = sb("f_w1s", [P, 2 * HID])
        b1s = sb("f_b1s", [P, 6])
        half_neg = sb("f_half_neg", [P, 2 * HEADS])

        hT = sb("f_hT", [P, T])
        sq = sb("f_sq", [P, 2, 512])
        qk = sb("f_qk", [P, 2, 512])
        ssq = sb("f_ssq", [P, 2 * HEADS])
        ssq_c = sb("f_ssq_c", [P, 2 * HEADS])
        rnorm = sb("f_rnorm", [P, 2 * HEADS])
        by_cos = sb("f_by_cos", [P, 2 * 512])
        by_sin = sb("f_by_sin", [P, 2 * 512])
        qk_n = sb("f_qk_n", [P, 2 * 512])
        qT = sb("f_qT", [P, 4, P])
        kT = sb("f_kT", [P, 4, WIN + T])
        V_here = sb("f_V_here", [P, NT, HEADS, DH + 1])
        V_prev = sb("f_V_prev", [P, NT, HEADS, DH + 1])
        masked = sb("f_masked", [P, 8, P])
        top = sb("f_top", [P, 8])
        probs = sb("f_probs", [P, 8, P])
        PT = sb("f_PT", [P, 8, P])
        rden = sb("f_rden", [P, 8])
        o_tok = sb("f_o_tok", [P, 512])
        oT = sb("f_oT", [P, 4, T])
        h2T = sb("f_h2T", [P, T])
        h2c = sb("f_h2c", [P, T])
        h2sq = sb("f_h2sq", [P, T])
        var_eps = sb("f_var_eps", [P, NT])
        rstd = sb("f_rstd", [P, NT])
        one_dth = sb("f_one_dth", [P, 1])
        h2n = sb("f_h2n", [P, T])
        gelu = sb("f_gelu", [P, 3, T])
        hid = sb("f_hid", [P, 3, T])

        ps0, ps1, ps2, psF, psE, psO, psU, psW = (ps(f"f_bank{i}") for i in range(8))
        psS, psV = (psE, psO), (psU, psW)

        ident, centring = cst[:, C_ID:C_ID + P], cst[:, C_CENTRE:C_CENTRE + P]
        masks = [cst[:, m:m + P] for m in (C_MASK0, C_MASK)]

        def counted(name, n):
            return sem("f_" + name), n

        s_const, s_setup, s_w = sem("f_s_const"), sem("f_s_setup"), sem("f_s_w")
        w1s_done, b1_full, tab_done = counted("w1s_done", 1), counted("b1_full", 1), counted("tab_done", 8)
        hT_done = counted("hT_done", 1)
        q_full, k_full, v_full = counted("q_full", 4), counted("k_full", 4), counted("v_full", 4)
        shift_done = [counted(f"shift_done{u}", 32 if u < NT - 1 else 16) for u in range(NT)]
        sq_done, qk_done, v_done = counted("sq_done", 8), counted("qk_done", 8), counted("v_done", 4)
        ssq_done, cos_done, sin_done = counted("ssq_done", 12), counted("cos_done", 8), counted("sin_done", 8)
        rnorm_done, rot_done, unit_done = counted("rnorm_done", 4), counted("rot_done", 8), counted("unit_done", 4)
        tq_full, tk_full = counted("tq_full", 4), counted("tk_full", 4)
        tq_done, tk_done = counted("tq_done", 4), counted("tk_done", 4)
        sim_full = counted("sim_full", 8)
        masked_done, top_done, less_done = counted("masked_done", 8), counted("top_done", 8), counted("less_done", 8)
        probs_done = counted("probs_done", 8)
        pt_full, pt_done = counted("pt_full", 8), counted("pt_done", 8)
        pv_full, rden_done, o_done = counted("pv_full", 8), counted("rden_done", 8), counted("o_done", 8)
        ot_full, ot_done = counted("ot_full", 4), counted("ot_done", 4)
        f_full = counted("f_full", 11)
        x2_done, h2_done, h2c_done, h2sq_done = (counted(n, 1) for n in ("x2_done", "h2_done", "h2c_done", "h2sq_done"))
        ve_done, rstd_done, h2n_done = (counted(n, 1) for n in ("ve_done", "rstd_done", "h2n_done"))
        gelu_done, hid_done, y_done = counted("gelu_done", 3), counted("hid_done", 3), counted("y_done", 1)
        f_order = {"wo": (x2_done, 1), "centre": (h2sq_done, 1), "var": (ve_done, 1), "rstd": (h2n_done, 1),
                   "g0": (gelu_done, 1), "g1": (gelu_done, 2), "g2": (gelu_done, 3),
                   "a0": (hid_done, 1), "a1": (hid_done, 2), "a2": (hid_done, 3), "y": (y_done, 1)}
        names = list(f_order)

        producers = {
            "pe": [q_full, k_full, v_full, tq_full, tk_full, sim_full, pt_full, pv_full, ot_full, f_full],
            "act": [hT_done, sq_done, qk_done, v_done, tq_done, tk_done, probs_done, pt_done, ot_done, h2_done,
                    h2c_done, h2sq_done, gelu_done],
            "dve": [ssq_done, cos_done, sin_done, masked_done, top_done, less_done, rden_done, o_done, x2_done,
                    ve_done, h2n_done, hid_done, y_done],
            "pool": [rnorm_done, rot_done, unit_done, rstd_done],
            "sp": shift_done,
        }

        def credit(eng, who):
            for semaphore, n in producers[who]:
                eng.sem_inc(semaphore, n)

        def has(eng, c, G, k=None):
            l, s = G
            assert k is None or k > -c[1]
            eng.wait_ge(c[0], (l * NB + s + 1) * c[1] + (c[1] if k is None else k))

        def f_bank(eng, name, G):
            i = names.index(name)
            before, k = f_order[names[i - 1]]
            has(eng, before, G, k if i else k - before[1])
            return psF

        def f_wait(eng, name, G):
            has(eng, f_full, G, names.index(name) + 1)
            return psF

        def tile_back(l, s, t, back):
            ds, at = divmod(t - back, NT)
            if isinstance(s, int) and not 0 <= s + ds < NB:
                return None
            return (l, s + ds), at

        def seq_back(l, s, back):
            if isinstance(s, int) and not 0 <= s - back < NB:
                return None
            return l, s - back

        slots = {(2, 4): ("wo", 1), (3, 1): ("centre", 1), (3, 2): ("var", 1), (3, 3): ("rstd", 1),
                 (0, 2): ("g0", 2), (0, 3): ("g1", 2), (0, 4): ("g2", 2),
                 (1, 1): ("a0", 2), (1, 2): ("a1", 2), (1, 3): ("a2", 2), (2, 1): ("y", 2)}

        def f_slot(l, s, t, n, do):
            if (t, n) in slots:
                name, back = slots[t, n]
                G = seq_back(l, s, back)
                if G is not None:
                    do(name, G)

        def over_layers(eng, body, start=lambda l: None):
            with eng.Fori(0, DEPTH) as l:
                start(l)
                for s in (0, 1):
                    body(l, s)
                with eng.Fori(2, NB - 1) as s:
                    body(l, s)
                for s in (NB - 1, NB, NB + 1):
                    body(l, s)

        def rows_of(c):
            return min(P, HID - c * P)

        block = ctx.enter_context(nc.Block())

        @block.sync
        def _(sp):
            sp.dma_start(cst[:, :], consts[:, 0:C_OWN]).then_inc(s_const, 16)
            sp.dma_start(tab[:, :, :, :].rearrange("p a t d -> p (a t d)"), consts[:, C_TAB:C_SEL]).then_inc(s_const, 16)
            credit(sp, "sp")

            def start(l):
                sp.wait_ge(y_done[0], l * NB + 1)
                sp.dma_start(w[:, :], wf[bass.ds(l, 1), :, :].rearrange("a p n -> (a p) n")).then_inc(s_w, 16)
                sp.dma_start(vec[:, :], vecs[bass.ds(l, 1), :, :].rearrange("a p n -> (a p) n")).then_inc(s_w, 16)
                sp.dma_start(scales[:, :, :].rearrange("p a d -> p (a d)"),
                             qk_scales[bass.ds(l, 1), :].broadcast_to([P, 2 * DH])).then_inc(s_w, 16)

            def body(l, s):
                for t in range(NT):
                    now = tile_back(l, s, t, 0)
                    if now:
                        G, u = now
                        has(sp, v_done, G, u + 1)
                        has(sp, pv_full, G, 2 * u - 6)
                        sp.dma_start(V_prev[WIN:P, u, :, :], V_here[0:WIN, u, :, :]).then_inc(shift_done[u][0], 16)
                        if u < NT - 1:
                            has(sp, pv_full, G, 2 * u - 4)
                            sp.dma_start(V_prev[0:WIN, u + 1, :, :], V_here[WIN:P, u, :, :]).then_inc(shift_done[u][0], 16)

            over_layers(sp, body, start)

        @block.tensor
        def _(pe):
            credit(pe, "pe")
            pe.wait_ge(s_const, 32)
            pe.wait_ge(s_setup, 8)

            def start(l):
                pe.wait_ge(s_w, (l + 1) * 48)
                for c in range(6):
                    r, at = rows_of(c % 3), (c // 3) * HID + (c % 3) * P
                    mm = pe.matmul(psF[0:r, c:c + 1], w[:, F_1 + at:F_1 + at + r], vec[:, 7:8], start=True, stop=True)
                mm.then_inc(b1_full[0], 1)
                pe.wait_ge(w1s_done[0], l + 1)
                pe.wait_ge(tab_done[0], (l + 1) * 8)

            def half(name, G):
                bank = f_bank(pe, name, G)
                if name == "wo":
                    has(pe, ot_done, G)
                    for p in range(4):
                        mm = pe.matmul(bank[:, :], w[:, F_O + p * P:F_O + (p + 1) * P], oT[:, p, :], start=(p == 0),
                                       stop=(p == 3))
                elif name == "centre":
                    has(pe, h2_done, G)
                    mm = pe.matmul(bank[:, :], centring, h2T[:, :], start=True, stop=True)
                elif name == "var":
                    has(pe, h2sq_done, G)
                    for t in range(NT):
                        mm = pe.matmul(bank[:, t:t + 1], h2sq[:, t * P:(t + 1) * P], one_dth[:, :], start=True, stop=True)
                elif name == "rstd":
                    has(pe, rstd_done, G)
                    for t in range(NT):
                        mm = pe.matmul(bank[:, t * P:(t + 1) * P], rstd[:, t:t + 1].broadcast_to([P, P]), ident,
                                       start=True, stop=True)
                elif name == "y":
                    has(pe, hid_done, G)
                    for c in range(3):
                        r = rows_of(c)
                        mm = pe.matmul(bank[:, :], w[0:r, F_2 + c * P:F_2 + (c + 1) * P], hid[0:r, c, :],
                                       start=(c == 0), stop=(c == 2))
                else:
                    has(pe, h2n_done, G)
                    c = int(name[1])
                    r, at = rows_of(c), (HID if name[0] == "g" else 0) + c * P
                    mm = pe.matmul(bank[0:r, :], w1s[:, at:at + r], h2n[:, :], start=True, stop=True)
                mm.then_inc(f_full[0], 1)

            def body(l, s):
                for t in range(NT):
                    now, b1, b2, b3 = (tile_back(l, s, t, k) for k in range(4))
                    if now:
                        G, u = now
                        has(pe, hT_done, G)
                        x = hT[:, u * P:(u + 1) * P]
                        if not b2:
                            has(pe, qk_done, G, 2 * u - 1)
                            has(pe, v_done, G, u)
                        has(pe, tq_done, G, u - 1)
                        pe.matmul(ps0[:, :], x, w[:, F_QKV + 512:F_QKV + 1024], start=True,
                                  stop=True).then_inc(k_full[0], 1)
                        has(pe, tk_done, G, u - 1)
                        pe.matmul(ps1[:, :], x, w[:, F_QKV + 1024:F_QKV + 1536], start=True,
                                  stop=True).then_inc(v_full[0], 1)
                        has(pe, ot_done, G, u - 3)
                        has(pe, qk_done, G, 2 * u)
                        pe.matmul(ps2[:, :], x, w[:, F_QKV:F_QKV + 512], start=True, stop=True).then_inc(q_full[0], 1)
                    f_slot(l, s, t, 1, half)
                    if b1:
                        G, u = b1
                        has(pe, unit_done, G, u + 1)
                        if now:
                            has(pe, qk_done, G, 2 * (u + 1) + 1)
                        else:
                            has(pe, tk_done, G, u)
                        for p in range(4):
                            mm = pe.transpose(ps0[:, p * P:(p + 1) * P], qk_n[:, p * P:(p + 1) * P], ident)
                        mm.then_inc(tq_full[0], 1)
                        if now:
                            has(pe, v_done, G, u + 2)
                        for p in range(4):
                            mm = pe.transpose(ps1[:, p * P:(p + 1) * P], qk_n[:, 512 + p * P:512 + (p + 1) * P], ident)
                        mm.then_inc(tk_full[0], 1)
                    if b2:
                        G, u = b2
                        for e in range(2):
                            has(pe, probs_done, G, 2 * u + e + 1)
                            for p in range(4):
                                mm = pe.transpose(psS[e][:, p * P:(p + 1) * P], probs[:, e * 4 + p, :], ident)
                            mm.then_inc(pt_full[0], 1)
                    f_slot(l, s, t, 2, half)
                    if b3:
                        G, u = b3
                        has(pe, o_done, G, 2 * u + 2)
                        if now:
                            has(pe, qk_done, G, 2 * (u + 3) + 2)
                        else:
                            has(pe, ot_done, G, u)
                        for p in range(4):
                            mm = pe.transpose(ps2[:, p * P:(p + 1) * P], o_tok[:, p * P:(p + 1) * P], ident)
                        mm.then_inc(ot_full[0], 1)
                    if b2:
                        G, u = b2
                        has(pe, shift_done[u], G)
                        for e in range(2):
                            has(pe, pt_done, G, 2 * u + e + 1)
                            has(pe, o_done, G, 2 * u + e - 1)
                            for p in range(4):
                                for win, V in enumerate((V_prev, V_here)):
                                    r = slice(win * WIN, (win + 1) * WIN)
                                    mm = pe.matmul(psV[e][r, p * (DH + 1):(p + 1) * (DH + 1)], PT[:, e * 4 + p, r],
                                                   V[:, u, 2 * p + e, :], start=True, stop=True)
                            mm.then_inc(pv_full[0], 1)
                    f_slot(l, s, t, 3, half)
                    if b1:
                        G, u = b1
                        has(pe, tq_done, G, u + 1)
                        has(pe, tk_done, G, u + 1)
                        for e in range(2):
                            r = slice(e * DH, (e + 1) * DH)
                            has(pe, pt_done, G, 2 * u + e - 1)
                            pe.nop(nofuse=True)
                            for p in range(4):
                                for win in range(2):
                                    at = u * P + win * WIN
                                    mm = pe.matmul(psS[e][win * WIN:(win + 1) * WIN, p * P:(p + 1) * P],
                                                   qT[r, p, win * WIN:(win + 1) * WIN], kT[r, p, at:at + P],
                                                   start=True, stop=True)
                            mm.then_inc(sim_full[0], 1)
                    f_slot(l, s, t, 4, half)

            over_layers(pe, body, start)

        @block.scalar
        def _(act):
            credit(act, "act")
            act.wait_ge(s_setup, 8)

            def start(l):
                act.wait_ge(y_done[0], l * NB + 1)
                act.wait_ge(s_w, (l + 1) * 48)
                act.activation(w1s[:, :], w[:, F_1:F_1 + 2 * HID], ACT.Copy, scale=vec[:, 6:7]).then_inc(w1s_done[0], 1)
                shifted(hT, (l, 0), hT_done)

            def shifted(dst, G, done):
                act.activation(dst[0:64, :], XT[0:64, bass.ds(G[1] * T, T)], ACT.Copy)
                act.activation(dst[64:P, 1:T], XT[64:P, bass.ds(G[1] * T, T - 1)],
                               ACT.Copy).then_inc(done[0], 1)

            def half(name, G):
                if name == "wo":
                    has(act, x2_done, G)
                    shifted(h2T, G, h2_done)
                elif name == "centre":
                    bank = f_wait(act, name, G)
                    has(act, h2n_done, G, 0)
                    act.activation(h2c[:, :], bank[:, :], ACT.Copy).then_inc(h2c_done[0], 1)
                    act.activation(h2sq[:, :], bank[:, :], ACT.Square).then_inc(h2sq_done[0], 1)
                elif name[0] == "g":
                    bank, c = f_wait(act, name, G), int(name[1])
                    r = rows_of(c)
                    has(act, hid_done, G, 0)
                    act.activation(gelu[0:r, c, :], bank[0:r, :], ACT.Gelu, bias=b1s[0:r, 3 + c:4 + c]).then_inc(gelu_done[0], 1)

            def body(l, s):
                for t in range(NT):
                    now, b1, b2, b3 = (tile_back(l, s, t, k) for k in range(4))
                    if now:
                        G, u = now

                        def take(half_of, bank, full):
                            has(act, full, G, u + 1)
                            has(act, ssq_done, G, 3 * u - 1 - half_of)
                            act.activation(sq[:, half_of, :], bank[:, :], ACT.Square).then_inc(sq_done[0], 1)
                            has(act, sin_done, G, 2 * u - half_of)
                            act.activation(qk[:, half_of, :], bank[:, :], ACT.Copy).then_inc(qk_done[0], 1)

                        take(1, ps0, k_full)
                        has(act, v_full, G, u + 1)
                        heads = ps1[:, :].rearrange("p (h d) -> p h d", d=DH)
                        has(act, shift_done[u], G, 0)
                        act.activation(V_here[:, u, :, 0:DH], heads, ACT.Copy).then_inc(v_done[0], 1)
                    if b2:
                        for e in range(2):
                            h = slice(e * 4, e * 4 + 4)
                            has(act, less_done, b2[0], 2 * b2[1] + e + 1)
                            has(act, pt_full, b2[0], 2 * b2[1] + e - 1)
                            act.activation(probs[:, h, :], masked[:, h, :], ACT.Exp).then_inc(probs_done[0], 1)
                    f_slot(l, s, t, 1, half)
                    if now:
                        take(0, ps2, q_full)
                    if b2:
                        G, u = b2
                        has(act, pv_full, G, 2 * u)
                        for e in range(2):
                            has(act, pt_full, G, 2 * u + e + 1)
                            act.activation(PT[:, e * 4:e * 4 + 4, :], psS[e][:, :].rearrange("p (a b) -> p a b", a=4),
                                           ACT.Copy).then_inc(pt_done[0], 1)
                    f_slot(l, s, t, 2, half)
                    if b1:
                        G, u = b1
                        has(act, sim_full, G, 2 * u)
                        has(act, tq_full, G, u + 1)
                        act.activation(qT[:, :, :], ps0[:, :].rearrange("p (a b) -> p a b", a=4),
                                       ACT.Copy).then_inc(tq_done[0], 1)
                        has(act, tk_full, G, u + 1)
                        act.activation(kT[:, :, WIN + u * P:WIN + (u + 1) * P], ps1[:, :].rearrange("p (a b) -> p a b", a=4),
                                       ACT.Copy).then_inc(tk_done[0], 1)
                    if b3:
                        G, u = b3
                        has(act, ot_full, G, u + 1)
                        act.activation(oT[:, :, u * P:(u + 1) * P], ps2[:, :].rearrange("p (a b) -> p a b", a=4),
                                       ACT.Copy).then_inc(ot_done[0], 1)
                    if now and t == NT - 1 and not (isinstance(s, int) and s == NB - 1):
                        shifted(hT, (l, s + 1), hT_done)
                    f_slot(l, s, t, 3, half)
                    f_slot(l, s, t, 4, half)

            over_layers(act, body, start)

        @block.gpsimd
        def _(pool):
            credit(pool, "pool")
            for n, (part, value) in enumerate((
                    (half_neg[:, :], -0.5), (one_dth[:, :], 1 / D), (hT[64:P, 0:1], 0.0), (h2T[64:P, 0:1], 0.0), (kT[:, :, 0:WIN], 0.0),
                    (V_prev[0:WIN, 0, :, 0:DH], 0.0), (V_prev[0:WIN, 0, :, DH:DH + 1], 1.0),
                    (V_here[:, :, :, DH:DH + 1], 1.0))):
                pool.memset(part, value).then_inc(s_setup, 1)
                pool.wait_ge(s_setup, n + 1)

            def half(name, G):
                if name == "var":
                    has(pool, ve_done, G)
                    has(pool, h2n_done, G, 0)
                    pool.tensor_tensor(rstd[:, :], var_eps[:, :], half_neg[:, 0:NT], ALU.pow).then_inc(rstd_done[0], 1)

            def body(l, s):
                for t in range(NT):
                    now = tile_back(l, s, t, 0)
                    if not now:
                        f_slot(l, s, t, 2, half)
                    else:
                        G, u = now
                        for n, i in ((1, 1), (2, 0)):
                            if n == 2:
                                f_slot(l, s, t, 2, half)
                            part = slice(i * 512, (i + 1) * 512)
                            has(pool, sin_done, G, 2 * u + n)
                            has(pool, tk_full, G, u)
                            pool.tensor_tensor(qk_n[:, part], by_cos[:, part], by_sin[:, part],
                                               ALU.add).then_inc(rot_done[0], 1)
                        has(pool, ssq_done, G, 3 * u + 3)
                        has(pool, unit_done, G, u)
                        pool.tensor_tensor(rnorm[:, :], ssq_c[:, :], half_neg[:, :], ALU.pow).then_inc(rnorm_done[0], 1)
                        has(pool, rot_done, G, 2 * u + 2)
                        has(pool, rnorm_done, G, u + 1)
                        heads = qk_n[:, :].rearrange("p (h d) -> p h d", d=DH)
                        pool.tensor_tensor(heads, heads, rnorm[:, :].unsqueeze(2).broadcast_to([P, 2 * HEADS, DH]),
                                           ALU.mult).then_inc(unit_done[0], 1)

            over_layers(pool, body)

        @block.vector
        def _(dve):
            credit(dve, "dve")
            dve.wait_ge(s_const, 32)
            dve.wait_ge(s_setup, 8)

            def start(l):
                dve.wait_ge(s_w, (l + 1) * 48)
                for i in range(2):
                    scale = scales[:, i:i + 1, :].broadcast_to([P, NT, DH])
                    dve.tensor_tensor(cos_t[:, :, i, :], tab[:, 2 * i, :, :], scale, ALU.mult).then_inc(tab_done[0], 1)
                    for a, b in ((0, 32), (32, 0)):
                        dve.tensor_tensor(sin_t[:, :, i, a:a + 32], tab[:, 2 * i + 1, :, a:a + 32],
                                          scale[:, :, b:b + 32], ALU.mult).then_inc(tab_done[0], 1)
                dve.wait_ge(b1_full[0], l + 1)
                r = rows_of(2)
                b1 = vec[:, 0:6].rearrange("p (a c) -> p a c", c=3)
                b1_to = b1s[:, :].rearrange("p (a c) -> p a c", c=3)
                b1_ps = psF[:, 0:6].rearrange("p (a c) -> p a c", c=3)
                dve.tensor_tensor(b1_to[:, :, 0:2], b1_ps[:, :, 0:2], b1[:, :, 0:2], ALU.add).then_inc(tab_done[0], 1)
                dve.tensor_tensor(b1_to[0:r, :, 2:3], b1_ps[0:r, :, 2:3], b1[0:r, :, 2:3], ALU.add).then_inc(tab_done[0], 1)
                dve.wait_ge(tab_done[0], (l + 1) * 8)

            def cols(G):
                return bass.ds(G[1] * T, T)

            def half(name, G):
                if name == "wo":
                    bank = f_wait(dve, name, G)
                    x = XT[:, cols(G)]
                    dve.tensor_tensor(x, bank[:, :], x, ALU.add).then_inc(x2_done[0], 1)
                elif name == "var":
                    bank = f_wait(dve, name, G)
                    dve.tensor_scalar(var_eps[:, :], bank[:, 0:NT], EPS, None, ALU.add).then_inc(ve_done[0], 1)
                elif name == "rstd":
                    bank = f_wait(dve, name, G)
                    has(dve, h2c_done, G)
                    dve.tensor_tensor(h2n[:, :], bank[:, :], h2c[:, :], ALU.mult).then_inc(h2n_done[0], 1)
                elif name[0] == "a":
                    bank, c = f_wait(dve, name, G), int(name[1])
                    r = rows_of(c)
                    dve.scalar_tensor_tensor(out=hid[0:r, c, :], in0=bank[0:r, :], scalar=b1s[0:r, c:c + 1],
                                             in1=gelu[0:r, c, :], op0=ALU.add, op1=ALU.mult).then_inc(hid_done[0], 1)
                elif name == "y":
                    bank = f_wait(dve, name, G)
                    x = XT[:, cols(G)]
                    has(dve, x2_done, G)
                    dve.scalar_tensor_tensor(out=x, in0=bank[:, :], scalar=vec[:, 8:9], in1=x, op0=ALU.add,
                                             op1=ALU.add).then_inc(y_done[0], 1)

            def body(l, s):
                for t in range(NT):
                    now, b1, b2, _ = (tile_back(l, s, t, k) for k in range(4))

                    def by_tables(i, n):
                        G, u = now
                        x = qk[:, i, :].rearrange("p (h d) -> p h d", d=DH)
                        c = by_cos[:, i * 512:(i + 1) * 512].rearrange("p (h d) -> p h d", d=DH)
                        sn = by_sin[:, i * 512:(i + 1) * 512].rearrange("p (h d) -> p h d", d=DH)
                        tabs = sin_t[:, u, i, :].unsqueeze(1).broadcast_to([P, HEADS, DH])
                        has(dve, qk_done, G, 2 * u + n)
                        has(dve, rot_done, G, 2 * u + n - 2)
                        dve.tensor_tensor(c, x, cos_t[:, u, i, :].unsqueeze(1).broadcast_to([P, HEADS, DH]),
                                          ALU.mult).then_inc(cos_done[0], 1)
                        if n == 2:
                            f_slot(l, s, t, 2, half)
                        dve.tensor_tensor(sn[:, :, 0:32], x[:, :, 32:64], tabs[:, :, 0:32], ALU.mult)
                        dve.tensor_tensor(sn[:, :, 32:64], x[:, :, 0:32], tabs[:, :, 32:64],
                                          ALU.mult).then_inc(sin_done[0], 1)
                        has(dve, sq_done, G, 2 * u + n)
                        has(dve, ssq_done, G, 3 * u)
                        dve.tensor_reduce(ssq[:, i * HEADS:(i + 1) * HEADS], sq[:, i, :].rearrange("p (h d) -> p h d", d=DH),
                                          AX.X, ALU.add).then_inc(ssq_done[0], 1)

                    if now:
                        by_tables(1, 1)
                    f_slot(l, s, t, 1, half)
                    if now:
                        by_tables(0, 2)
                        G, u = now
                        has(dve, ssq_done, G, 3 * u + 2)
                        has(dve, rnorm_done, G, u)
                        dve.tensor_scalar(ssq_c[:, :], ssq[:, :], 1e-24, None, ALU.max).then_inc(ssq_done[0], 1)
                    else:
                        f_slot(l, s, t, 2, half)
                    if b2:
                        G, u = b2
                        has(dve, ot_full, G, u)
                        for e in range(2):
                            has(dve, pv_full, G, 2 * u + e + 1)
                            pv = psV[e][:, 0:4 * (DH + 1)].rearrange("p (a d) -> p a d", d=DH + 1)
                            dve.reciprocal(rden[:, e * 4:e * 4 + 4], pv[:, :, DH]).then_inc(rden_done[0], 1)
                        for e in range(2):
                            has(dve, rden_done, G, 2 * u + e + 1)
                            pv = psV[e][:, 0:4 * (DH + 1)].rearrange("p (a d) -> p a d", d=DH + 1)
                            dve.tensor_tensor(o_tok[:, :].rearrange("p (a e d) -> p a e d", e=2, d=DH)[:, :, e, :],
                                              pv[:, :, 0:DH], rden[:, e * 4:e * 4 + 4].unsqueeze(2).broadcast_to([P, 4, DH]),
                                              ALU.mult).then_inc(o_done[0], 1)
                    f_slot(l, s, t, 3, half)
                    if b1:
                        G, u = b1
                        for e in range(2):
                            h = slice(e * 4, e * 4 + 4)
                            has(dve, probs_done, G, 2 * u + e - 1)
                            has(dve, sim_full, G, 2 * u + e + 1)
                            dve.tensor_tensor(masked[:, h, :], psS[e][:, :].rearrange("p (a b) -> p a b", a=4),
                                              masks[min(u, 1)].unsqueeze(1).broadcast_to([P, 4, P]),
                                              ALU.add).then_inc(masked_done[0], 1)
                            has(dve, masked_done, G, 2 * u + e + 1)
                            dve.tensor_reduce(top[:, h], masked[:, h, :], AX.X, ALU.max).then_inc(top_done[0], 1)
                            has(dve, top_done, G, 2 * u + e + 1)
                            dve.tensor_tensor(masked[:, h, :], masked[:, h, :], top[:, h].unsqueeze(2).broadcast_to([P, 4, P]),
                                              ALU.subtract).then_inc(less_done[0], 1)
                    f_slot(l, s, t, 4, half)

            over_layers(dve, body, start)


def output_phase(nc, consts, X1, XT, out):
    with ExitStack() as ctx:
        ident = ctx.enter_context(nc.sbuf_tensor("o_ident", [P, P], F32))
        back = ctx.enter_context(nc.sbuf_tensor("o_back", [P, 2, T], F32))
        banks = [ctx.enter_context(nc.psum_tensor(f"o_bank{i}", [P, 512], F32)) for i in range(2)]
        s_id, s_copied, s_turned, s_added, s_out = (ctx.enter_context(nc.semaphore("o_" + n)) for n in
                                                    ("s_id", "s_copied", "s_turned", "s_added", "s_out"))
        block = ctx.enter_context(nc.Block())

        @block.sync
        def _(sp):
            sp.dma_start(ident[:, :], consts[:, C_ID:C_ID + P]).then_inc(s_id, 16)
            with sp.Fori(0, NB) as s:
                sp.wait_ge(s_added, s + 3)
                sp.dma_start(out[bass.ds(s, 1)].rearrange("a (t p) d -> p (a t) d", p=P),
                             X1[:, bass.ds(s * NT, NT), :]).then_inc(s_out, 16)
            sp.wait_ge(s_out, 16 * NB)

        @block.scalar
        def _(act):
            act.sem_inc(s_copied, 2)
            with act.Fori(0, NB // 2) as pair:
                for b in range(2):
                    s = pair * 2
                    act.wait_ge(s_turned, s + b + 1)
                    act.activation(back[:, b, :], XT[:, bass.ds((s + b) * T, T)], ACT.Copy).then_inc(s_copied, 1)

        @block.tensor
        def _(pe):
            pe.sem_inc(s_turned, 2)
            pe.wait_ge(s_id, 16)
            with pe.Fori(0, NB // 2) as pair:
                for b in range(2):
                    s = pair * 2
                    pe.wait_ge(s_copied, s + b + 3)
                    pe.wait_ge(s_added, s + b + 1)
                    for t in range(NT):
                        mm = pe.transpose(banks[b][:, t * P:(t + 1) * P], back[:, b, t * P:(t + 1) * P], ident[:, :])
                    mm.then_inc(s_turned, 1)

        @block.vector
        def _(dve):
            dve.sem_inc(s_added, 2)
            with dve.Fori(0, NB // 2) as pair:
                for b in range(2):
                    s = pair * 2
                    dve.wait_ge(s_turned, s + b + 3)
                    x = X1[:, bass.ds((s + b) * NT, NT), :]
                    dve.tensor_tensor(x, banks[b][:, :].rearrange("p (t d) -> p t d", d=D), x, ALU.add).then_inc(s_added, 1)


def program(nc, x, wm, rows, wf, vecs, qk_scales, consts, out):
    with ExitStack() as top:
        X1 = top.enter_context(nc.sbuf_tensor("X1", [P, NB * NT, D], F32))
        XT = top.enter_context(nc.sbuf_tensor("XT", [P, NB * T], F32))
        mixer_phase(nc, x, wm, rows, consts, X1, XT)
        layers_phase(nc, wf, vecs, qk_scales, consts, XT)
        output_phase(nc, consts, X1, XT, out)


def constants():
    import numpy as np
    f = np.float32
    c = np.zeros((P, C_N), f)
    j, i = np.arange(P)[:, None], np.arange(P)[None, :]
    c[:, C_ID:C_ID + P] = j == i
    c[:, C_CAUSAL:C_CAUSAL + P] = np.where(j > i, f(-1e30), f(0))
    q, k = j % 64, i
    ok = np.where(k < 64, q <= k, k - 64 <= q)
    c[:, C_MASK:C_MASK + P] = np.where(ok, f(0), f(-1e30))
    c[:, C_MASK0:C_MASK0 + P] = np.where(ok & ((j >= 64) | (k >= 64)), f(0), f(-1e30))
    c[:, C_CENTRE:C_CENTRE + P] = (j == i) - f(1 / D)
    head = np.arange(D) // CH
    for part in range(3):
        for h in range(MH):
            r = 32 * part + h
            c[r, C_NAT:C_NAT + D] = head == h
            c[r, C_HEADS + h], c[r, C_HEADS + MH + h] = 1, -1
            c[r, C_SEL + h * P:C_SEL + (h + 1) * P] = 1
            c[r, C_NSEL + h * P:C_NSEL + (h + 1) * P] = -1
    for r in range(P):
        for p in range(PAIRS):
            own_head = 2 * p + r // 64
            at = C_OWN + 32 * p + (own_head % HQ) * CH
            c[r, at:at + CH] = 1
    c[:, C_SCAN:C_SCAN + T] = (np.arange(T) % P != 0)
    half = np.arange(0, DH, 2, dtype=f)
    inv_freq = f(1) / f(10000) ** (half / f(DH))
    pos = np.arange(T, dtype=f)
    angle = pos[:, None] * inv_freq[None, :]
    base = (half + f(0.4 * DH)) / f(1.4 * DH)
    scale = base[None, :] ** ((pos - T // 2) / f(WIN // 2))[:, None]
    sign = np.concatenate([-np.ones(32, f), np.ones(32, f)])
    twice = lambda m: np.concatenate([m, m], 1)
    tabs = [twice(np.cos(angle) * scale) * f(8), twice(np.sin(angle) * scale) * sign * f(8),
            twice(np.cos(angle) / scale), twice(np.sin(angle) / scale) * sign]
    tabs = np.stack(tabs).reshape(4, NT, P, DH).transpose(2, 0, 1, 3)
    c[:, C_TAB:C_SEL] = tabs.reshape(P, -1)
    return c


def kernel(**inputs):
    import numpy as np
    import concourse.bacc as bacc
    from concourse.bass_utils import run_bass_kernel_spmd

    a = {k: np.asarray(v) for k, v in inputs.items()}
    n = "L0_attn_"
    xbc, bxbc = a[n + "W_XBC"], a[n + "b_XBC"]
    wm = np.zeros((P, W_N), np.float32)
    for h in range(MH):
        r, pc = slice(h * CH, (h + 1) * CH), (h // 2) * P + (h % 2) * NS
        wm[r, W_X + h * CH:W_X + (h + 1) * CH] = xbc[h, 0:CH].T
        wm[r, W_B + pc:W_B + pc + NS] = xbc[h, CH:CH + NS].T
        wm[r, W_C + pc:W_C + pc + NS] = xbc[h, CH + NS:].T
        wm[r, W_G + h * CH:W_G + (h + 1) * CH] = a[n + "W_gate"][h].T
        wm[r, W_LA + h] = a[n + "W_logA"][h, 0]
        half = slice((h % 2) * NS, (h % 2) * NS + NS)
        wm[half, W_BB + h // 2] = bxbc[h, CH:CH + NS]
        wm[half, W_BC + h // 2] = bxbc[h, CH + NS:]
    wm[:, W_O:W_O + D] = a[n + "W_out"].T
    wm[:, W_BG] = a[n + "b_gate"].reshape(D)
    wm[0:MH, W_BLA] = a[n + "b_logA"][:, 0]
    rows = np.stack([bxbc[:, 0:CH].reshape(D), a[n + "b_out"]])

    n = "L0_ffn_"
    by_rows = lambda m: m.reshape(-1, P, m.shape[-1]).transpose(1, 0, 2).reshape(P, -1)
    wf = np.zeros((DEPTH, P, F_N), np.float32)
    vecs = np.zeros((DEPTH, P, 9), np.float32)
    for l in range(DEPTH):
        wf[l, :, F_QKV:F_O] = a[n + "wqkv"][l]
        wf[l, :, F_O:F_1] = by_rows(a[n + "wo"][l])
        wf[l, :, F_1:F_2] = a[n + "w1"][l]
        for c in range(3):
            r = min(P, HID - c * P)
            wf[l, 0:r, F_2 + c * P:F_2 + (c + 1) * P] = a[n + "w2"][l, c * P:c * P + r]
            vecs[l, 0:r, c] = a[n + "b1"][l, c * P:c * P + r]
            vecs[l, 0:r, 3 + c] = a[n + "b1"][l, HID + c * P:HID + c * P + r]
        vecs[l, :, 6], vecs[l, :, 7], vecs[l, :, 8] = a[n + "ln_g"][l], a[n + "ln_b"][l], a[n + "b2"][l]
    qk_scales = np.concatenate([a[n + "q_scale"], a[n + "k_scale"]], 1)

    arrays = {"x": a["L0_attn_inp"], "wm": wm, "rows": rows, "wf": wf, "vecs": vecs, "qk_scales": qk_scales,
              "consts": constants()}
    nc = bacc.Bacc("TRN2", target_bir_lowering=False, num_devices=1)
    args = [nc.dram_tensor(k, v.shape, mybir.dt.from_np(v.dtype), kind="ExternalInput").ap() for k, v in arrays.items()]
    out = nc.dram_tensor("out", (NB, T, D), F32, kind="ExternalOutput").ap()
    program(nc, *args, out)
    r = run_bass_kernel_spmd(nc, [arrays], core_ids=[0])
    return r.results[0]["out"]
```

```python
from contextlib import ExitStack

import concourse.bass as bass
from concourse import mybir

F32 = mybir.dt.float32
BF16 = mybir.dt.bfloat16
F32R = mybir.dt.float32r
ALU = mybir.AluOpType
ACT = mybir.ActivationFunctionType
AX = mybir.AxisListType

NB, T, D = 8, 512, 128
P = 128
NT = T // P
MH, CH, NS = 16, D // 16, 64
PAIRS = MH // 2
HQ = 4
XW = 160
PARTS = 80
EPS = 1e-5
HEADS, DH, WIN, DEPTH = 8, 64, 64, 2
HID = D * 4 * 2 // 3
F_QKV, F_O, F_1 = 0, 1536, 2048
F_2 = F_1 + 2 * HID
F_N = F_2 + 3 * P

FADE_N = (NT - 2) * D
OUT_AT, TURN_AT, TURN1_AT, LOG_A_AT = 2, 7, 8, 9
GATE_AT = 8

C_ID, C_CAUSAL, C_MASK, C_MASK0, C_CENTRE, C_NAT, C_OWN, C_HEADS = 0, 128, 256, 384, 512, 640, 768, 1024
C_SCAN = C_HEADS + 2 * MH
C_TAB = C_SCAN + T
C_SEL = C_TAB + 4 * NT * 64
C_N = C_SEL + MH * P
W_B, W_C, W_G, W_LA = 0, 1024, 2048, 2176
W_SPLIT = W_LA + MH
W_X, W_O, W_BB, W_BC, W_BG, W_BLA = (W_SPLIT + n for n in (0, 128, 256, 264, 272, 273))
W_N = W_BLA + 1


def mixer_phase(nc, x, wm, rows, consts, X1, XT, cst, loads, loaded):
    with ExitStack() as ctx:
        def sb(name, shape, dt=F32):
            return ctx.enter_context(nc.sbuf_tensor(name, shape, dt))

        def sem(name):
            return ctx.enter_context(nc.semaphore(name))

        w_rest = sb("m_w_rest", [P, W_N - W_SPLIT])
        w_parts = [sb(f"m_w_part{i}", [P, W_SPLIT], F32R) for i in range(2)]
        bias_x = sb("m_bias_x", [P, D])
        bias_o = sb("m_bias_o", [P, D])
        ident_b = sb("m_ident_b", [P, P], BF16)
        causal_b = sb("m_causal_b", [P, NT, P], BF16)
        nat_b = sb("m_nat_b", [P, P], BF16)
        sel_b = sb("m_sel_b", [P, MH, P], BF16)
        nsel_b = sb("m_nsel_b", [P, MH, P], BF16)
        heads_b = sb("m_heads_b", [P, 2 * MH], BF16)
        half_neg = sb("m_half_neg", [P, NT])

        sums = [sb(f"m_sums{n}", [P, NT]) for n in range(2)]
        mean = [sb(f"m_mean{n}", [P, NT]) for n in range(2)]
        centred = [sb(f"m_centred{n}", [P, NT, D]) for n in range(2)]
        csq = [sb(f"m_csq{n}", [P, NT, D]) for n in range(2)]
        square_sums = [sb(f"m_square_sums{n}", [P, NT]) for n in range(2)]
        var_eps = [sb(f"m_var_eps{n}", [P, NT]) for n in range(2)]
        rstd = [sb(f"m_rstd{n}", [P, NT]) for n in range(2)]
        xn = [sb(f"m_xn{n}", [P, NT, D]) for n in range(2)]

        xnT = sb("m_xnT", [P, T])
        xnT_parts = [sb(f"m_xnT_part{i}", [P, T], F32R) for i in range(2)]
        log_a = sb("m_log_a", [MH, T])
        cum = sb("m_cum", [MH, T])
        rest1 = sb("m_rest1", [MH, T])
        rest2 = sb("m_rest2", [MH, T])
        part2 = sb("m_part2", [MH, T], BF16)
        cum_parts = sb("m_cum_parts", [P, T], BF16)
        x_biased = sb("m_x_biased", [P, T])
        x_spread = sb("m_x_spread", [P, NT * HQ, XW])
        x_fade = sb("m_x_fade", [P, NT - 1, D])
        BT = sb("m_BT", [P, PAIRS, T])
        sel_f = BT[:, :, :].rearrange("p a t -> p (a t)")[:, 0:MH * P]
        CT = sb("m_CT", [P, PAIRS, T])
        w_whole = CT[:, :, :].rearrange("p a t -> p (a t)")[:, 0:W_SPLIT]
        decay = sb("m_decay", [P, 4, T])
        AG = sb("m_AG", [P, 4, T])
        B_tok = sb("m_B_tok", [P, NT - 1, PAIRS * P])
        from_start = sb("m_from_start", [P, T])
        fades = sb("m_fades", [P, FADE_N + (NT - 1) * MH])
        delta = sb("m_delta", [P, NT - 1, PAIRS, 32])
        state = sb("m_state", [P, NT - 1, PAIRS, 32])
        gate = sb("m_gate", [P, T])
        y_gated = sb("m_y_gated", [P, T])
        y_inter = sb("m_y_inter", [P, T - P])
        x_plus = sb("m_x_plus", [P, T])

        psP = [ctx.enter_context(nc.psum_tensor(f"m_ring{i}", [P, 512], F32)) for i in range(2)]
        psD = [ctx.enter_context(nc.psum_tensor(f"m_diff{i}", [P, 512], F32)) for i in range(2)]
        psG = [ctx.enter_context(nc.psum_tensor(f"m_G{i}", [P, 512], F32)) for i in range(2)]
        psY = ctx.enter_context(nc.psum_tensor("m_Y", [P, 512], F32))
        psI = ctx.enter_context(nc.psum_tensor("m_I", [P, 512], F32))

        ident = cst[:, C_ID:C_ID + P]
        own = cst[:, C_OWN:C_OWN + 256].rearrange("p (a b) -> p a b", b=32)

        ring_banks = psP + psG
        projections = ["X"] + [k + str(p) for p in range(PAIRS) for k in "BC"]
        projections.insert(1 + 2 * GATE_AT, "gate")
        later = ["start", "fade"] + [f"Bt{i}" for i in range(6)] + ["dS0", "dS1", "dS2"]
        held = [projections[b::4] for b in range(4)]
        for b in range(2):
            held[b] = held[b] + later[b::2]
            held[2 + b] = held[2 + b] + [f"G{b}"]
        place = {name: (b, u) for b in range(4) for u, name in enumerate(held[b])}
        uses = [len(held[0]), len(held[1]), len(held[2]) - 1, len(held[3]) - 1]
        ring_full = [sem(f"m_ring_full{b}") for b in range(4)]

        def counted(name, n):
            return name, sem("m_" + name), n

        s_x, s_const, s_w, s_sel, s_bias = (sem("m_s_" + n) for n in ("x", "const", "w", "sel", "bias"))
        zeroed, converted, split_done = sem("m_zeroed"), sem("m_converted"), sem("m_split_done")
        norm_names = ("mean", "centred", "csq", "ve", "rstd", "xn")
        norm_done = [{k: counted(f"{k}{n}_done", 2 if k in ("mean", "ve") else 1) for k in norm_names} for n in range(2)]
        xT_full, xnT_done, xnT_rest_done = counted("xT_full", 1), counted("xnT_done", 2), counted("xnT_rest_done", 1)
        la_full, la_done, cum_done = counted("la_full", 1), counted("la_done", 1), counted("cum_done", 1)
        part_done = counted("part_done", 4)
        rest_done = counted("rest_done", 2)
        xb_done, xs_done = counted("xb_done", 1), counted("xs_done", 1)
        bc_done, gate_done = counted("bc_done", 2 * PAIRS), counted("gate_done", 1)
        start_done, fade_done = counted("start_done", 1), counted("fade_done", 1)
        diff_full, decay_done = counted("diff_full", MH), counted("decay_done", MH)
        g_full, ag_done, y_full = counted("g_full", MH), counted("ag_done", MH), counted("y_full", MH)
        bt_done, xf_done, delta_done = counted("bt_done", 6), counted("xf_done", 1), counted("delta_done", 3)
        state_done, i_full, mix_done = counted("state_done", 4), counted("i_full", 1), counted("mix_done", 4)
        plus_done, o_full, x1_done = counted("plus_done", 1), counted("o_full", 1), counted("x1_done", 1)
        x1T_full, xT2_done = counted("x1T_full", 1), counted("xT2_done", 1)

        def has(eng, c, s, k=None):
            _, semaphore, n = c
            assert k is None or k > -n
            eng.wait_ge(semaphore, (s + 1) * n + (n if k is None else k))

        read_by = {"X": (xb_done, 1), "gate": (gate_done, 1), "start": (start_done, 1), "fade": (fade_done, 1)}
        read_by |= {k + str(p): (bc_done, 2 * p + i + 1) for p in range(PAIRS) for i, k in enumerate("BC")}
        read_by |= {"G0": (ag_done, MH - 1), "G1": (ag_done, MH)}
        read_by |= {f"Bt{i}": (bt_done, i + 1) for i in range(6)}
        read_by |= {f"dS{c}": (delta_done, c + 1) for c in range(NT - 1)}

        def ring_wait_free(eng, name, s):
            b, u = place[name]
            before, k = read_by[held[b][u - 1]]
            has(eng, before, s, k if u else k - before[2])
            return ring_banks[b]

        def ring_wait_full(eng, name, s):
            b, u = place[name]
            eng.wait_ge(ring_full[b], (s + 1) * uses[b] + u + 1)
            return ring_banks[b]

        def filled(mm, name):
            mm.then_inc(ring_full[place[name][0]], 1)

        producers = {
            "pe": [xT_full, la_full, diff_full, g_full, y_full, i_full, o_full, x1T_full],
            "act": [norm_done[0]["csq"], xnT_done, la_done, xs_done, bc_done,
                    start_done, fade_done, decay_done, bt_done, xT2_done],
            "dve": [norm_done[n][k] for n in range(2) for k in ("mean", "centred", "ve", "xn")]
                   + [norm_done[1]["csq"], xnT_rest_done, part_done, gate_done, cum_done, rest_done, xb_done, ag_done,
                      xf_done, delta_done, state_done, mix_done, x1_done],
            "pool": [norm_done[0]["rstd"], norm_done[1]["rstd"], plus_done],
        }

        def credit(eng, who):
            for _, semaphore, n in producers[who]:
                eng.sem_inc(semaphore, n)

        def over_sequences(eng, first, body, last):
            first()
            body(0, False, True)
            with eng.Fori(1, NB - 1) as s:
                body(s, True, True)
            body(NB - 1, True, False)
            last()

        block = ctx.enter_context(nc.Block())

        @block.sync
        def _(sp):
            sp.dma_start(X1[:, 0:NT, :], x[0].rearrange("(t p) d -> p t d", p=P)).then_inc(s_x, 16)
            sp.dma_start(cst[:, :], consts[:, 0:C_TAB]).then_inc(s_const, 16)
            sp.dma_start(w_whole, wm[:, 0:W_SPLIT]).then_inc(s_w, 16)
            sp.dma_start(w_rest[:, :], wm[:, W_SPLIT:]).then_inc(s_w, 16)
            sp.dma_start(sel_f, consts[:, C_SEL:C_N]).then_inc(s_sel, 16)
            sp.dma_start(bias_o[:, :], rows[1:2, :].broadcast_to([P, D])).then_inc(s_bias, 16)
            sp.dma_start(bias_x[:, :], rows[0:1, :].broadcast_to([P, D])).then_inc(s_bias, 16)
            for s in range(1, NB):
                sp.wait_ge(s_x, 16 * s)
                sp.dma_start(X1[:, s * NT:(s + 1) * NT, :],
                             x[s].rearrange("(t p) d -> p t d", p=P)).then_inc(s_x, 16)
            for to, source in loads:
                sp.dma_start(to, source).then_inc(loaded, 16)

        @block.tensor
        def _(pe):
            credit(pe, "pe")
            for b in range(4):
                pe.sem_inc(ring_full[b], uses[b])
            pe.wait_ge(s_const, 16)

            def product(out, at, n):
                for i, (wp, xp) in enumerate(((0, 0), (0, 1), (1, 0))):
                    mm = pe.matmul(out, w_parts[wp][:, at:at + n], xnT_parts[xp][:, :], start=(i == 0), stop=(i == 2))
                return mm

            def turn_norm(n, s):
                has(pe, norm_done[n]["xn"], s)
                for t in range(NT):
                    mm = pe.transpose(psI[:, t * P:(t + 1) * P], xn[n][:, t, :], ident)
                mm.then_inc((xT_full, x1T_full)[n][1], 1)

            def turn_first(s):
                has(pe, xT2_done, s - 1, 0)
                has(pe, la_done, s - 1)
                turn_norm(0, s)

            def log_a_of(s):
                has(pe, xnT_rest_done, s)
                pe.wait_ge(s_w, 32)
                pe.wait_ge(split_done, 2)
                product(psI[0:MH, :], W_LA, MH).then_inc(la_full[1], 1)

            def project_out(s):
                has(pe, mix_done, s)
                for t in range(NT):
                    mm = pe.matmul(psI[:, t * P:(t + 1) * P], y_gated[:, t * P:(t + 1) * P],
                                   w_rest[:, W_O - W_SPLIT:W_O - W_SPLIT + D], start=True, stop=True)
                mm.then_inc(o_full[1], 1)

            def turn_second(s):
                has(pe, x1_done, s)
                turn_norm(1, s)

            def intra(h, s):
                g, j = h // HQ, h % HQ
                has(pe, ag_done, s, h + 1)
                if h == 0:
                    has(pe, xs_done, s)
                    has(pe, mix_done, s, 0)
                for c in range(NT):
                    mm = pe.matmul(psY[32 * g:32 * g + 32, c * P:(c + 1) * P],
                                   x_spread[:, c * HQ + g, 32 * j:32 * j + 32], AG[:, h % 4, c * P:(c + 1) * P],
                                   start=(j == 0 and c == 0), stop=(j == HQ - 1), skip_group_check=True)
                mm.then_inc(y_full[1], 1)

            def states(i, s, after):
                if 1 <= i < 7:
                    n = i - 1
                    bank = ring_wait_free(pe, f"Bt{n}", s)
                    for q in range(4):
                        p = (n % 2) * 4 + q
                        mm = pe.transpose(bank[:, q * P:(q + 1) * P], BT[:, p, (n // 2) * P:(n // 2 + 1) * P], ident)
                    filled(mm, f"Bt{n}")
                elif 7 <= i < 10:
                    c = i - 7
                    has(pe, xf_done, s)
                    has(pe, bt_done, s, 2 * c + 2)
                    bank = ring_wait_free(pe, f"dS{c}", s)
                    for p in range(PAIRS):
                        g = p // 2
                        mm = pe.matmul(bank[:, 32 * p:32 * p + 32], B_tok[:, c, p * P:(p + 1) * P],
                                       x_fade[:, c, 32 * g:32 * g + 32], start=True, stop=True)
                    filled(mm, f"dS{c}")
                elif 12 <= i < 15:
                    c = i - 12
                    if c == 0:
                        has(pe, delta_done, s)
                        if after:
                            has(pe, la_done, s + 1)
                        else:
                            has(pe, xT2_done, s, 0)
                    else:
                        has(pe, state_done, s, 2 * c)
                    for p in range(PAIRS):
                        g = p // 2
                        mm = pe.matmul(psI[32 * g:32 * g + 32, c * P:(c + 1) * P], state[:, c, p, :],
                                       CT[:, p, (c + 1) * P:(c + 2) * P], start=(c == 0 and p % 2 == 0),
                                       stop=(p % 2 == 1), skip_group_check=True)
                    if c == NT - 2:
                        mm.then_inc(i_full[1], 1)

            def first():
                turn_first(0)
                log_a_of(0)

            def body(s, before, after):
                has(pe, xnT_done, s)
                has(pe, xnT_rest_done, s)
                bank = ring_wait_free(pe, "X", s)
                for t in range(NT):
                    mm = pe.matmul(bank[:, t * P:(t + 1) * P], xnT[:, t * P:(t + 1) * P],
                                   w_rest[:, W_X - W_SPLIT:W_X - W_SPLIT + D], start=True, stop=True)
                filled(mm, "X")
                if before:
                    intra(MH - 1, s - 1)
                for p in range(PAIRS):
                    for k, off in (("B", W_B), ("C", W_C)):
                        bank = ring_wait_free(pe, f"{k}{p}", s)
                        filled(product(bank[:, :], off + p * P, P), f"{k}{p}")
                    if before and p == OUT_AT:
                        project_out(s - 1)
                    if before and p == TURN_AT:
                        turn_second(s - 1)
                    if p + 1 == GATE_AT:
                        bank = ring_wait_free(pe, "gate", s)
                        filled(product(bank[:, :], W_G, D), "gate")

                if not before:
                    pe.wait_ge(converted, 6)

                def chunk_sums():
                    has(pe, part_done, s)
                    bank = ring_wait_free(pe, "start", s)
                    filled(pe.matmul(bank[:, :], nat_b[0:PARTS, :], cum_parts[0:PARTS, :], start=True, stop=True), "start")
                    bank = ring_wait_free(pe, "fade", s)
                    for c in range(NT - 1):
                        end = cum_parts[0:PARTS, c * P + P - 1:c * P + P].broadcast_to([PARTS, P])
                        if c:
                            pe.matmul(bank[:, (c - 1) * D:c * D], end, nat_b[0:PARTS, :], start=True, stop=True)
                        to = bank[:, FADE_N + c * MH:FADE_N + (c + 1) * MH]
                        pe.matmul(to, end, heads_b[0:PARTS, 0:MH], start=True, stop=False)
                        mm = pe.matmul(to, cum_parts[0:PARTS, c * P:(c + 1) * P], heads_b[0:PARTS, MH:2 * MH], start=False,
                                       stop=True)
                    filled(mm, "fade")

                for h in range(MH):
                    p, r = h // 2, 64 * (h % 2)
                    has(pe, bc_done, s, 2 * p + 2)
                    if h < 2:
                        ring_wait_free(pe, f"G{h}", s)
                    has(pe, ag_done, s, h - 1)
                    for c in range(NT):
                        cols = slice(c * P, (c + 1) * P)
                        mm = pe.matmul(psG[h % 2][:, cols], BT[r:r + NS, p, cols], CT[r:r + NS, p, cols],
                                       start=True, stop=True)
                    mm.then_inc(g_full[1], 1)
                    if h == 0:
                        chunk_sums()
                    has(pe, decay_done, s, h - 1)
                    pe.matmul(psD[h % 2][:, :], sel_b[0:PARTS, h, :], cum_parts[0:PARTS, :], start=True, stop=False,
                              skip_group_check=True)
                    pe.matmul(psD[h % 2][:, :], ident_b[:, :], causal_b[:, :, :].rearrange("p c i -> p (c i)"),
                              start=False, stop=False, skip_group_check=True)
                    for c in range(NT):
                        cols = slice(c * P, (c + 1) * P)
                        mm = pe.matmul(psD[h % 2][:, cols], cum_parts[0:PARTS, cols], nsel_b[0:PARTS, h, :],
                                       start=False, stop=(c == NT - 1), skip_group_check=True)
                    mm.then_inc(diff_full[1], 1)
                    if after and h == TURN1_AT:
                        turn_first(s + 1)
                    if after and h == LOG_A_AT:
                        log_a_of(s + 1)
                    states(h, s, after)
                    if h:
                        intra(h - 1, s)

            def last():
                intra(MH - 1, NB - 1)
                project_out(NB - 1)
                turn_second(NB - 1)

            over_sequences(pe, first, body, last)

        @block.scalar
        def _(act):
            credit(act, "act")
            def squares(s):
                done = norm_done[0]
                has(act, done["centred"], s)
                has(act, done["ve"], s, -1)
                act.activation(csq[0][:, :, :], centred[0][:, :, :], ACT.Square).then_inc(done["csq"][1], 1)

            def xnT_of(s):
                has(act, xT_full, s)
                act.activation(xnT_parts[0][:, :], psI[:, :], ACT.Copy).then_inc(xnT_done[1], 1)
                act.activation(xnT[:, :], psI[:, :], ACT.Copy).then_inc(xnT_done[1], 1)

            def log_a_of(s):
                has(act, la_full, s)
                has(act, cum_done, s, 0)
                act.activation(log_a[:, :], psI[0:MH, :], ACT.Identity,
                               bias=w_rest[0:MH, W_BLA - W_SPLIT:W_BLA - W_SPLIT + 1]).then_inc(la_done[1], 1)

            def second_norm(s):
                has(act, x1T_full, s)
                act.activation(XT[:, bass.ds(s * T, T)], psI[:, :], ACT.Copy).then_inc(xT2_done[1], 1)

            def first():
                squares(0)
                act.wait_ge(s_const, 16)
                act.activation(ident_b[:, :], cst[:, C_ID:C_ID + P], ACT.Copy).then_inc(converted, 1)
                act.activation(nat_b[:, :], cst[:, C_NAT:C_NAT + P], ACT.Copy).then_inc(converted, 1)
                act.activation(causal_b[:, :, :], cst[:, C_CAUSAL:C_CAUSAL + P].unsqueeze(1).broadcast_to([P, NT, P]),
                               ACT.Copy).then_inc(converted, 1)
                act.activation(heads_b[:, :], cst[:, C_HEADS:C_HEADS + 2 * MH], ACT.Copy).then_inc(converted, 1)
                act.wait_ge(s_w, 32)
                act.activation(w_parts[0][:, :], w_whole, ACT.Copy).then_inc(split_done, 1)
                xnT_of(0)
                act.wait_ge(s_sel, 16)
                act.activation(sel_b[:, :, :].rearrange("p h i -> p (h i)"), sel_f, ACT.Copy).then_inc(converted, 1)
                log_a_of(0)
                act.activation(nsel_b[:, :, :].rearrange("p h i -> p (h i)"), sel_f, ACT.Copy,
                               scale=-1.0).then_inc(converted, 1)
                act.wait_ge(converted, 6)
                act.wait_ge(zeroed, 3)

            def body(s, before, after):
                has(act, g_full, s, 0)
                has(act, i_full, s, 0)
                for p in range(PAIRS):
                    for k, off, to in (("B", W_BB - W_SPLIT, BT), ("C", W_BC - W_SPLIT, CT)):
                        bank = ring_wait_full(act, f"{k}{p}", s)
                        act.activation(to[:, p, :], bank[:, :], ACT.Silu,
                                       bias=w_rest[:, off + p:off + p + 1]).then_inc(bc_done[1], 1)
                    if p == 3:
                        has(act, xb_done, s)
                        has(act, y_full, s, 0)
                        has(act, xf_done, s, 0)
                        act.activation(x_spread[:, :, :].rearrange("p a (h x) -> p a h x", x=40)[:, :, :, 0:CH],
                                       x_biased[:, :].rearrange("p (a h x) -> p a h x", h=HQ, x=CH),
                                       ACT.Silu).then_inc(xs_done[1], 1)
                    if p == TURN_AT and before:
                        second_norm(s - 1)
                bank = ring_wait_full(act, "start", s)
                has(act, mix_done, s, 0)
                act.activation(from_start[:, :], bank[:, :], ACT.Exp).then_inc(start_done[1], 1)
                bank = ring_wait_full(act, "fade", s)
                has(act, state_done, s, 0)
                act.activation(fades[:, :], bank[:, 0:FADE_N + (NT - 1) * MH], ACT.Exp).then_inc(fade_done[1], 1)
                for h in range(MH):
                    has(act, diff_full, s, h + 1)
                    has(act, ag_done, s, h - 3)
                    act.activation(decay[:, h % 4, :], psD[h % 2][:, :], ACT.Exp).then_inc(decay_done[1], 1)
                    if 1 <= h < 7:
                        n = h - 1
                        bank = ring_wait_full(act, f"Bt{n}", s)
                        has(act, delta_done, s, 0)
                        act.activation(B_tok[:, n // 2, (n % 2) * 512:(n % 2) * 512 + 512], bank[:, :],
                                       ACT.Copy).then_inc(bt_done[1], 1)
                    if after and h == 4:
                        squares(s + 1)
                    if after and h == TURN1_AT:
                        xnT_of(s + 1)
                    if after and h == LOG_A_AT:
                        log_a_of(s + 1)

            def last():
                second_norm(NB - 1)

            over_sequences(act, first, body, last)

        @block.gpsimd
        def _(pool):
            credit(pool, "pool")
            pool.memset(half_neg[:, :], -0.5).then_inc(zeroed, 1)
            pool.memset(cum_parts[:, :], 0.0).then_inc(zeroed, 1)
            pool.memset(x_spread[:, :, :], 0.0).then_inc(zeroed, 1)
            pool.wait_ge(zeroed, 3)

            def inverse_root(n, s):
                has(pool, norm_done[n]["ve"], s)
                pool.tensor_tensor(rstd[n][:, :], var_eps[n][:, :], half_neg[:, :],
                                   ALU.pow).then_inc(norm_done[n]["rstd"][1], 1)

            def body(s, before, after):
                if before:
                    inverse_root(1, s - 1)
                pool.wait_ge(s_x, (s + 1) * 16)
                pool.wait_ge(s_bias, 32)
                has(pool, x1_done, s, 0)
                pool.tensor_tensor(x_plus[:, :].rearrange("p (t d) -> p t d", d=D), X1[:, bass.ds(s * NT, NT), :],
                                   bias_o[:, :].unsqueeze(1).broadcast_to([P, NT, D]), ALU.add).then_inc(plus_done[1], 1)
                if after:
                    inverse_root(0, s + 1)

            over_sequences(pool, lambda: inverse_root(0, 0), body, lambda: inverse_root(1, NB - 1))

        @block.vector
        def _(dve):
            credit(dve, "dve")
            def norm(n, s, step):
                done = norm_done[n]
                tiles = X1[:, bass.ds(s * NT, NT), :]

                def spread(v):
                    return v.unsqueeze(2).broadcast_to([P, NT, D])
                if step == 0:
                    dve.nop(nofuse=True)
                    dve.tensor_reduce(sums[n][:, :], tiles, AX.X, ALU.add).then_inc(done["mean"][1], 1)
                    has(dve, done["mean"], s, 1)
                    dve.tensor_scalar(mean[n][:, :], sums[n][:, :], 1 / D, None, ALU.mult).then_inc(done["mean"][1], 1)
                elif step == 1:
                    has(dve, done["mean"], s)
                    has(dve, done["csq"], s, 0)
                    has(dve, done["xn"], s, 0)
                    dve.tensor_tensor(centred[n][:, :, :], tiles, spread(mean[n][:, :]),
                                      ALU.subtract).then_inc(done["centred"][1], 1)
                elif step == 2:
                    has(dve, done["csq"], s)
                    dve.tensor_reduce(square_sums[n][:, :], csq[n][:, :, :], AX.X, ALU.add).then_inc(done["ve"][1], 1)
                    has(dve, done["ve"], s, 1)
                    dve.tensor_scalar(var_eps[n][:, :], square_sums[n][:, :], 1 / D, EPS, ALU.mult,
                                      ALU.add).then_inc(done["ve"][1], 1)
                else:
                    has(dve, (xnT_done, xT2_done)[n], s, 0)
                    has(dve, done["rstd"], s)
                    dve.tensor_tensor(xn[n][:, :, :], centred[n][:, :, :], spread(rstd[n][:, :]),
                                      ALU.mult).then_inc(done["xn"][1], 1)

            def rest_of_xnT(s):
                has(dve, xnT_done, s)
                has(dve, gate_done, s - 1)
                dve.tensor_tensor(xnT_parts[1][:, :], psI[:, :], xnT_parts[0][:, :].bitcast(F32),
                                  ALU.subtract).then_inc(xnT_rest_done[1], 1)

            def cumulate(s):
                has(dve, part_done, s, 0)
                has(dve, rest_done, s, 0)
                has(dve, la_done, s)
                dve.tensor_tensor_scan(cum[:, :], cst[0:MH, C_SCAN:C_SCAN + T], log_a[:, :], 0.0, ALU.mult,
                                       ALU.add).then_inc(cum_done[1], 1)

            def combine(s, step):
                if step == 0:
                    has(dve, i_full, s)
                    has(dve, start_done, s)
                    dve.tensor_tensor(y_inter[:, :], psI[:, 0:T - P], from_start[:, P:], ALU.mult).then_inc(mix_done[1], 1)
                    has(dve, gate_done, s)
                    has(dve, mix_done, s, 1)
                    dve.tensor_tensor(y_inter[:, :], y_inter[:, :], gate[:, P:], ALU.mult).then_inc(mix_done[1], 1)
                else:
                    has(dve, y_full, s)
                    dve.tensor_tensor(y_gated[:, :], psY[:, :], gate[:, :], ALU.mult).then_inc(mix_done[1], 1)
                    has(dve, mix_done, s, 3)
                    dve.tensor_tensor(y_gated[:, P:], y_gated[:, P:], y_inter[:, :], ALU.add).then_inc(mix_done[1], 1)

            def add_output(s):
                has(dve, plus_done, s)
                has(dve, o_full, s)
                dve.tensor_tensor(X1[:, bass.ds(s * NT, NT), :], psI[:, :].rearrange("p (t d) -> p t d", d=D),
                                  x_plus[:, :].rearrange("p (t d) -> p t d", d=D), ALU.add).then_inc(x1_done[1], 1)
                has(dve, x1_done, s)
                for step in range(4):
                    norm(1, s, step)
                    if step == 1:
                        has(dve, norm_done[1]["centred"], s)
                        dve.tensor_tensor(csq[1][:, :, :], centred[1][:, :, :], centred[1][:, :, :],
                                          ALU.mult).then_inc(norm_done[1]["csq"][1], 1)

            def states(i, s):
                if i == 0:
                    has(dve, fade_done, s)
                    has(dve, xs_done, s)
                    spread = x_spread[:, 0:(NT - 1) * HQ, :].rearrange("p a (h x) -> p (a h) x", x=40)
                    dve.tensor_tensor(x_fade[:, :, :].rearrange("p c (h x) -> p (c h) x", x=CH), spread[:, :, 0:CH],
                                      fades[:, FADE_N:].unsqueeze(2).broadcast_to([P, (NT - 1) * MH, CH]),
                                      ALU.mult).then_inc(xf_done[1], 1)
                elif 8 <= i < 11:
                    c = i - 8
                    bank = ring_wait_full(dve, f"dS{c}", s)
                    to = state[:, 0, :, :] if c == 0 else delta[:, c, :, :]
                    dve.tensor_tensor(to, bank[:, 0:PAIRS * 32].rearrange("p (a b) -> p a b", b=32), own,
                                      ALU.mult).then_inc(delta_done[1], 1)
                elif i in (11, 12):
                    c = i - 10
                    if c == 1:
                        has(dve, delta_done, s)
                    else:
                        has(dve, state_done, s, 2)
                    halves = lambda ap: ap.rearrange("p (g r) x -> p g r x", r=2)
                    dve.tensor_tensor(halves(state[:, c, :, :]), halves(state[:, c - 1, :, :]),
                                      fades[:, (c - 1) * D:c * D].rearrange("p (g x) -> p g x", x=32).unsqueeze(2)
                                      .broadcast_to([P, HQ, 2, 32]), ALU.mult).then_inc(state_done[1], 1)
                    has(dve, state_done, s, 2 * c - 1)
                    dve.tensor_tensor(state[:, c, :, :], state[:, c, :, :], delta[:, c, :, :],
                                      ALU.add).then_inc(state_done[1], 1)

            def first():
                dve.wait_ge(s_x, 16)
                for step in range(4):
                    norm(0, 0, step)
                dve.wait_ge(split_done, 1)
                dve.tensor_tensor(w_parts[1][:, :], w_whole, w_parts[0][:, :].bitcast(F32),
                                  ALU.subtract).then_inc(split_done, 1)
                rest_of_xnT(0)
                dve.wait_ge(s_const, 16)
                cumulate(0)
                dve.wait_ge(zeroed, 3)
                dve.wait_ge(s_bias, 32)

            def body(s, before, after):
                bank = ring_wait_full(dve, "X", s)
                has(dve, xs_done, s, 0)
                dve.tensor_tensor(x_biased[:, :].rearrange("p (t d) -> p t d", d=D),
                                  bank[:, :].rearrange("p (t d) -> p t d", d=D),
                                  bias_x[:, :].unsqueeze(1).broadcast_to([P, NT, D]), ALU.add).then_inc(xb_done[1], 1)
                has(dve, fade_done, s, 0)
                has(dve, diff_full, s, 0)
                has(dve, rest_done, s, 0)
                has(dve, cum_done, s)
                dve.tensor_copy(cum_parts[0:MH, :], cum[:, :]).then_inc(part_done[1], 1)
                if before:
                    combine(s - 1, 0)
                has(dve, part_done, s, 1)
                dve.tensor_tensor(rest1[:, :], cum[:, :], cum_parts[0:MH, :], ALU.subtract).then_inc(rest_done[1], 1)
                if before:
                    combine(s - 1, 1)
                has(dve, rest_done, s, 1)
                dve.tensor_copy(part2[:, :], rest1[:, :]).then_inc(part_done[1], 1)
                dve.tensor_copy(cum_parts[32:32 + MH, :], rest1[:, :]).then_inc(part_done[1], 1)
                has(dve, part_done, s, 2)
                dve.tensor_tensor(rest2[:, :], rest1[:, :], part2[:, :], ALU.subtract).then_inc(rest_done[1], 1)
                has(dve, rest_done, s, 2)
                dve.tensor_copy(cum_parts[64:64 + MH, :], rest2[:, :]).then_inc(part_done[1], 1)
                if before:
                    add_output(s - 1)
                bank = ring_wait_full(dve, "gate", s)
                has(dve, mix_done, s, 0)
                dve.tensor_scalar(gate[:, :], bank[:, :], w_rest[:, W_BG - W_SPLIT:W_BG - W_SPLIT + 1], None,
                                  ALU.add).then_inc(gate_done[1], 1)
                for h in range(MH):
                    has(dve, g_full, s, h + 1)
                    has(dve, decay_done, s, h + 1)
                    has(dve, y_full, s, h - 3)
                    dve.tensor_tensor(AG[:, h % 4, :], psG[h % 2][:, :], decay[:, h % 4, :],
                                      ALU.mult).then_inc(ag_done[1], 1)
                    states(h, s)
                    if after:
                        if h == 1:
                            dve.wait_ge(s_x, (s + 2) * 16)
                        if h in (1, 2, 4, 6):
                            norm(0, s + 1, (1, 2, 4, 6).index(h))
                        if h == TURN1_AT:
                            rest_of_xnT(s + 1)
                        if h == LOG_A_AT + 1:
                            cumulate(s + 1)

            def last():
                combine(NB - 1, 0)
                combine(NB - 1, 1)
                add_output(NB - 1)

            over_sequences(dve, first, body, last)


def layers_phase(nc, wf, consts, X1, XT, given, out):
    with ExitStack() as ctx:
        def sb(name, shape, dt=F32):
            return ctx.enter_context(nc.sbuf_tensor(name, shape, dt))

        def ps(name):
            return ctx.enter_context(nc.psum_tensor(name, [P, 512], F32))

        def sem(name):
            return ctx.enter_context(nc.semaphore(name))

        cst, w0, vec, scales, loaded, loads = given
        w = [w0] + [sb(f"f_w{l}", [P, F_N]) for l in range(1, DEPTH)]
        tab = sb("f_tab", [P, 4, NT, DH])
        cos_t = sb("f_cos_t", [P, DEPTH, NT, 2, DH])
        sin_t = sb("f_sin_t", [P, DEPTH, NT, 2, DH])
        w1s = sb("f_w1s", [P, 2 * HID])
        wqkv_parts = [sb(f"f_wqkv_part{i}", [P, DEPTH, F_O], F32R) for i in range(2)]
        w1s_parts = [sb(f"f_w1s_part{i}", [P, DEPTH, 2 * HID], F32R) for i in range(2)]
        hT_parts = [sb(f"f_hT_part{i}", [P, T], F32R) for i in range(2)]
        h2n_parts = [sb(f"f_h2n_part{i}", [P, T], F32R) for i in range(2)]
        b1s = sb("f_b1s", [P, DEPTH, 6])
        half_neg = sb("f_half_neg", [P, 2 * HEADS])

        sq = sb("f_sq", [P, 2, 512])
        qk = sb("f_qk", [P, 2, 512])
        ssq = sb("f_ssq", [P, 2 * HEADS])
        ssq_c = sb("f_ssq_c", [P, 2 * HEADS])
        rnorm = sb("f_rnorm", [P, 2 * HEADS])
        by_cos = sb("f_by_cos", [P, 2 * 512])
        by_sin = sb("f_by_sin", [P, 2 * 512])
        qk_n = sb("f_qk_n", [P, 2 * 512])
        qT = sb("f_qT", [P, 4, P])
        kT = sb("f_kT", [P, 4, WIN + T])
        V_here = sb("f_V_here", [P, NT, HEADS, DH + 1])
        V_prev = sb("f_V_prev", [P, NT, HEADS, DH + 1])
        less = sb("f_less", [P, 8, P])
        ident_b = sb("f_ident_b", [P, P], BF16)
        masks_b = sb("f_masks_b", [P, 2, P], BF16)
        top = sb("f_top", [P, 8])
        probs = sb("f_probs", [P, 8, P])
        PT = sb("f_PT", [P, 8, P])
        rden = sb("f_rden", [P, 8])
        o_tok = sb("f_o_tok", [P, 512])
        oT = sb("f_oT", [P, 4, T])
        h2T = sb("f_h2T", [P, T])
        h2c = sb("f_h2c", [P, T])
        h2sq = sb("f_h2sq", [P, T])
        var_eps = sb("f_var_eps", [P, NT])
        rstd = sb("f_rstd", [P, NT])
        one_dth = sb("f_one_dth", [P, 1])
        h2n = sb("f_h2n", [P, T])
        y_last = sb("f_y_last", [P, T])
        hid = sb("f_hid", [P, 3, T])

        ps0, ps1, ps2, psF, psE, psO, psU, psW = (ps(f"f_bank{i}") for i in range(8))
        psS, psV = (psE, psO), (psU, psW)

        ident, centring = cst[:, C_ID:C_ID + P], cst[:, C_CENTRE:C_CENTRE + P]

        def counted(name, n):
            return sem("f_" + name), n

        s_setup, converted = sem("f_s_setup"), sem("f_converted")
        tab_loaded, w_loaded = sem("f_tab_loaded"), sem("f_w_loaded")
        wqkv_done, w1s_done = sem("f_wqkv_done"), sem("f_w1s_done")
        b1_full, b1_done, tab_done = sem("f_b1_full"), sem("f_b1_done"), sem("f_tab_done")
        hT_done, hT_rest_done = counted("hT_done", 1), counted("hT_rest_done", 1)
        q_full, k_full, v_full = counted("q_full", 4), counted("k_full", 4), counted("v_full", 4)
        shift_done = [counted(f"shift_done{u}", 32 if u < NT - 1 else 16) for u in range(NT)]
        sq_done, qk_done, v_done = counted("sq_done", 8), counted("qk_done", 8), counted("v_done", 4)
        ssq_done, cos_done, sin_done = counted("ssq_done", 12), counted("cos_done", 8), counted("sin_done", 8)
        rnorm_done, rot_done, unit_done = counted("rnorm_done", 4), counted("rot_done", 8), counted("unit_done", 4)
        tq_full, tk_full = counted("tq_full", 4), counted("tk_full", 4)
        tq_done, tk_done = counted("tq_done", 4), counted("tk_done", 4)
        sim_full = counted("sim_full", 8)
        top_done, less_done = counted("top_done", 8), counted("less_done", 8)
        probs_done = counted("probs_done", 8)
        pt_full, pt_done = counted("pt_full", 8), counted("pt_done", 8)
        pv_full, rden_done, o_done = counted("pv_full", 8), counted("rden_done", 8), counted("o_done", 8)
        ot_full, ot_done = counted("ot_full", 4), counted("ot_done", 4)
        f_full = counted("f_full", 12)
        x2_done, h2_done, h2c_done, h2sq_done = (counted(n, 1) for n in ("x2_done", "h2_done", "h2c_done", "h2sq_done"))
        ve_done, rstd_done, h2n_done, h2n_first_done, h2n_rest_done = (
            counted(n, 1) for n in ("ve_done", "rstd_done", "h2n_done", "h2n_first_done", "h2n_rest_done"))
        gelu_done, hid_done = counted("gelu_done", 3), counted("hid_done", 3)
        y_done, out_done, s_out = counted("y_done", 1), counted("out_done", 1), sem("f_s_out")
        f_order = {"wo": (x2_done, 1), "centre": (h2sq_done, 1), "var": (ve_done, 1), "rstd": (h2n_done, 1),
                   "g0": (gelu_done, 1), "g1": (gelu_done, 2), "g2": (gelu_done, 3),
                   "a0": (hid_done, 1), "a1": (hid_done, 2), "a2": (hid_done, 3), "y": (y_done, 1),
                   "out": (out_done, 1)}
        names = list(f_order)

        producers = {
            "pe": [q_full, k_full, v_full, tq_full, tk_full, sim_full, pt_full, pv_full, ot_full, f_full],
            "act": [hT_done, h2n_first_done, sq_done, qk_done, v_done, tq_done, tk_done, probs_done, pt_done, ot_done,
                    h2_done, h2c_done, h2sq_done, gelu_done],
            "dve": [hT_rest_done, h2n_rest_done, ssq_done, cos_done, sin_done, top_done, less_done, rden_done,
                    o_done, x2_done, ve_done, h2n_done, hid_done, y_done, out_done],
            "pool": [rnorm_done, rot_done, unit_done, rstd_done],
            "sp": shift_done,
        }

        def credit(eng, who):
            for semaphore, n in producers[who]:
                eng.sem_inc(semaphore, n)

        def has(eng, c, G, k=None):
            l, s = G
            assert k is None or k > -c[1]
            eng.wait_ge(c[0], (l * NB + s + 1) * c[1] + (c[1] if k is None else k))

        def f_bank(eng, name, G):
            i = names.index(name)
            before, k = f_order[names[i - 1]]
            has(eng, before, G, k if i else k - before[1])
            return psF

        def f_wait(eng, name, G):
            has(eng, f_full, G, names.index(name) + 1)
            return psF

        def place(l, n):
            return divmod(l * NB + n, NB) if 0 <= l * NB + n < DEPTH * NB else None

        def tile_back(l, s, t, back):
            ds, at = divmod(t - back, NT)
            G = place(l, s + ds) if isinstance(s, int) else (l, s + ds)
            return G and (G, at)

        def seq_back(l, s, back):
            return place(l, s - back) if isinstance(s, int) else (l, s - back)

        slots = {(2, 3): ("wo", 1), (3, 1): ("centre", 1), (3, 2): ("var", 1), (3, 3): ("rstd", 1),
                 (0, 2): ("g0", 2), (0, 3): ("g1", 2), (0, 4): ("g2", 2),
                 (1, 1): ("a0", 2), (1, 2): ("a1", 2), (1, 3): ("a2", 2), (2, 1): ("y", 2), (2, 2): ("out", 2)}

        def f_slot(l, s, t, n, do):
            if (t, n) in slots:
                name, back = slots[t, n]
                G = seq_back(l, s, back)
                if G:
                    do(name, G)

        def over_layers(eng, body, after=lambda l, s: None):
            for l in range(DEPTH):
                for s in (0, 1):
                    body(l, s)
                    after(l, s)
                with eng.Fori(2, NB - 1) as s:
                    body(l, s)
                body(l, NB - 1)
            for s in (NB, NB + 1):
                body(DEPTH - 1, s)

        def rows_of(c):
            return min(P, HID - c * P)

        block = ctx.enter_context(nc.Block())

        @block.sync
        def _(sp):
            sp.dma_start(tab[:, :, :, :].rearrange("p a t d -> p (a t d)"), consts[:, C_TAB:C_SEL]).then_inc(tab_loaded, 16)
            for l in range(1, DEPTH):
                sp.dma_start(w[l][:, :], wf[l]).then_inc(w_loaded, 16)
            credit(sp, "sp")

            def body(l, s):
                for t in range(NT):
                    now = tile_back(l, s, t, 0)
                    if now:
                        G, u = now
                        has(sp, v_done, G, u + 1)
                        has(sp, pv_full, G, 2 * u - 6)
                        sp.dma_start(V_prev[WIN:P, u, :, :], V_here[0:WIN, u, :, :]).then_inc(shift_done[u][0], 16)
                        if u < NT - 1:
                            has(sp, pv_full, G, 2 * u - 4)
                            sp.dma_start(V_prev[0:WIN, u + 1, :, :], V_here[WIN:P, u, :, :]).then_inc(shift_done[u][0], 16)
                G = seq_back(l, s, 2)
                if G and G[0] == DEPTH - 1:
                    has(sp, out_done, G)
                    sp.dma_start(out[bass.ds(G[1], 1)].rearrange("a (t p) d -> p (a t) d", p=P),
                                 X1[:, bass.ds(G[1] * NT, NT), :]).then_inc(s_out, 16)

            over_layers(sp, body)
            sp.wait_ge(s_out, 16 * NB)

        @block.tensor
        def _(pe):
            credit(pe, "pe")
            pe.wait_ge(loaded, loads)
            pe.wait_ge(s_setup, 9)
            def first_bias(l):
                for c in range(6):
                    r, at = rows_of(c % 3), F_1 + (c // 3) * HID + (c % 3) * P
                    mm = pe.matmul(psF[0:r, c:c + 1], w[l][:, at:at + r], vec[:, l, 7:8], start=True, stop=True)
                mm.then_inc(b1_full, 1)

            first_bias(0)
            pe.wait_ge(converted, 3)

            def after(l, s):
                if s == 1 and l + 1 < DEPTH:
                    pe.wait_ge(w_loaded, 16 * (DEPTH - 1))
                    has(pe, h2n_done, (l, 0))
                    first_bias(l + 1)

            def product(out, stationary, moving):
                for i, (a, b) in enumerate(((0, 0), (0, 1), (1, 0))):
                    mm = pe.matmul(out, stationary(a), moving(b), start=(i == 0), stop=(i == 2))
                return mm

            def half(name, G):
                bank = f_bank(pe, name, G)
                if name == "wo":
                    has(pe, ot_done, G)
                    pe.wait_ge(b1_done, 2 * (G[0] + 1))
                    for p in range(4):
                        mm = pe.matmul(bank[:, :], w[G[0]][:, F_O + p * P:F_O + (p + 1) * P], oT[:, p, :], start=(p == 0),
                                       stop=(p == 3))
                elif name == "centre":
                    has(pe, h2_done, G)
                    mm = pe.matmul(bank[:, :], centring, h2T[:, :], start=True, stop=True)
                elif name == "var":
                    has(pe, h2sq_done, G)
                    for t in range(NT):
                        mm = pe.matmul(bank[:, t:t + 1], h2sq[:, t * P:(t + 1) * P], one_dth[:, :], start=True, stop=True)
                elif name == "rstd":
                    has(pe, rstd_done, G)
                    for t in range(NT):
                        mm = pe.matmul(bank[:, t * P:(t + 1) * P], rstd[:, t:t + 1].broadcast_to([P, P]), ident,
                                       start=True, stop=True)
                elif name == "out":
                    if G[0] < DEPTH - 1:
                        pe.sem_inc(f_full[0], 1)
                        return
                    for t in range(NT):
                        mm = pe.transpose(bank[:, t * P:(t + 1) * P], y_last[:, t * P:(t + 1) * P], ident)
                elif name == "y":
                    has(pe, hid_done, G)
                    for c in range(3):
                        r = rows_of(c)
                        mm = pe.matmul(bank[:, :], w[G[0]][0:r, F_2 + c * P:F_2 + (c + 1) * P], hid[0:r, c, :],
                                       start=(c == 0), stop=(c == 2))
                else:
                    has(pe, h2n_rest_done, G)
                    if name == "g0":
                        pe.wait_ge(w1s_done, 3 * (G[0] + 1))
                        pe.wait_ge(b1_done, 2 * min(DEPTH, G[0] + 2))
                    c = int(name[1])
                    r, at = rows_of(c), (HID if name[0] == "g" else 0) + c * P
                    mm = product(bank[0:r, :], lambda a: w1s_parts[a][:, G[0], at:at + r], lambda b: h2n_parts[b][:, :])
                mm.then_inc(f_full[0], 1)

            def body(l, s):
                for t in range(NT):
                    now, b1, b2, b3 = (tile_back(l, s, t, k) for k in range(4))
                    if now:
                        G, u = now
                        has(pe, hT_rest_done, G)
                        if u == 0:
                            pe.wait_ge(wqkv_done, 2 * (G[0] + 1))

                        def project(out, at):
                            return product(out, lambda a: hT_parts[a][:, u * P:(u + 1) * P],
                                           lambda b: wqkv_parts[b][:, G[0], at:at + 512])
                        if not b2:
                            has(pe, sq_done, G, 2 * u - 1)
                            has(pe, v_done, G, u)
                        has(pe, tq_done, G, u - 1)
                        project(ps0[:, :], 512).then_inc(k_full[0], 1)
                        has(pe, tk_done, G, u - 1)
                        project(ps1[:, :], 1024).then_inc(v_full[0], 1)
                        has(pe, ot_done, G, u - 3)
                        has(pe, sq_done, G, 2 * u)
                        project(ps2[:, :], 0).then_inc(q_full[0], 1)
                    f_slot(l, s, t, 1, half)
                    if b1:
                        G, u = b1
                        has(pe, unit_done, G, u + 1)
                        if now:
                            has(pe, sq_done, G, 2 * (u + 1) + 1)
                        else:
                            has(pe, tk_done, G, u)
                        for p in range(4):
                            mm = pe.transpose(ps0[:, p * P:(p + 1) * P], qk_n[:, p * P:(p + 1) * P], ident)
                        mm.then_inc(tq_full[0], 1)
                        if now:
                            has(pe, v_done, G, u + 2)
                        for p in range(4):
                            mm = pe.transpose(ps1[:, p * P:(p + 1) * P], qk_n[:, 512 + p * P:512 + (p + 1) * P], ident)
                        mm.then_inc(tk_full[0], 1)
                    if b2:
                        G, u = b2
                        for e in range(2):
                            has(pe, probs_done, G, 2 * u + e + 1)
                            for p in range(4):
                                mm = pe.transpose(psS[e][:, p * P:(p + 1) * P], probs[:, e * 4 + p, :], ident)
                            mm.then_inc(pt_full[0], 1)
                    f_slot(l, s, t, 2, half)
                    if b3:
                        G, u = b3
                        has(pe, o_done, G, 2 * u + 2)
                        if now:
                            has(pe, sq_done, G, 2 * (u + 3) + 2)
                        else:
                            has(pe, ot_done, G, u)
                        for p in range(4):
                            mm = pe.transpose(ps2[:, p * P:(p + 1) * P], o_tok[:, p * P:(p + 1) * P], ident)
                        mm.then_inc(ot_full[0], 1)
                    if b2:
                        G, u = b2
                        has(pe, shift_done[u], G)
                        for e in range(2):
                            has(pe, pt_done, G, 2 * u + e + 1)
                            has(pe, o_done, G, 2 * u + e - 1)
                            for p in range(4):
                                for win, V in enumerate((V_prev, V_here)):
                                    r = slice(win * WIN, (win + 1) * WIN)
                                    mm = pe.matmul(psV[e][r, p * (DH + 1):(p + 1) * (DH + 1)], PT[:, e * 4 + p, r],
                                                   V[:, u, 2 * p + e, :], start=True, stop=True)
                            mm.then_inc(pv_full[0], 1)
                    f_slot(l, s, t, 3, half)
                    if b1:
                        G, u = b1
                        has(pe, tq_done, G, u + 1)
                        has(pe, tk_done, G, u + 1)

                        def of_pair(e, p):
                            r = slice(e * DH, (e + 1) * DH)
                            if p == 0:
                                has(pe, pt_done, G, 2 * u + e - 1)
                                pe.matmul(psS[e][:, :], ident_b[:, :],
                                          masks_b[:, min(u, 1), :].unsqueeze(1).broadcast_to([P, 4, P]), start=True,
                                          stop=False, skip_group_check=True)
                            for win in range(2):
                                at = u * P + win * WIN
                                mm = pe.matmul(psS[e][win * WIN:(win + 1) * WIN, p * P:(p + 1) * P],
                                               qT[r, p, win * WIN:(win + 1) * WIN], kT[r, p, at:at + P],
                                               start=False, stop=(p == 3), skip_group_check=True)
                            if p == 3:
                                mm.then_inc(sim_full[0], 1)

                        for i in range(6):
                            if i < 4:
                                of_pair(0, i)
                            if i >= 2:
                                of_pair(1, i - 2)
                    f_slot(l, s, t, 4, half)

            over_layers(pe, body, after)

        @block.scalar
        def _(act):
            credit(act, "act")
            act.wait_ge(s_setup, 9)

            def shifted(dst, G, done):
                act.activation(dst[0:64, :], XT[0:64, bass.ds(G[1] * T, T)], ACT.Copy)
                act.activation(dst[64:P, 1:T], XT[64:P, bass.ds(G[1] * T, T - 1)],
                               ACT.Copy).then_inc(done[0], 1)

            def tokens_of(G):
                if G[0]:
                    has(act, y_done, (G[0] - 1, G[1]))
                shifted(hT_parts[0], G, hT_done)

            def first_part_wqkv(l):
                if l:
                    act.wait_ge(w_loaded, 16 * (DEPTH - 1))
                act.activation(wqkv_parts[0][:, l, :], w[l][:, 0:F_O], ACT.Copy).then_inc(wqkv_done, 1)

            def first_part_w1(l):
                if l:
                    act.wait_ge(w1s_done, 3 * l)
                act.activation(w1s[:, :], w[l][:, F_1:F_1 + 2 * HID], ACT.Copy, scale=vec[:, l, 6:7]).then_inc(w1s_done, 1)
                act.wait_ge(w1s_done, l * 3 + 1)
                act.activation(w1s_parts[0][:, l, :], w1s[:, :], ACT.Copy).then_inc(w1s_done, 1)

            act.activation(ident_b[:, :], ident, ACT.Copy).then_inc(converted, 1)
            for i, at in enumerate((C_MASK0, C_MASK)):
                act.activation(masks_b[:, i, :], cst[:, at:at + P], ACT.Copy).then_inc(converted, 1)
            act.wait_ge(loaded, loads)
            tokens_of((0, 0))
            first_part_wqkv(0)

            def after(l, s):
                if (l, s) == (0, 0):
                    first_part_w1(0)
                elif s == 1 and l + 1 < DEPTH:
                    first_part_wqkv(l + 1)
                    first_part_w1(l + 1)

            def half(name, G):
                if name == "wo":
                    has(act, x2_done, G)
                    shifted(h2T, G, h2_done)
                elif name == "centre":
                    bank = f_wait(act, name, G)
                    has(act, h2n_done, G, 0)
                    act.activation(h2c[:, :], bank[:, :], ACT.Copy).then_inc(h2c_done[0], 1)
                    act.activation(h2sq[:, :], bank[:, :], ACT.Square).then_inc(h2sq_done[0], 1)
                elif name == "rstd":
                    has(act, h2n_done, G)
                    has(act, hid_done, G, 0)
                    act.activation(h2n_parts[0][:, :], h2n[:, :], ACT.Copy).then_inc(h2n_first_done[0], 1)
                elif name[0] == "g":
                    bank, c = f_wait(act, name, G), int(name[1])
                    r = rows_of(c)
                    has(act, hid_done, G, 0)
                    act.activation(hid[0:r, c, :], bank[0:r, :], ACT.Gelu,
                                   bias=b1s[0:r, G[0], 3 + c:4 + c]).then_inc(gelu_done[0], 1)

            def body(l, s):
                for t in range(NT):
                    now, b1, b2, b3 = (tile_back(l, s, t, k) for k in range(4))
                    if now:
                        G, u = now

                        def take(half_of, bank, full):
                            has(act, full, G, u + 1)
                            has(act, sin_done, G, 2 * u - half_of)
                            act.activation(qk[:, half_of, :], bank[:, :], ACT.Copy).then_inc(qk_done[0], 1)
                            has(act, ssq_done, G, 3 * u - 1 - half_of)
                            act.activation(sq[:, half_of, :], bank[:, :], ACT.Square).then_inc(sq_done[0], 1)

                        take(1, ps0, k_full)
                        has(act, v_full, G, u + 1)
                        heads = ps1[:, :].rearrange("p (h d) -> p h d", d=DH)
                        has(act, shift_done[u], G, 0)
                        act.activation(V_here[:, u, :, 0:DH], heads, ACT.Copy).then_inc(v_done[0], 1)
                    if b2:
                        for e in range(2):
                            h = slice(e * 4, e * 4 + 4)
                            has(act, less_done, b2[0], 2 * b2[1] + e + 1)
                            has(act, pt_full, b2[0], 2 * b2[1] + e - 1)
                            act.activation(probs[:, h, :], less[:, h, :], ACT.Exp).then_inc(probs_done[0], 1)
                    f_slot(l, s, t, 1, half)
                    if now:
                        take(0, ps2, q_full)
                    if b2:
                        G, u = b2
                        has(act, pv_full, G, 2 * u)
                        for e in range(2):
                            has(act, pt_full, G, 2 * u + e + 1)
                            act.activation(PT[:, e * 4:e * 4 + 4, :], psS[e][:, :].rearrange("p (a b) -> p a b", a=4),
                                           ACT.Copy).then_inc(pt_done[0], 1)
                    f_slot(l, s, t, 2, half)
                    if b1:
                        G, u = b1
                        has(act, sim_full, G, 2 * u)
                        has(act, tq_full, G, u + 1)
                        act.activation(qT[:, :, :], ps0[:, :].rearrange("p (a b) -> p a b", a=4),
                                       ACT.Copy).then_inc(tq_done[0], 1)
                        has(act, tk_full, G, u + 1)
                        act.activation(kT[:, :, WIN + u * P:WIN + (u + 1) * P], ps1[:, :].rearrange("p (a b) -> p a b", a=4),
                                       ACT.Copy).then_inc(tk_done[0], 1)
                    if t == NT - 1 and seq_back(l, s, -1):
                        tokens_of(seq_back(l, s, -1))
                    if b3:
                        G, u = b3
                        has(act, ot_full, G, u + 1)
                        act.activation(oT[:, :, u * P:(u + 1) * P], ps2[:, :].rearrange("p (a b) -> p a b", a=4),
                                       ACT.Copy).then_inc(ot_done[0], 1)
                    f_slot(l, s, t, 3, half)
                    f_slot(l, s, t, 4, half)

            over_layers(act, body, after)

        @block.gpsimd
        def _(pool):
            credit(pool, "pool")
            for n, (part, value) in enumerate((
                    (half_neg[:, :], -0.5), (one_dth[:, :], 1 / D), (hT_parts[0][64:P, 0:1].bitcast(F32), 0.0),
                    (hT_parts[1][64:P, 0:1].bitcast(F32), 0.0), (h2T[64:P, 0:1], 0.0), (kT[:, :, 0:WIN], 0.0),
                    (V_prev[0:WIN, 0, :, 0:DH], 0.0), (V_prev[0:WIN, 0, :, DH:DH + 1], 1.0),
                    (V_here[:, :, :, DH:DH + 1], 1.0))):
                pool.memset(part, value).then_inc(s_setup, 1)
                pool.wait_ge(s_setup, n + 1)

            def half(name, G):
                if name == "var":
                    has(pool, ve_done, G)
                    has(pool, h2n_done, G, 0)
                    pool.tensor_tensor(rstd[:, :], var_eps[:, :], half_neg[:, 0:NT], ALU.pow).then_inc(rstd_done[0], 1)

            def body(l, s):
                for t in range(NT):
                    now = tile_back(l, s, t, 0)
                    if not now:
                        f_slot(l, s, t, 2, half)
                    else:
                        G, u = now
                        for n, i in ((1, 1), (2, 0)):
                            if n == 2:
                                f_slot(l, s, t, 2, half)
                            part = slice(i * 512, (i + 1) * 512)
                            has(pool, sin_done, G, 2 * u + n)
                            has(pool, tk_full, G, u)
                            pool.tensor_tensor(qk_n[:, part], by_cos[:, part], by_sin[:, part],
                                               ALU.add).then_inc(rot_done[0], 1)
                        has(pool, ssq_done, G, 3 * u + 3)
                        has(pool, unit_done, G, u)
                        pool.tensor_tensor(rnorm[:, :], ssq_c[:, :], half_neg[:, :], ALU.pow).then_inc(rnorm_done[0], 1)
                        has(pool, rot_done, G, 2 * u + 2)
                        has(pool, rnorm_done, G, u + 1)
                        heads = qk_n[:, :].rearrange("p (h d) -> p h d", d=DH)
                        pool.tensor_tensor(heads, heads, rnorm[:, :].unsqueeze(2).broadcast_to([P, 2 * HEADS, DH]),
                                           ALU.mult).then_inc(unit_done[0], 1)

            over_layers(pool, body)

        @block.vector
        def _(dve):
            credit(dve, "dve")
            dve.wait_ge(loaded, loads)
            dve.wait_ge(s_setup, 9)

            def rest_of_wqkv(l):
                dve.wait_ge(wqkv_done, 2 * l + 1)
                dve.tensor_tensor(wqkv_parts[1][:, l, :], w[l][:, 0:F_O], wqkv_parts[0][:, l, :].bitcast(F32),
                                  ALU.subtract).then_inc(wqkv_done, 1)

            def rest_of_w1(l):
                dve.wait_ge(w1s_done, 3 * l + 2)
                dve.tensor_tensor(w1s_parts[1][:, l, :], w1s[:, :], w1s_parts[0][:, l, :].bitcast(F32),
                                  ALU.subtract).then_inc(w1s_done, 1)

            def tables(l):
                for i in range(2):
                    scale = scales[:, l, i:i + 1, :].broadcast_to([P, NT, DH])
                    dve.tensor_tensor(cos_t[:, l, :, i, :], tab[:, 2 * i, :, :], scale, ALU.mult).then_inc(tab_done, 1)
                    for a, b in ((0, 32), (32, 0)):
                        dve.tensor_tensor(sin_t[:, l, :, i, a:a + 32], tab[:, 2 * i + 1, :, a:a + 32],
                                          scale[:, :, b:b + 32], ALU.mult).then_inc(tab_done, 1)

            def rest_of_hT(G):
                has(dve, hT_done, G)
                if G[0]:
                    has(dve, y_done, (G[0] - 1, G[1]))
                dve.tensor_tensor(hT_parts[1][0:64, :], XT[0:64, bass.ds(G[1] * T, T)],
                                  hT_parts[0][0:64, :].bitcast(F32), ALU.subtract)
                dve.tensor_tensor(hT_parts[1][64:P, 1:T], XT[64:P, bass.ds(G[1] * T, T - 1)],
                                  hT_parts[0][64:P, 1:T].bitcast(F32), ALU.subtract).then_inc(hT_rest_done[0], 1)

            def first_bias(l):
                dve.wait_ge(b1_full, l + 1)
                r = rows_of(2)
                b1 = vec[:, l, 0:6].rearrange("p (a c) -> p a c", c=3)
                b1_to = b1s[:, l, :].rearrange("p (a c) -> p a c", c=3)
                b1_ps = psF[:, 0:6].rearrange("p (a c) -> p a c", a=2, c=3)
                dve.tensor_tensor(b1_to[:, :, 0:2], b1_ps[:, :, 0:2], b1[:, :, 0:2], ALU.add).then_inc(b1_done, 1)
                dve.tensor_tensor(b1_to[0:r, :, 2:3], b1_ps[0:r, :, 2:3], b1[0:r, :, 2:3], ALU.add).then_inc(b1_done, 1)

            rest_of_hT((0, 0))
            rest_of_wqkv(0)
            dve.wait_ge(tab_loaded, 16)
            tables(0)
            first_bias(0)

            def after(l, s):
                if (l, s) == (0, 0):
                    rest_of_w1(0)
                elif s == 1 and l + 1 < DEPTH:
                    rest_of_wqkv(l + 1)
                    rest_of_w1(l + 1)
                    first_bias(l + 1)
                    tables(l + 1)

            def cols(G):
                return bass.ds(G[1] * T, T)

            def half(name, G):
                if name == "wo":
                    bank = f_wait(dve, name, G)
                    x = XT[:, cols(G)]
                    dve.tensor_tensor(x, bank[:, :], x, ALU.add).then_inc(x2_done[0], 1)
                elif name == "var":
                    bank = f_wait(dve, name, G)
                    dve.tensor_scalar(var_eps[:, :], bank[:, 0:NT], EPS, None, ALU.add).then_inc(ve_done[0], 1)
                elif name == "rstd":
                    bank = f_wait(dve, name, G)
                    has(dve, h2c_done, G)
                    dve.tensor_tensor(h2n[:, :], bank[:, :], h2c[:, :], ALU.mult).then_inc(h2n_done[0], 1)
                elif name[0] == "a":
                    bank, c = f_wait(dve, name, G), int(name[1])
                    r = rows_of(c)
                    dve.scalar_tensor_tensor(out=hid[0:r, c, :], in0=bank[0:r, :], scalar=b1s[0:r, G[0], c:c + 1],
                                             in1=hid[0:r, c, :], op0=ALU.add, op1=ALU.mult).then_inc(hid_done[0], 1)
                elif name == "y":
                    bank = f_wait(dve, name, G)
                    x = XT[:, cols(G)]
                    has(dve, x2_done, G)
                    to = x if G[0] < DEPTH - 1 else y_last[:, :]
                    dve.scalar_tensor_tensor(out=to, in0=bank[:, :], scalar=vec[:, G[0], 8:9], in1=x, op0=ALU.add,
                                             op1=ALU.add).then_inc(y_done[0], 1)
                elif name == "out":
                    if G[0] < DEPTH - 1:
                        dve.sem_inc(out_done[0], 1)
                        return
                    bank = f_wait(dve, name, G)
                    x = X1[:, bass.ds(G[1] * NT, NT), :]
                    dve.tensor_tensor(x, bank[:, :].rearrange("p (t d) -> p t d", d=D), x, ALU.add).then_inc(out_done[0], 1)

            def body(l, s):
                for t in range(NT):
                    now, b1, b2, _ = (tile_back(l, s, t, k) for k in range(4))

                    def by_tables(i, n):
                        G, u = now
                        x = qk[:, i, :].rearrange("p (h d) -> p h d", d=DH)
                        c = by_cos[:, i * 512:(i + 1) * 512].rearrange("p (h d) -> p h d", d=DH)
                        sn = by_sin[:, i * 512:(i + 1) * 512].rearrange("p (h d) -> p h d", d=DH)
                        tabs = sin_t[:, G[0], u, i, :].unsqueeze(1).broadcast_to([P, HEADS, DH])
                        has(dve, qk_done, G, 2 * u + n)
                        has(dve, rot_done, G, 2 * u + n - 2)
                        dve.tensor_tensor(c, x, cos_t[:, G[0], u, i, :].unsqueeze(1).broadcast_to([P, HEADS, DH]),
                                          ALU.mult).then_inc(cos_done[0], 1)
                        if n == 2:
                            f_slot(l, s, t, 2, half)
                        dve.tensor_tensor(sn[:, :, 0:32], x[:, :, 32:64], tabs[:, :, 0:32], ALU.mult)
                        dve.tensor_tensor(sn[:, :, 32:64], x[:, :, 0:32], tabs[:, :, 32:64],
                                          ALU.mult).then_inc(sin_done[0], 1)
                        has(dve, sq_done, G, 2 * u + n)
                        has(dve, ssq_done, G, 3 * u)
                        dve.tensor_reduce(ssq[:, i * HEADS:(i + 1) * HEADS], sq[:, i, :].rearrange("p (h d) -> p h d", d=DH),
                                          AX.X, ALU.add).then_inc(ssq_done[0], 1)

                    if now:
                        if now[1] == 0:
                            dve.wait_ge(tab_done, 6 * (now[0][0] + 1))
                        by_tables(1, 1)
                    f_slot(l, s, t, 1, half)
                    if now:
                        by_tables(0, 2)
                        G, u = now
                        has(dve, ssq_done, G, 3 * u + 2)
                        has(dve, rnorm_done, G, u)
                        dve.tensor_scalar(ssq_c[:, :], ssq[:, :], 1e-24, None, ALU.max).then_inc(ssq_done[0], 1)
                    else:
                        f_slot(l, s, t, 2, half)
                    if b2:
                        G, u = b2
                        has(dve, ot_full, G, u)
                        for e in range(2):
                            has(dve, pv_full, G, 2 * u + e + 1)
                            pv = psV[e][:, 0:4 * (DH + 1)].rearrange("p (a d) -> p a d", d=DH + 1)
                            dve.reciprocal(rden[:, e * 4:e * 4 + 4], pv[:, :, DH]).then_inc(rden_done[0], 1)
                        for e in range(2):
                            has(dve, rden_done, G, 2 * u + e + 1)
                            pv = psV[e][:, 0:4 * (DH + 1)].rearrange("p (a d) -> p a d", d=DH + 1)
                            dve.tensor_tensor(o_tok[:, :].rearrange("p (a e d) -> p a e d", e=2, d=DH)[:, :, e, :],
                                              pv[:, :, 0:DH], rden[:, e * 4:e * 4 + 4].unsqueeze(2).broadcast_to([P, 4, DH]),
                                              ALU.mult).then_inc(o_done[0], 1)
                    f_slot(l, s, t, 3, half)
                    if t == NT - 1 and seq_back(l, s, -1):
                        rest_of_hT(seq_back(l, s, -1))
                    if b1:
                        G, u = b1
                        for e in range(2):
                            h = slice(e * 4, e * 4 + 4)
                            has(dve, probs_done, G, 2 * u + e - 1)
                            has(dve, sim_full, G, 2 * u + e + 1)
                            scores = psS[e][:, :].rearrange("p (a b) -> p a b", a=4)
                            dve.tensor_reduce(top[:, h], scores, AX.X, ALU.max).then_inc(top_done[0], 1)
                            has(dve, top_done, G, 2 * u + e + 1)
                            dve.tensor_tensor(less[:, h, :], scores, top[:, h].unsqueeze(2).broadcast_to([P, 4, P]),
                                              ALU.subtract).then_inc(less_done[0], 1)
                    f_slot(l, s, t, 4, half)
                    if t == NT - 1 and seq_back(l, s, 1):
                        G = seq_back(l, s, 1)
                        has(dve, h2n_first_done, G)
                        dve.tensor_tensor(h2n_parts[1][:, :], h2n[:, :], h2n_parts[0][:, :].bitcast(F32),
                                          ALU.subtract).then_inc(h2n_rest_done[0], 1)

            over_layers(dve, body, after)


def program(nc, x, wm, rows, wf, vecs, qk_scales, consts, out):
    with ExitStack() as top:
        def sb(name, shape):
            return top.enter_context(nc.sbuf_tensor(name, shape, F32))

        X1, XT = sb("X1", [P, NB * NT, D]), sb("XT", [P, NB * T])
        cst = sb("const", [P, C_TAB])
        w0, vec = sb("f_w0", [P, F_N]), sb("f_vec", [P, DEPTH, 9])
        scales = sb("f_scales", [P, DEPTH, 2, DH])
        loaded = top.enter_context(nc.semaphore("f_loaded"))
        loads = [(w0[:, :], wf[0])]
        for l in range(DEPTH):
            loads += [(vec[:, l, :], vecs[l]),
                      (scales[:, l, :, :].rearrange("p a d -> p (a d)"),
                       qk_scales[l:l + 1, :].broadcast_to([P, 2 * DH]))]
        given = cst, w0, vec, scales, loaded, 16 * len(loads)
        mixer_phase(nc, x, wm, rows, consts, X1, XT, cst, loads, loaded)
        layers_phase(nc, wf, consts, X1, XT, given, out)


def constants():
    import numpy as np
    f = np.float32
    c = np.zeros((P, C_N), f)
    j, i = np.arange(P)[:, None], np.arange(P)[None, :]
    c[:, C_ID:C_ID + P] = j == i
    c[:, C_CAUSAL:C_CAUSAL + P] = np.where(j > i, f(-1e30), f(0))
    q, k = j % 64, i
    ok = np.where(k < 64, q <= k, k - 64 <= q)
    c[:, C_MASK:C_MASK + P] = np.where(ok, f(0), f(-1e30))
    c[:, C_MASK0:C_MASK0 + P] = np.where(ok & ((j >= 64) | (k >= 64)), f(0), f(-1e30))
    c[:, C_CENTRE:C_CENTRE + P] = (j == i) - f(1 / D)
    head = np.arange(D) // CH
    for part in range(3):
        for h in range(MH):
            r = 32 * part + h
            c[r, C_NAT:C_NAT + D] = head == h
            c[r, C_HEADS + h], c[r, C_HEADS + MH + h] = 1, -1
            c[r, C_SEL + h * P:C_SEL + (h + 1) * P] = 1
    for r in range(P):
        for p in range(PAIRS):
            own_head = 2 * p + r // 64
            at = C_OWN + 32 * p + (own_head % HQ) * CH
            c[r, at:at + CH] = 1
    c[:, C_SCAN:C_SCAN + T] = (np.arange(T) % P != 0)
    half = np.arange(0, DH, 2, dtype=f)
    inv_freq = f(1) / f(10000) ** (half / f(DH))
    pos = np.arange(T, dtype=f)
    angle = pos[:, None] * inv_freq[None, :]
    base = (half + f(0.4 * DH)) / f(1.4 * DH)
    scale = base[None, :] ** ((pos - T // 2) / f(WIN // 2))[:, None]
    sign = np.concatenate([-np.ones(32, f), np.ones(32, f)])
    twice = lambda m: np.concatenate([m, m], 1)
    tabs = [twice(np.cos(angle) * scale) * f(8), twice(np.sin(angle) * scale) * sign * f(8),
            twice(np.cos(angle) / scale), twice(np.sin(angle) / scale) * sign]
    tabs = np.stack(tabs).reshape(4, NT, P, DH).transpose(2, 0, 1, 3)
    c[:, C_TAB:C_SEL] = tabs.reshape(P, -1)
    return c


def kernel(**inputs):
    import numpy as np
    import concourse.bacc as bacc
    from concourse.bass_utils import run_bass_kernel_spmd

    a = {k: np.asarray(v) for k, v in inputs.items()}
    n = "L0_attn_"
    xbc, bxbc = a[n + "W_XBC"], a[n + "b_XBC"]
    wm = np.zeros((P, W_N), np.float32)
    for h in range(MH):
        r, pc = slice(h * CH, (h + 1) * CH), (h // 2) * P + (h % 2) * NS
        wm[r, W_X + h * CH:W_X + (h + 1) * CH] = xbc[h, 0:CH].T
        wm[r, W_B + pc:W_B + pc + NS] = xbc[h, CH:CH + NS].T
        wm[r, W_C + pc:W_C + pc + NS] = xbc[h, CH + NS:].T
        wm[r, W_G + h * CH:W_G + (h + 1) * CH] = a[n + "W_gate"][h].T
        wm[r, W_LA + h] = a[n + "W_logA"][h, 0]
        half = slice((h % 2) * NS, (h % 2) * NS + NS)
        wm[half, W_BB + h // 2] = bxbc[h, CH:CH + NS]
        wm[half, W_BC + h // 2] = bxbc[h, CH + NS:]
    wm[:, W_O:W_O + D] = a[n + "W_out"].T
    wm[:, W_BG] = a[n + "b_gate"].reshape(D)
    wm[0:MH, W_BLA] = a[n + "b_logA"][:, 0]
    rows = np.stack([bxbc[:, 0:CH].reshape(D), a[n + "b_out"]])

    n = "L0_ffn_"
    by_rows = lambda m: m.reshape(-1, P, m.shape[-1]).transpose(1, 0, 2).reshape(P, -1)
    wf = np.zeros((DEPTH, P, F_N), np.float32)
    vecs = np.zeros((DEPTH, P, 9), np.float32)
    for l in range(DEPTH):
        wf[l, :, F_QKV:F_O] = a[n + "wqkv"][l]
        wf[l, :, F_O:F_1] = by_rows(a[n + "wo"][l])
        wf[l, :, F_1:F_2] = a[n + "w1"][l]
        for c in range(3):
            r = min(P, HID - c * P)
            wf[l, 0:r, F_2 + c * P:F_2 + (c + 1) * P] = a[n + "w2"][l, c * P:c * P + r]
            vecs[l, 0:r, c] = a[n + "b1"][l, c * P:c * P + r]
            vecs[l, 0:r, 3 + c] = a[n + "b1"][l, HID + c * P:HID + c * P + r]
        vecs[l, :, 6], vecs[l, :, 7], vecs[l, :, 8] = a[n + "ln_g"][l], a[n + "ln_b"][l], a[n + "b2"][l]
    qk_scales = np.concatenate([a[n + "q_scale"], a[n + "k_scale"]], 1)

    arrays = {"x": a["L0_attn_inp"], "wm": wm, "rows": rows, "wf": wf, "vecs": vecs, "qk_scales": qk_scales,
              "consts": constants()}
    nc = bacc.Bacc("TRN2", target_bir_lowering=False, num_devices=1)
    args = [nc.dram_tensor(k, v.shape, mybir.dt.from_np(v.dtype), kind="ExternalInput").ap() for k, v in arrays.items()]
    out = nc.dram_tensor("out", (NB, T, D), F32, kind="ExternalOutput").ap()
    program(nc, *args, out)
    r = run_bass_kernel_spmd(nc, [arrays], core_ids=[0])
    return r.results[0]["out"]
```
